# Optimizing a Trainium2 kernel written in Bass

```python
import numpy as np
import jax
import jax.numpy as jnp

def _softmax(x, axis=-1):
    return jax.nn.softmax(x, axis=axis)

def _gelu(x):
    return jax.nn.gelu(x, approximate=True)

def _silu(x):
    return jax.nn.silu(x)

def _sigmoid(x):
    return jax.nn.sigmoid(x)

def _layernorm(x, axis=-1, eps=1e-05):
    m = jnp.mean(x, axis=axis, keepdims=True)
    v = jnp.var(x, axis=axis, keepdims=True)
    return (x - m) / jnp.sqrt(v + eps)

def _scatter_add(tgt, idx, src, axis=0):
    return tgt.at[idx].add(src)

def _segment_sum(src, seg, n):
    return jax.ops.segment_sum(src, seg, n)
kernel_name = 'mk_sandwich_d2_jaxref_r8_17ba9d'

def setup_inputs(seed: int=0):
    np.random.seed(seed)
    _w = jnp.asarray

    def _L0_attn_setup():
        import jax, jax.numpy as jnp
        import numpy as np
        K = 128
        H = 16
        key = jax.random.key(seed)
        ks = jax.random.split(key, 6)
        s = 1.0 / np.sqrt(K)
        return {'x': jax.random.normal(ks[0], (2, 256, K), dtype=jnp.float32), 'Wq': jax.random.uniform(ks[1], (K, K), jnp.float32, -s, s), 'Wk': jax.random.uniform(ks[2], (K, K), jnp.float32, -s, s), 'Wv': jax.random.uniform(ks[3], (K, K), jnp.float32, -s, s), 'Wu': jax.random.uniform(ks[4], (K, K), jnp.float32, -s, s), 'bu': jax.random.uniform(ks[5], (K,), jnp.float32, -s, s)}
    _L0_attn_in = _L0_attn_setup()

    def _L0_ffn_setup():
        import jax, jax.numpy as jnp
        import numpy as np
        B, S, D, E, H, K = (4, 256, 128, 8, 512, 2)
        EPS = 1e-06

        def _ln(x, scale, bias):
            m = jnp.mean(x, axis=-1, keepdims=True)
            v = jnp.mean(jnp.square(x - m), axis=-1, keepdims=True)
            return (x - m) * jax.lax.rsqrt(v + EPS) * scale + bias
        key = jax.random.key(seed)
        ks = jax.random.split(key, 4)
        s1 = 1.0 / np.sqrt(D)
        s2 = 1.0 / np.sqrt(H)
        return {'x': jax.random.normal(ks[0], (B, S, D), jnp.float32), 'router_ln_scale': jnp.ones((D,), jnp.float32), 'router_ln_bias': jnp.zeros((D,), jnp.float32), 'router_w': jax.random.normal(ks[1], (E, D), jnp.float32) * s1, 'router_b': jnp.zeros((E,), jnp.float32), 'expert_ln_scale': jnp.ones((E, D), jnp.float32), 'expert_ln_bias': jnp.zeros((E, D), jnp.float32), 'w1': jax.random.normal(ks[2], (E, H, D), jnp.float32) * s1, 'b1': jnp.zeros((E, H), jnp.float32), 'w2': jax.random.normal(ks[3], (E, D, H), jnp.float32) * s2, 'b2': jnp.zeros((E, D), jnp.float32)}
    _L0_ffn_in = _L0_ffn_setup()

    def _L1_attn_setup():
        import jax, jax.numpy as jnp
        import numpy as np
        D_MODEL = 128
        N_HEADS = 16
        N_GROUPS = 4
        D_K = D_MODEL // N_HEADS
        HEADS_PER_GROUP = N_HEADS // N_GROUPS

        def rope(x):
            s, d = (x.shape[1], x.shape[2])
            theta = 1.0 / 10000.0 ** (jnp.arange(d // 2, dtype=jnp.float32) / (d // 2))
            ang = jnp.arange(s, dtype=jnp.float32)[:, None] * theta[None, :]
            cos, sin = (jnp.cos(ang), jnp.sin(ang))
            xe, xo = (x[..., 0::2], x[..., 1::2])
            return jnp.concatenate([xe * cos - xo * sin, xe * sin + xo * cos], axis=-1)
        key = jax.random.key(seed)
        k1, k2, k3, k4, k5 = jax.random.split(key, 5)
        b, s = (1, 256)
        scale = 0.02
        X = jax.random.normal(k1, (b, s, D_MODEL), dtype=jnp.float32)
        W_q = jax.random.normal(k2, (D_MODEL, D_MODEL), dtype=jnp.float32) * scale
        W_k = jax.random.normal(k3, (N_GROUPS * D_K, D_MODEL), dtype=jnp.float32) * scale
        W_v = jax.random.normal(k4, (N_GROUPS * D_K, D_MODEL), dtype=jnp.float32) * scale
        W_o = jax.random.normal(k5, (D_MODEL, D_MODEL), dtype=jnp.float32) * scale
        return {'X': X, 'W_q': W_q, 'W_k': W_k, 'W_v': W_v, 'W_o': W_o}
    _L1_attn_in = _L1_attn_setup()

    def _L1_ffn_setup():
        import jax, jax.numpy as jnp
        import numpy as np
        DIM = 128

        def _reference_tuple_inner(x, W_r, W_k, W_v, mu_r, mu_k):
            B, T, C = x.shape
            x_prev = jnp.concatenate([jnp.zeros((B, 1, C), x.dtype), x[:, :-1, :]], axis=1)
            xr = mu_r * x + (1.0 - mu_r) * x_prev
            xk = mu_k * x + (1.0 - mu_k) * x_prev
            r = jax.nn.sigmoid(jnp.einsum('btc,dc->btd', xr, W_r))
            k = jnp.einsum('btc,dc->btd', xk, W_k)
            k_act = jnp.square(jax.nn.relu(k))
            out = r * jnp.einsum('btc,dc->btd', k_act, W_v)
            new_state = x[:, -1, :]
            return (out, new_state)
        key = jax.random.key(seed)
        ks = jax.random.split(key, 6)
        B, T, C = (8, 256, DIM)
        x = jax.random.normal(ks[0], (B, T, C), dtype=jnp.float32)
        s = 1.0 / np.sqrt(C)
        W_r = jax.random.uniform(ks[1], (C, C), jnp.float32, -s, s)
        W_k = jax.random.uniform(ks[2], (C, C), jnp.float32, -s, s)
        W_v = jax.random.uniform(ks[3], (C, C), jnp.float32, -s, s)
        mu_r = jax.random.uniform(ks[4], (C,), jnp.float32)
        mu_k = jax.random.uniform(ks[5], (C,), jnp.float32)
        return {'x': x, 'W_r': W_r, 'W_k': W_k, 'W_v': W_v, 'mu_r': mu_r, 'mu_k': mu_k}
    _L1_ffn_in = _L1_ffn_setup()
    _d = {'L0_attn_x': _L0_attn_in['x'], 'L0_attn_Wq': _L0_attn_in['Wq'], 'L0_attn_Wk': _L0_attn_in['Wk'], 'L0_attn_Wv': _L0_attn_in['Wv'], 'L0_attn_Wu': _L0_attn_in['Wu'], 'L0_attn_bu': _L0_attn_in['bu'], 'L0_ffn_router_ln_scale': _L0_ffn_in['router_ln_scale'], 'L0_ffn_router_ln_bias': _L0_ffn_in['router_ln_bias'], 'L0_ffn_router_w': _L0_ffn_in['router_w'], 'L0_ffn_router_b': _L0_ffn_in['router_b'], 'L0_ffn_expert_ln_scale': _L0_ffn_in['expert_ln_scale'], 'L0_ffn_expert_ln_bias': _L0_ffn_in['expert_ln_bias'], 'L0_ffn_w1': _L0_ffn_in['w1'], 'L0_ffn_b1': _L0_ffn_in['b1'], 'L0_ffn_w2': _L0_ffn_in['w2'], 'L0_ffn_b2': _L0_ffn_in['b2'], 'L1_attn_W_q': _L1_attn_in['W_q'], 'L1_attn_W_k': _L1_attn_in['W_k'], 'L1_attn_W_v': _L1_attn_in['W_v'], 'L1_attn_W_o': _L1_attn_in['W_o'], 'L1_ffn_W_r': _L1_ffn_in['W_r'], 'L1_ffn_W_k': _L1_ffn_in['W_k'], 'L1_ffn_W_v': _L1_ffn_in['W_v'], 'L1_ffn_mu_r': _L1_ffn_in['mu_r'], 'L1_ffn_mu_k': _L1_ffn_in['mu_k']}
    _x0 = _d['L0_attn_x']
    _d['L0_attn_x'] = jax.random.normal(jax.random.fold_in(jax.random.key(seed), 1), (8, 512, 128), dtype=_x0.dtype)
    del _x0
    return _d

def reference(L0_attn_x, L0_attn_Wq, L0_attn_Wk, L0_attn_Wv, L0_attn_Wu, L0_attn_bu, L0_ffn_router_ln_scale, L0_ffn_router_ln_bias, L0_ffn_router_w, L0_ffn_router_b, L0_ffn_expert_ln_scale, L0_ffn_expert_ln_bias, L0_ffn_w1, L0_ffn_b1, L0_ffn_w2, L0_ffn_b2, L1_attn_W_q, L1_attn_W_k, L1_attn_W_v, L1_attn_W_o, L1_ffn_W_r, L1_ffn_W_k, L1_ffn_W_v, L1_ffn_mu_r, L1_ffn_mu_k):

    def _L0_attn_ref(x, Wq, Wk, Wv, Wu, bu):
        import jax, jax.numpy as jnp
        import numpy as np
        K = 128
        H = 16
        b, t, k = x.shape
        hd = k // H
        scale = jnp.asarray(k, x.dtype) ** 0.25
        q = (jnp.einsum('btk,ok->bto', x, Wq) / scale).reshape(b, t, H, hd)
        kk = (jnp.einsum('btk,ok->bto', x, Wk) / scale).reshape(b, t, H, hd)
        v = jnp.einsum('btk,ok->bto', x, Wv).reshape(b, t, H, hd)
        dot = jnp.einsum('bthd,bshd->bhts', q, kk)
        att = jax.nn.softmax(dot, axis=-1)
        out = jnp.einsum('bhts,bshd->bthd', att, v).reshape(b, t, k)
        return jnp.einsum('btk,ok->bto', out, Wu) + bu

    def _L0_ffn_ref(x, router_ln_scale, router_ln_bias, router_w, router_b, expert_ln_scale, expert_ln_bias, w1, b1, w2, b2):
        import jax, jax.numpy as jnp
        import numpy as np
        B, S, D, E, H, K = (4, 256, 128, 8, 512, 2)
        EPS = 1e-06

        def _ln(x, scale, bias):
            m = jnp.mean(x, axis=-1, keepdims=True)
            v = jnp.mean(jnp.square(x - m), axis=-1, keepdims=True)
            return (x - m) * jax.lax.rsqrt(v + EPS) * scale + bias
        orig_shape = x.shape
        xf = x.reshape(-1, D)
        T = xf.shape[0]
        logits = _ln(xf, router_ln_scale, router_ln_bias) @ router_w.T + router_b
        probs = jax.nn.softmax(logits, axis=-1)
        topw, topi = jax.lax.top_k(probs, K)
        topw = topw / jnp.sum(topw, axis=-1, keepdims=True)
        gates = jnp.zeros((T, E), xf.dtype).at[jnp.arange(T)[:, None], topi].set(topw)

        def expert(ls, lb, W1, B1, W2, B2):
            h = jax.nn.gelu(_ln(xf, ls, lb) @ W1.T + B1, approximate=False)
            return h @ W2.T + B2
        ys = jax.vmap(expert)(expert_ln_scale, expert_ln_bias, w1, b1, w2, b2)
        out = jnp.einsum('te,etd->td', gates, ys)
        return out.reshape(orig_shape)

    def _L1_attn_ref(X, W_q, W_k, W_v, W_o):
        import jax, jax.numpy as jnp
        import numpy as np
        D_MODEL = 128
        N_HEADS = 16
        N_GROUPS = 4
        D_K = D_MODEL // N_HEADS
        HEADS_PER_GROUP = N_HEADS // N_GROUPS

        def rope(x):
            s, d = (x.shape[1], x.shape[2])
            theta = 1.0 / 10000.0 ** (jnp.arange(d // 2, dtype=jnp.float32) / (d // 2))
            ang = jnp.arange(s, dtype=jnp.float32)[:, None] * theta[None, :]
            cos, sin = (jnp.cos(ang), jnp.sin(ang))
            xe, xo = (x[..., 0::2], x[..., 1::2])
            return jnp.concatenate([xe * cos - xo * sin, xe * sin + xo * cos], axis=-1)
        b, s, _ = X.shape
        Xr = rope(X)
        Q = (Xr @ W_q.T).reshape(b, s, N_HEADS, D_K).transpose(0, 2, 1, 3)
        K = (Xr @ W_k.T).reshape(b, s, N_GROUPS, D_K).transpose(0, 2, 1, 3)
        V = (Xr @ W_v.T).reshape(b, s, N_GROUPS, D_K).transpose(0, 2, 1, 3)
        Q = Q.reshape(b, N_GROUPS, HEADS_PER_GROUP, s, D_K)
        scores = jnp.einsum('bghsd,bgtd->bghst', Q, K) / jnp.sqrt(jnp.float32(D_K))
        mask = jnp.triu(jnp.ones((s, s), dtype=scores.dtype), k=1) * -1000000000.0
        attn = jax.nn.softmax(scores + mask, axis=-1)
        out = jnp.einsum('bghst,bgtd->bghsd', attn, V)
        out = out.reshape(b, N_HEADS, s, D_K).transpose(0, 2, 1, 3).reshape(b, s, D_MODEL)
        return out @ W_o.T

    def _L1_ffn_ref(x, W_r, W_k, W_v, mu_r, mu_k):
        import jax, jax.numpy as jnp
        import numpy as np
        DIM = 128

        def _reference_tuple_inner(x, W_r, W_k, W_v, mu_r, mu_k):
            B, T, C = x.shape
            x_prev = jnp.concatenate([jnp.zeros((B, 1, C), x.dtype), x[:, :-1, :]], axis=1)
            xr = mu_r * x + (1.0 - mu_r) * x_prev
            xk = mu_k * x + (1.0 - mu_k) * x_prev
            r = jax.nn.sigmoid(jnp.einsum('btc,dc->btd', xr, W_r))
            k = jnp.einsum('btc,dc->btd', xk, W_k)
            k_act = jnp.square(jax.nn.relu(k))
            out = r * jnp.einsum('btc,dc->btd', k_act, W_v)
            new_state = x[:, -1, :]
            return (out, new_state)
        return _reference_tuple_inner(x, W_r, W_k, W_v, mu_r, mu_k)[0]
    x = L0_attn_x
    x = x + _layernorm(_L0_attn_ref(_layernorm(x, axis=-1), L0_attn_Wq, L0_attn_Wk, L0_attn_Wv, L0_attn_Wu, L0_attn_bu), axis=-1)
    x = x + _layernorm(_L0_ffn_ref(_layernorm(x, axis=-1), L0_ffn_router_ln_scale, L0_ffn_router_ln_bias, L0_ffn_router_w, L0_ffn_router_b, L0_ffn_expert_ln_scale, L0_ffn_expert_ln_bias, L0_ffn_w1, L0_ffn_b1, L0_ffn_w2, L0_ffn_b2), axis=-1)
    x = x + _layernorm(_L1_attn_ref(_layernorm(x, axis=-1), L1_attn_W_q, L1_attn_W_k, L1_attn_W_v, L1_attn_W_o), axis=-1)
    x = x + _layernorm(_L1_ffn_ref(_layernorm(x, axis=-1), L1_ffn_W_r, L1_ffn_W_k, L1_ffn_W_v, L1_ffn_mu_r, L1_ffn_mu_k), axis=-1)
    return x

_drawn_inputs = setup_inputs


def setup_inputs(seed=0):
    import zlib

    import numpy as np

    out = dict(_drawn_inputs(seed))
    spreads = {'L0_ffn_router_ln_scale': (1.0, 0.2),
     'L0_ffn_router_ln_bias': (0.0, 0.1),
     'L0_ffn_router_b': (0.0, 0.1),
     'L0_ffn_expert_ln_scale': (1.0, 0.2),
     'L0_ffn_expert_ln_bias': (0.0, 0.1),
     'L0_ffn_b1': (0.0, 0.1),
     'L0_ffn_b2': (0.0, 0.1)}
    factors = {'L1_attn_W_q': 8.0, 'L1_attn_W_k': 8.0}
    for name, (base, spread) in spreads.items():
        noise = np.random.default_rng([zlib.crc32(name.encode()), seed]).standard_normal(out[name].shape)
        drawn = base * np.exp(spread * noise) if base else spread * noise
        out[name] = jnp.asarray(drawn.astype(out[name].dtype))
    for name, factor in factors.items():
        out[name] = (out[name] * factor).astype(out[name].dtype)
    return out
```

```python
from contextlib import ExitStack

import numpy as np

import concourse.bass as bass
from concourse import mybir

F32 = mybir.dt.float32
BF16 = mybir.dt.bfloat16
I32 = mybir.dt.int32
ALU = mybir.AluOpType
ACT = mybir.ActivationFunctionType
AX = mybir.AxisListType

NB = 8
T = 512
D = 128
NT = T // 128
NH = 16
HD = D // NH
HG = 4
NG = NH // HG
UNITS = NG * NT
NE = 8
HID = 512
HB = HID // 128
SPLITS = 3
TERM_ROWS = SPLITS * SPLITS * HD
MAX_ROW = 96
MAX_PARTS = 2
LOADED_W = 64
CONSTS = 7
GOLD = 0x5F3759DF

WCOLS = [("wq1", D), ("wk1", D), ("wv1", D), ("wu1", D), ("wq2", D), ("wk2", NG * HD), ("wv2", NG * HD),
         ("wo2", D), ("wr", D), ("wkk", D), ("wvv", D), ("ident", D), ("router_w", NE),
         ("router_s", 1), ("router_t", 1), ("expert_s", NE), ("expert_t", NE), ("b1", NE * HB),
         ("mu_r", 1), ("mu_k", 1)]
WAT, WN = {}, 0
for _name, _n in WCOLS:
    WAT[_name] = (WN, WN + _n)
    WN += _n
RCOLS = [("bu", D), ("b2", NE * D), ("router_b", NE), ("earlier", NE * NE)]
RAT, RN = {}, 0
for _name, _n in RCOLS:
    RAT[_name] = (RN, RN + _n)
    RN += _n

MISC = {1: ("xT", "project"), 2: ("oT3", "finish"), 3: ("q", "project"), 4: ("xoT", "finish"),
        5: ("k", "project"), 6: ("oT0", "attend"), 7: ("v", "score"), 8: ("m3", "attend"),
        9: ("out", "finish"), 10: ("oT1", "attend"), 11: ("m0", "score"), 12: ("m1", "score"),
        13: ("m2", "score"), 14: ("oT2", "attend")}
FIRST_STEP, LAST_STEP = -2, NB
FULL = (1, NB - 3)


def stages(b):
    s = set()
    if b + 2 < NB:
        s.add("project")
    if 0 <= b + 1 < NB:
        s.add("score")
    if 0 <= b < NB:
        s.add("attend")
    if 0 <= b - 1:
        s.add("finish")
    return s


def misc_count(b, b_int, unit):
    st = stages(b_int)
    n = sum(1 for u in MISC if u <= unit and MISC[u][1] in st)
    n += sum(1 for s in range(FIRST_STEP, b_int) for u in MISC if MISC[u][1] in stages(s))
    return (b - b_int) * len(MISC) + n if not isinstance(b, int) else n


def run_steps(eng, step):
    for b in range(FIRST_STEP, FULL[0]):
        step(b, b)
    with eng.Fori(FULL[0], FULL[1], 2) as i:
        step(i, FULL[0])
        step(i + 1, FULL[0] + 1)
    for b in range(FULL[1], LAST_STEP + 1):
        step(b, b)


def build(nc, x_in, weights, rows, w1, w2, rope, mask, out):
    with ExitStack() as ctx:
        def sb(name, shape, dt=F32):
            return ctx.enter_context(nc.sbuf_tensor(name, shape, dt))

        def psum(name, shape):
            return ctx.enter_context(nc.psum_tensor(name, shape, F32))

        def sem(name):
            return ctx.enter_context(nc.semaphore(name))

        X = sb("X", [128, NB * T])
        W = sb("W", [128, WN])
        R = sb("R", [128, RN])
        W1 = sb("W1", [128, NE * HID])
        W2 = sb("W2", [128, NE * HB * D])
        ident_b = sb("ident_b", [128, 128], BF16)
        mask_b = sb("mask_b", [128, 128], BF16)
        rope_t = sb("rope_t", [128, NT, 2, D // 2])
        stat = sb("stat", [128, NT, 8])
        mv = sb("mv", [128, NT, 2])
        rs = sb("rs", [128, 4, NT])
        rstd = sb("rstd", [128, NT])
        ops = sb("ops", [128, 2 * 2 * NH * T], BF16)
        QO = ops[:, 0:2 * NH * T].rearrange("p (c h t) -> p c h t", c=2, h=NH)
        KO = ops[:, 2 * NH * T:].rearrange("p (c h t) -> p c h t", c=2, h=NH)
        arena = sb("arena", [128, 4 * HG * T])
        P = arena[:, :].rearrange("p (r h t) -> p r h t", r=4, h=HG)
        VO = sb("VO", [128, 2, NT, NH, 32])
        XN = sb("XN", [128, NT, D])
        XR = sb("XR", [128, NT, D])
        RT = sb("RT", [128, 2, NT, D // 2])
        XNT = sb("XNT", [128, 2, T])
        QS = sb("QS", [128, 2, T])
        RES = sb("RES", [128, T])
        zero = sb("zero", [128, 1])
        SPL = sb("SPL", [128, 2, SPLITS, T], BF16)
        MX = sb("MX", [128, 2, NG, NT, HG])
        MR = sb("MR", [128, NT, HG])
        MS = sb("MS", [128, 2, NT, MAX_PARTS, HG], BF16)
        MT = sb("MT", [MAX_PARTS * HG, 2, T], BF16)
        OT = sb("OT", [128, T])
        RL = sb("RL", [128, NT, HG])
        XO = sb("XO", [128, NT, D])
        XOT = sb("XOT", [128, T])
        Y = sb("Y", [128, NT, D])

        PA = [psum("PA0", [128, 512]), psum("PA1", [128, 512])]
        PB = [psum("PB0", [128, 1024]), psum("PB1", [128, 1024])]
        PV = psum("PV", [128, 512])
        PM = psum("PM", [128, 512])
        PMb = PM[:, :].bitcast(BF16)

        scratch = {k: nc.dram_tensor(f"scratch_{k}", (2, SPLITS * HD, NH * T), BF16).ap() for k in ("q", "k")}

        def w(name):
            return W[:, WAT[name][0]:WAT[name][1]]

        def row(name):
            return R[:, RAT[name][0]:RAT[name][1]]

        ident = w("ident")
        loaded_x, loaded_w, loaded_mw = sem("loaded_x"), sem("loaded_w"), sem("loaded_mw")
        consts = sem("consts")
        all_out = sem("all_out")

        def xcols(b, i):
            return X[:, bass.ds(b * T + i * D, D)]

        def layer_norm(v, src, dst, eps, chain, base):
            n = [0]

            def link(ins):
                n[0] += 1
                ins.then_inc(chain, 1)
                v.wait_ge(chain, base + n[0])
                if n[0] == 1:
                    nc.vector.memset(stat[:, 0, 6:7], 0.0)

            for i in range(NT):
                ins = nc.vector.bn_stats(stat[:, i, 0:6], src(i))
            link(ins)
            for i in range(NT):
                ins = nc.vector.bn_aggr(mv[:, i, :], stat[:, i, 0:6])
            link(ins)
            rsqrt(link, mv[:, :, 1], rs, rstd[:, :], eps)
            for i in range(NT):
                ins = nc.vector.tensor_scalar(dst(i), src(i), mv[:, i, 0:1], rstd[:, i:i + 1],
                                              ALU.subtract, ALU.mult)
            link(ins)
            return n[0]

        def rsqrt(link, var, tmp, result, eps):
            ve, y, t = tmp[:, 0, :], tmp[:, 1, :], tmp[:, 2, :]
            link(nc.vector.tensor_scalar(ve, var, eps, None, ALU.add))
            link(nc.vector.tensor_scalar(t.bitcast(I32), ve.bitcast(I32), 1, None, ALU.logical_shift_right))
            link(nc.vector.tensor_scalar(y.bitcast(I32), t.bitcast(I32), -1.0, float(GOLD), ALU.mult, ALU.add))
            for k in range(3):
                link(nc.vector.tensor_tensor(t, y, y, ALU.mult))
                link(nc.vector.scalar_tensor_tensor(out=t, in0=t, scalar=-0.5, in1=ve, op0=ALU.mult, op1=ALU.mult))
                link(nc.vector.scalar_tensor_tensor(out=result if k == 2 else y, in0=t, scalar=1.5, in1=y,
                                                    op0=ALU.add, op1=ALU.mult))
        LN_LINKS = 15

        with nc.Block() as block:

            @block.sync
            def _(sp):
                sp.dma_start(X[:, 0:T].rearrange("p (i d) -> p i d", d=D),
                             x_in[0].rearrange("(i p) d -> p i d", p=128)).then_inc(loaded_x, 16)
                sp.dma_start(X[:, T:].rearrange("p (c d) -> p c d", d=D),
                             x_in[1:NB].rearrange("b (i p) d -> p (b i) d", p=128)).then_inc(loaded_x, 16)
                sp.dma_start(W[:, :], weights).then_inc(loaded_w, 16)
                sp.dma_start(R[:, :], rows.partition_broadcast(128)).then_inc(loaded_w, 16)
                sp.dma_start(rope_t[:, :, :, :].rearrange("p i c f -> p i (c f)"),
                             rope.rearrange("(i p) f -> p i f", p=128)).then_inc(loaded_w, 16)
                sp.dma_start(RES[:, 0:128], mask).then_inc(loaded_w, 16)
                sp.dma_start(W1[:, :], w1).then_inc(loaded_mw, 16)
                sp.dma_start(W2[:, :], w2).then_inc(loaded_mw, 16)


            @block.gpsimd
            def _(pool):
                pool.memset(ops[:, :], 0.0).then_inc(consts, 1)
                pool.memset(VO[:, :, :, :, :].rearrange("p a b c d -> p (a b c d)"), 0.0).then_inc(consts, 1)
                pool.wait_ge(consts, 2)
                pool.memset(KO[MAX_ROW:MAX_ROW + MAX_PARTS], 1.0).then_inc(consts, 1)
                pool.wait_ge(consts, 3)
                pool.memset(VO[:, :, :, :, HD:HD + 1], 1.0).then_inc(consts, 1)
                pool.wait_ge(loaded_w, LOADED_W)
                pool.wait_ge(consts, 4)
                pool.tensor_copy(ident_b[:, :], ident).then_inc(consts, 1)
                pool.tensor_copy(mask_b[:, :], RES[:, 0:128]).then_inc(consts, 1)
                pool.memset(zero[:, :], 0.0).then_inc(consts, 1)
                pool.wait_ge(consts, CONSTS)

        def attention(tag, causal, kv_heads, wq, wk, wv, wo, bias, q_scale, k_scale, before, roped):
            S = {n: sem(f"{tag}_{n}") for n in (
                "pre_ln", "post_ln", "xr_ready", "misc_full", "misc_free", "split", "q_scratch", "k_scratch",
                "a_full", "a_free", "m_chain", "m_split", "b_full", "p_ready", "pv_done",
                "ot_ready", "rl_ready", "x_done", "rope_chain")}
            qk_loaded = [sem(f"{tag}_qk_loaded{g}") for g in range(NG)]
            m_loaded = [sem(f"{tag}_m_loaded{g}") for g in range(NG)]
            share = NH // kv_heads
            kg = HG // share
            KROWS = kv_heads * HD
            QK_DMAS = 8

            def keys(i):
                return (i + 1) * 128 if causal else T

            def q0(t):
                return t * 128 if causal else 0

            def misc_evict(eng, b, bi, u):
                eng.wait_ge(S["misc_full"], misc_count(b, bi, u))

            with nc.Block() as block:
                @block.tensor
                def _(pe):
                    pe.wait_ge(loaded_w, LOADED_W)
                    pe.wait_ge(consts, CONSTS)

                    def misc(b, bi, u):
                        item = MISC[u][0]
                        n = misc_count(b, bi, u)
                        if not (isinstance(n, int) and n == 1):
                            pe.wait_ge(S["misc_free"], n - 1)
                        if item == "xT":
                            pe.wait_ge(S["xr_ready"] if roped else S["pre_ln"], b + 3 if roped else (b + 3) * LN_LINKS)
                            for i in range(NT):
                                m = pe.transpose(PM[:, i * 128:(i + 1) * 128], (XR if roped else XN)[:, i, :], ident)
                        elif item in ("q", "k"):
                            wt, n_out = (wq, D) if item == "q" else (wk, KROWS)
                            m = pe.matmul(PM[0:n_out, :], w(wt), XNT[:, bi % 2, :], start=True, stop=True)
                        elif item == "v":
                            for i in range(NT):
                                m = pe.matmul(PM[:, i * 128:i * 128 + KROWS], XNT[:, (bi + 1) % 2, i * 128:(i + 1) * 128],
                                              w(wv), start=True, stop=True)
                        elif item[0] == "m":
                            g = int(item[1])
                            mb = b if item == "m3" else b + 1
                            pe.wait_ge(S["m_split"], mb * NG + g + 1)
                            for i in range(NT):
                                m = pe.transpose(PMb[0:MAX_PARTS * HG, i * 128:(i + 1) * 128],
                                                 MS[:, g % 2, i, :, :].rearrange("p c h -> p (c h)"), ident_b[:, :])
                        elif item[0:2] == "oT":
                            g = int(item[2])
                            ob = b - 1 if g == NG - 1 else b
                            pe.wait_ge(S["ot_ready"], ob * NG + g + 1)
                            for i in range(NT):
                                m = pe.transpose(PM[:, i * 128:(i + 1) * 128], OT[:, i * 128:(i + 1) * 128], ident)
                        elif item == "xoT":
                            for i in range(NT):
                                m = pe.transpose(PM[:, i * 128:(i + 1) * 128], XO[:, i, :], ident)
                        else:
                            for i in range(NT):
                                m = pe.matmul(PM[:, i * 128:(i + 1) * 128], XOT[:, i * 128:(i + 1) * 128], w(wo),
                                              start=True, stop=True)
                        m.then_inc(S["misc_full"], 1)

                    def values(b, bi, u):
                        g, t = divmod(u, NT)
                        pe.wait_ge(S["p_ready"], (b * UNITS + u + 1) * 2)
                        if t == 0 and not (isinstance(b, int) and b == 0 and g == 0):
                            pe.wait_ge(S["ot_ready"], b * NG + g)
                        for j in range(HG):
                            kv = (g * HG + j) // share
                            m = pe.matmul(PV[32 * j:32 * j + 32, q0(t):T], VO[:, bi % 2, t, kv, :],
                                          P[:, u % 4, j, q0(t):T], start=(t == 0), stop=(t == NT - 1))
                        m.then_inc(S["pv_done"], 1)

                    def score_t(b, bi, u, half):
                        g, t = divmod(u, NT)
                        n = b * UNITS * 2 + u * 2 + half
                        if half == 0 and t == 0:
                            pe.wait_ge(m_loaded[g], (b + 1) * 16 * MAX_PARTS)
                        if not (isinstance(b, int) and b == 0 and u == 0):
                            pe.wait_ge(S["p_ready"], n - 1)
                        for j in range(2):
                            h = g * HG + half * 2 + j
                            kv = h // share
                            m = pe.matmul(PB[half][:, j * 512 + q0(t):j * 512 + T],
                                          KO[:, bi % 2, kv, t * 128:(t + 1) * 128], QO[:, bi % 2, h, q0(t):T],
                                          start=True, stop=not causal)
                            if causal:
                                at = j * 512 + q0(t)
                                m = pe.matmul(PB[half][:, at:at + 128], mask_b[:, :], ident_b[:, :],
                                              start=False, stop=True)
                        m.then_inc(S["b_full"], 1)

                    def score(b, bi, u, half):
                        kv = u // share
                        for i in (2 * half, 2 * half + 1):
                            n = b * UNITS * NT + u * NT + i
                            if i == 0 and u % HG == 0:
                                pe.wait_ge(qk_loaded[u // HG], (b + 1) * 16 * QK_DMAS)
                            if not (isinstance(b, int) and b == 0 and u == 0 and i < 2):
                                pe.wait_ge(S["a_free"], n - 1)
                            m = pe.matmul(PA[i % 2][:, 0:keys(i)], QO[0:96, bi % 2, u, i * 128:(i + 1) * 128],
                                          KO[0:96, bi % 2, kv, 0:keys(i)], start=True, stop=not causal)
                            if causal:
                                m = pe.matmul(PA[i % 2][:, i * 128:(i + 1) * 128], ident_b[:, :], mask_b[:, :],
                                              start=False, stop=True)
                            m.then_inc(S["a_full"], 1)

                    def step(b, bi):
                        st = stages(bi)
                        for u in range(UNITS):
                            for half in (0, 1):
                                if "attend" in st:
                                    score_t(b, bi, u, half)
                                if "score" in st:
                                    score(b + 1, bi + 1, u, half)
                            if "attend" in st and u > 0:
                                values(b, bi, u - 1)
                            if "finish" in st and u == 0:
                                values(b - 1, bi - 1, UNITS - 1)
                            if u in MISC and MISC[u][1] in st:
                                misc(b, bi, u)
                    run_steps(pe, step)

                @block.scalar
                def _(act):
                    def evict(b, bi, u):
                        item, stage = MISC[u]
                        if stage not in stages(bi) or item not in ("xT", "q", "k", "v", "xoT"):
                            return
                        misc_evict(act, b, bi, u)
                        if item == "xT":
                            ins = nc.scalar.activation(XNT[:, bi % 2, :], PM[:, :], ACT.Copy)
                        elif item in ("q", "k"):
                            k = int(item == "k")
                            n_out = KROWS if k else D
                            if not (isinstance(b, int) and b == FIRST_STEP):
                                act.wait_ge(S["split"], (b + 1) * 8 + 4 * (k + 1))
                            ins = nc.scalar.activation(QS[0:n_out, k, :], PM[0:n_out, :], ACT.Copy,
                                                       scale=k_scale if k else q_scale)
                        elif item == "v":
                            ins = nc.scalar.activation(
                                VO[:, (bi + 1) % 2, :, 0:kv_heads, 0:HD],
                                PM[:, :].rearrange("p (i h d) -> p i h d", i=NT, d=HD)[:, :, 0:kv_heads, :], ACT.Copy)
                        else:
                            ins = nc.scalar.activation(XOT[:, :], PM[:, :], ACT.Copy)
                        ins.then_inc(S["misc_free"], 1)

                    def drain_group(b, bi, g, before_it):
                        act.wait_ge(S["pv_done"], b * UNITS + (g + 1) * NT)
                        if before_it is not None:
                            act.wait_ge(S["misc_free"], before_it)
                        nc.scalar.activation(OT[:, :], PV[:, :], ACT.Copy).then_inc(S["ot_ready"], 1)

                    def step(b, bi):
                        st = stages(bi)
                        for u in range(UNITS):
                            if "attend" in st:
                                g, t = divmod(u, NT)
                                for half in (0, 1):
                                    n = b * UNITS * 2 + u * 2 + half
                                    act.wait_ge(S["b_full"], n + 1)
                                    if half == 0 and not (isinstance(b, int) and b == 0 and u < 4):
                                        act.wait_ge(S["pv_done"], b * UNITS + u - 3)
                                    nc.scalar.activation(
                                        P[:, u % 4, 2 * half:2 * half + 2, q0(t):T],
                                        PB[half][:, :].rearrange("p (j s) -> p j s", j=2)[:, :, q0(t):T],
                                        ACT.Exp).then_inc(S["p_ready"], 1)
                                if t == 0 and g > 0:
                                    first = isinstance(b, int) and b == 0 and g == 1
                                    drain_group(b, bi, g - 1, None if first else misc_count(b, bi, 4 * g - 2))
                            if "finish" in st and u == 0:
                                drain_group(b - 1, bi - 1, NG - 1, misc_count(b, bi, 0))
                            if u in MISC:
                                evict(b, bi, u)
                    run_steps(act, step)

                @block.gpsimd
                def _(pool):
                    def split(b, bi, k):
                        n = KROWS if k else D
                        src = QS[0:n, k, :]
                        pool.wait_ge(S["misc_free"], misc_count(b, bi, 5 if k else 3))
                        if not (isinstance(b, int) and b == FIRST_STEP):
                            pool.wait_ge(S["k_scratch" if k else "q_scratch"], (b + 2) * 16 * SPLITS)
                        base = (b + 2) * 8 + k * 4
                        cnt = [0]

                        def link(ins):
                            cnt[0] += 1
                            ins.then_inc(S["split"], 1)
                            pool.wait_ge(S["split"], base + cnt[0])
                        link(pool.tensor_tensor(SPL[0:n, k, 0, :], src, zero[0:n, :].to_broadcast([n, T]), ALU.add))
                        link(pool.tensor_tensor(RES[0:n, :], src, SPL[0:n, k, 0, :], ALU.subtract))
                        link(pool.tensor_tensor(SPL[0:n, k, 1, :], RES[0:n, :], zero[0:n, :].to_broadcast([n, T]), ALU.add))
                        link(pool.tensor_tensor(SPL[0:n, k, 2, :], RES[0:n, :], SPL[0:n, k, 1, :], ALU.subtract))

                    def split_max(b, bi, g, read_before):
                        n = b * NG + g
                        pool.wait_ge(S["a_free"], (n + 1) * HG * NT)
                        if not (isinstance(b, int) and b == 0 and g == 0):
                            pool.wait_ge(S["m_split"], n)
                        if read_before is not None:
                            pool.wait_ge(S["misc_free"], read_before)
                        zeros_m = zero[:, :].unsqueeze(2).to_broadcast([128, NT, HG])
                        mx = MX[:, bi % 2, g, :, :]
                        pool.tensor_tensor(MS[:, g % 2, :, 0, :], zeros_m, mx, ALU.subtract).then_inc(S["m_chain"], 1)
                        pool.tensor_tensor(MR[:, :, :], zeros_m, mx, ALU.subtract).then_inc(S["m_chain"], 1)
                        pool.wait_ge(S["m_chain"], n * 2 + 2)
                        pool.tensor_tensor(MS[:, g % 2, :, 1, :], MR[:, :, :], MS[:, g % 2, :, 0, :],
                                           ALU.subtract).then_inc(S["m_split"], 1)

                    def rotate(b, bi):
                        pool.wait_ge(S["pre_ln"], (b + 3) * LN_LINKS)
                        if not (isinstance(b, int) and b == FIRST_STEP):
                            pool.wait_ge(S["misc_free"], misc_count(b, bi, 0))
                        xe = XN[:, :, :].rearrange("p i (f e) -> p i f e", e=2)[:, :, :, 0]
                        xo = XN[:, :, :].rearrange("p i (f e) -> p i f e", e=2)[:, :, :, 1]
                        cos, sin = rope_t[:, :, 0, :], rope_t[:, :, 1, :]
                        H = D // 2
                        base = (b + 2) * 5

                        pool.tensor_tensor(RT[:, 0], xe, cos, ALU.mult).then_inc(S["rope_chain"], 1)
                        pool.tensor_tensor(RT[:, 1], xo, sin, ALU.mult).then_inc(S["rope_chain"], 1)
                        pool.wait_ge(S["rope_chain"], base + 2)
                        pool.tensor_tensor(XR[:, :, 0:H], RT[:, 0], RT[:, 1], ALU.subtract).then_inc(S["rope_chain"], 1)
                        pool.wait_ge(S["rope_chain"], base + 3)
                        pool.tensor_tensor(RT[:, 0], xe, sin, ALU.mult).then_inc(S["rope_chain"], 1)
                        pool.tensor_tensor(RT[:, 1], xo, cos, ALU.mult).then_inc(S["rope_chain"], 1)
                        pool.wait_ge(S["rope_chain"], base + 5)
                        pool.tensor_tensor(XR[:, :, H:D], RT[:, 0], RT[:, 1], ALU.add).then_inc(S["xr_ready"], 1)

                    def step(b, bi):
                        st = stages(bi)
                        for u in range(UNITS):
                            if u == 0 and "project" in st and roped:
                                rotate(b, bi)
                            if u == 1 and "attend" in st:
                                split_max(b, bi, NG - 1, misc_count(b, bi, 0))
                            if u == 4 and "score" in st:
                                early = isinstance(b, int) and b == -1
                                split_max(b + 1, bi + 1, 0, None if early else misc_count(b, bi, 0))
                            if u == 10 and "score" in st:
                                early = isinstance(b, int) and b == -1
                                split_max(b + 1, bi + 1, 1, None if early else misc_count(b, bi, 8))
                            if u == 12 and "score" in st:
                                split_max(b + 1, bi + 1, 2, misc_count(b, bi, 11))
                            if u in (5, 7) and "project" in st:
                                split(b, bi, int(u == 7))
                    run_steps(pool, step)

                @block.vector
                def _(v):
                    v.wait_ge(loaded_w, LOADED_W)
                    if before:
                        v.wait_ge(*before)
                    else:
                        v.wait_ge(loaded_x, 32)

                    def pre(b, bi):
                        if not (isinstance(b, int) and b == FIRST_STEP):
                            v.wait_ge(S["xr_ready"] if roped else S["misc_free"],
                                      b + 2 if roped else misc_count(b, bi, 0))
                        n = layer_norm(v, lambda i: xcols(b + 2, i), lambda i: XN[:, i, :], 1e-5, S["pre_ln"],
                                       (b + 2) * LN_LINKS)
                        assert n == LN_LINKS

                    def maxima(b, bi, u, half):
                        for i in (2 * half, 2 * half + 1):
                            v.wait_ge(S["a_full"], b * UNITS * NT + u * NT + i + 1)
                            nc.vector.tensor_reduce(MX[:, bi % 2, u // HG, i, u % HG:u % HG + 1], PA[i % 2][:, 0:keys(i)],
                                                    AX.X, ALU.max).then_inc(S["a_free"], 1)

                    def normalise(b, bi, u, g, ob):
                        misc_evict(v, b, bi, u)
                        o = PM[:, :].rearrange("p (i h c) -> p i h c", i=NT, h=HG)
                        n = ob * NG + g
                        nc.vector.reciprocal(RL[:, :, :], o[:, :, :, HD]).then_inc(S["rl_ready"], 1)
                        v.wait_ge(S["rl_ready"], n + 1)
                        nc.vector.tensor_tensor(
                            XO[:, :, g * HG * HD:(g + 1) * HG * HD].rearrange("p i (h d) -> p i h d", d=HD),
                            o[:, :, :, 0:HD], RL[:, :, :].unsqueeze(3).to_broadcast([128, NT, HG, HD]),
                            ALU.mult).then_inc(S["misc_free"], 1)

                    def post(b, bi, u):
                        ob = b - 1
                        misc_evict(v, b, bi, u)
                        pm = PM[:, :].rearrange("p (i d) -> p i d", i=NT)
                        if bias:
                            ins = nc.vector.tensor_tensor(
                                Y[:, :, :], pm, row(bias).unsqueeze(1).to_broadcast([128, NT, D]), ALU.add)
                        else:
                            ins = nc.vector.tensor_copy(Y[:, :, :], pm)
                        ins.then_inc(S["misc_free"], 1)
                        v.wait_ge(S["misc_free"], misc_count(b, bi, u))
                        layer_norm(v, lambda i: Y[:, i, :], lambda i: Y[:, i, :], 1e-5, S["post_ln"], ob * LN_LINKS)
                        xb = X[:, bass.ds(ob * T, T)]
                        nc.vector.tensor_tensor(xb, xb, Y[:, :, :].rearrange("p i d -> p (i d)"),
                                                ALU.add).then_inc(S["x_done"], 1)

                    def read_item(b, bi, u):
                        item, stage = MISC[u]
                        if stage not in stages(bi):
                            return
                        if item[0:2] == "oT":
                            g = int(item[2])
                            normalise(b, bi, u, g, b - 1 if g == NG - 1 else b)
                        elif item[0] == "m":
                            misc_evict(v, b, bi, u)
                            g = int(item[1])
                            mb = b if item == "m3" else b + 1
                            n = mb * NG + g
                            if not (isinstance(mb, int) and mb == 0 and g < 2):
                                v.wait_ge(m_loaded[(g + 2) % NG], (mb + 1 if g >= 2 else mb) * 16 * MAX_PARTS)
                            nc.vector.tensor_copy(MT[:, g % 2, :], PMb[0:MAX_PARTS * HG, 0:T]).then_inc(S["misc_free"], 1)
                        elif item == "out":
                            post(b, bi, u)

                    def step(b, bi):
                        st = stages(bi)
                        for u in range(UNITS):
                            if u == 0 and "project" in st:
                                pre(b, bi)
                            if "score" in st:
                                maxima(b + 1, bi + 1, u, 0)
                            if u - 1 in MISC:
                                read_item(b, bi, u - 1)
                            if "score" in st:
                                maxima(b + 1, bi + 1, u, 1)
                    run_steps(v, step)
                    v.wait_ge(S["x_done"], NB)

                @block.sync
                def _(sp):
                    def to_scratch(b, bi, k):
                        sp.wait_ge(S["split"], (b + 2) * 8 + 4 * (k + 1))
                        heads = kv_heads if k else NH
                        for s in range(SPLITS):
                            dst = scratch["k" if k else "q"][bi % 2, s * HD:(s + 1) * HD, 0:heads * T]
                            sp.dma_start(dst.rearrange("d (h t) -> h d t", h=heads),
                                         SPL[0:heads * HD, k, s, :]).then_inc(S["k_scratch" if k else "q_scratch"], 16)

                    def load_group(b, bi, g):
                        sp.wait_ge(S["q_scratch"], (b + 3) * 16 * SPLITS)
                        sp.wait_ge(S["k_scratch"], (b + 3) * 16 * SPLITS)
                        if "attend" in stages(bi):
                            sp.wait_ge(S["b_full"], (b * UNITS + (g + 1) * NT) * 2)
                        sk, sq = scratch["k"][bi % 2], scratch["q"][bi % 2]
                        n = SPLITS * HD
                        kc = slice(g * kg * T, (g + 1) * kg * T)
                        qc = slice(g * HG * T, (g + 1) * HG * T)
                        kd = KO[:, bi % 2].rearrange("p h t -> p (h t)")
                        qd = QO[:, bi % 2].rearrange("p h t -> p (h t)")
                        for s in range(SPLITS):
                            sp.dma_start(kd[n * s:n * (s + 1), kc], sk[:, kc]).then_inc(qk_loaded[g], 16)
                            cut = s * HD
                            sp.dma_start(qd[n * s:n * (s + 1) - cut, qc], sq[cut:n, qc]).then_inc(qk_loaded[g], 16)
                            if s:
                                sp.dma_start(qd[n * (s + 1) - cut:n * (s + 1), qc], sq[0:cut, qc]).then_inc(qk_loaded[g], 16)

                    def load_max(mb, mbi, g, item):
                        sp.wait_ge(S["misc_free"], item)
                        for c in range(MAX_PARTS):
                            sp.dma_start(QO[MAX_ROW + c:MAX_ROW + c + 1, mbi % 2, g * HG:(g + 1) * HG, :],
                                         MT[c * HG:(c + 1) * HG, g % 2, :]).then_inc(m_loaded[g], 16)

                    sp.wait_ge(consts, CONSTS)

                    def step(b, bi):
                        st = stages(bi)
                        if "project" in st:
                            to_scratch(b, bi, 0)
                            to_scratch(b, bi, 1)
                        if "attend" in st:
                            load_max(b, bi, NG - 1, misc_count(b, bi, 8))
                        if "project" in st:
                            load_group(b, bi, 0)
                            load_group(b, bi, 1)
                        if "score" in st:
                            load_max(b + 1, bi + 1, 0, misc_count(b, bi, 11))
                            load_max(b + 1, bi + 1, 1, misc_count(b, bi, 12))
                        if "project" in st:
                            load_group(b, bi, 2)
                        if "score" in st:
                            load_max(b + 1, bi + 1, 2, misc_count(b, bi, 13))
                        if "project" in st:
                            load_group(b, bi, 3)
                    run_steps(sp, step)
            return S["x_done"], NB

        first = attention("a1", False, NH, "wq1", "wk1", "wv1", "wu1", "bu", 128.0 ** -0.25, 128.0 ** -0.25,
                          None, False)

        def after_zt(k):
            at = NB * T + k * NB * NT * NE
            return arena[:, at:at + NB * NT * NE].rearrange("p (t e) -> p t e", e=NE)

        ZT = arena[:, 0:NB * T]
        LG = after_zt(0)
        TOP = arena[:, NB * T + 2 * NB * NT * NE:NB * T + 2 * NB * NT * NE + NB * NT]
        GT = after_zt(1)
        CMP = ops[:, 0:2 * NB * NT * NE * NE].bitcast(F32).rearrange("p (t e j) -> p t e j", e=NE, j=NE)
        EQ = ops[:, 2 * NB * NT * NE * NE:4 * NB * NT * NE * NE].bitcast(F32).rearrange(
            "p (t e j) -> p t e j", e=NE, j=NE)
        TB = NB * NT

        r_ln, r_zt, r_zt_ps, r_zr, r_lg_ps, r_lg = (sem(n) for n in (
            "r_ln", "r_zt", "r_zt_ps", "r_zr", "r_lg_ps", "r_lg"))
        r_soft, r_exp, r_gates = sem("r_soft"), sem("r_exp"), sem("r_gates")

        with nc.Block() as block:
            @block.vector
            def _(v):
                v.wait_ge(*first)
                with v.Fori(0, NB) as b:
                    layer_norm(v, lambda i: xcols(b, i), lambda i: XN[:, i, :], 1e-5, r_ln, b * 2 * LN_LINKS)
                    layer_norm(v, lambda i: XN[:, i, :], lambda i: Y[:, i, :], 1e-6, r_ln, (b * 2 + 1) * LN_LINKS)
                    v.wait_ge(r_zt, b + 1)
                    nc.vector.tensor_scalar(XOT[:, :], ZT[:, bass.ds(b * T, T)], w("router_s"), w("router_t"),
                                            ALU.mult, ALU.add).then_inc(r_zr, 1)
                    v.wait_ge(r_lg_ps, b + 1)
                    nc.vector.tensor_tensor(LG[:, :, :].rearrange("p t e -> p (t e)")[:, bass.ds(b * NT * NE, NT * NE)]
                                            .rearrange("p (t e) -> p t e", e=NE),
                                            PB[0][:, 0:NT * NE].rearrange("p (t e) -> p t e", e=NE),
                                            row("router_b").unsqueeze(1).to_broadcast([128, NT, NE]),
                                            ALU.add).then_inc(r_lg, 1)
                v.wait_ge(r_lg, NB)
                n = [0]

                def link(ins):
                    n[0] += 1
                    ins.then_inc(r_soft, 1)
                    v.wait_ge(r_soft, n[0])

                def over_e(ap):
                    return ap.unsqueeze(2).to_broadcast([128, TB, NE])
                link(nc.vector.tensor_reduce(TOP[:, :], LG[:, :, :], AX.X, ALU.max))
                link(nc.vector.tensor_tensor(LG[:, :, :], LG[:, :, :], over_e(TOP[:, :]), ALU.subtract))
                v.wait_ge(r_exp, 1)
                link(nc.vector.tensor_reduce(TOP[:, :], LG[:, :, :], AX.X, ALU.add))
                link(nc.vector.reciprocal(TOP[:, :], TOP[:, :]))
                link(nc.vector.tensor_tensor(LG[:, :, :], LG[:, :, :], over_e(TOP[:, :]), ALU.mult))
                pj = LG[:, :, :].unsqueeze(2).to_broadcast([128, TB, NE, NE])
                pe_ = LG[:, :, :].unsqueeze(3).to_broadcast([128, TB, NE, NE])
                earlier = row("earlier").rearrange("p (e j) -> p e j", j=NE).unsqueeze(1).to_broadcast([128, TB, NE, NE])
                link(nc.vector.tensor_tensor(EQ, pj, pe_, ALU.is_equal))
                link(nc.vector.tensor_tensor(EQ, EQ, earlier, ALU.mult))
                link(nc.vector.tensor_tensor(CMP, pj, pe_, ALU.is_gt))
                link(nc.vector.tensor_tensor(CMP, CMP, EQ, ALU.add))
                link(nc.vector.tensor_reduce(GT[:, :, :], CMP, AX.X, ALU.add))
                link(nc.vector.scalar_tensor_tensor(out=GT[:, :, :], in0=GT[:, :, :], scalar=1.5, in1=LG[:, :, :],
                                                    op0=ALU.is_lt, op1=ALU.mult))
                link(nc.vector.tensor_reduce(TOP[:, :], GT[:, :, :], AX.X, ALU.add))
                link(nc.vector.reciprocal(TOP[:, :], TOP[:, :]))
                nc.vector.tensor_tensor(GT[:, :, :], GT[:, :, :], over_e(TOP[:, :]), ALU.mult).then_inc(r_gates, 1)

            @block.tensor
            def _(pe):
                with pe.Fori(0, NB) as b:
                    pe.wait_ge(r_ln, (b + 1) * 2 * LN_LINKS)
                    for i in range(NT):
                        m = pe.transpose(PM[:, i * 128:(i + 1) * 128], Y[:, i, :], ident)
                    m.then_inc(r_zt_ps, 1)
                    pe.wait_ge(r_zr, b + 1)
                    for i in range(NT):
                        m = pe.matmul(PB[0][:, i * NE:(i + 1) * NE], XOT[:, i * 128:(i + 1) * 128], w("router_w"),
                                      start=True, stop=True)
                    m.then_inc(r_lg_ps, 1)

            @block.scalar
            def _(act):
                with act.Fori(0, NB) as b:
                    act.wait_ge(r_zt_ps, b + 1)
                    nc.scalar.activation(ZT[:, bass.ds(b * T, T)], PM[:, :], ACT.Copy).then_inc(r_zt, 1)
                act.wait_ge(r_soft, 2)
                nc.scalar.activation(LG[:, :, :], LG[:, :, :], ACT.Exp).then_inc(r_exp, 1)

        ZE = [XNT[:, 0, :], XNT[:, 1, :]]
        HT = ops[:, 0:2 * 2 * HB * T].bitcast(F32).rearrange("p (c k t) -> p c k t", c=2, k=HB)
        GS = SPL[:, 0, 0, 0:2 * NT * NE].bitcast(F32)
        e_ze, e_h_ps, e_h, e_y_ps, e_acc, e_gs, e_ln, e_x = (sem(n) for n in (
            "e_ze", "e_h_ps", "e_h", "e_y_ps", "e_acc", "e_gs", "e_ln", "e_x"))
        with nc.Block() as block:
            @block.vector
            def _(v):
                v.wait_ge(r_gates, 1)
                with v.Fori(0, NB) as b:
                    def scale(e):
                        if e >= 2:
                            v.wait_ge(e_h_ps, b * NE * HB + (e - 1) * HB)
                        nc.vector.tensor_scalar(ZE[e % 2], ZT[:, bass.ds(b * T, T)],
                                                w("expert_s")[:, e:e + 1], w("expert_t")[:, e:e + 1],
                                                ALU.mult, ALU.add).then_inc(e_ze, 1)

                    def add(e):
                        v.wait_ge(e_y_ps, b * NE + e + 1)
                        for i in range(NT):
                            ins = nc.vector.scalar_tensor_tensor(
                                out=Y[:, i, :], in0=PA[e % 2][:, i * 128:(i + 1) * 128],
                                scalar=GS[:, i * NE + e:i * NE + e + 1], in1=Y[:, i, :], op0=ALU.mult, op1=ALU.add)
                        ins.then_inc(e_acc, 1)
                        v.wait_ge(e_acc, b * 2 * NE + NE + e + 1)

                    nc.vector.tensor_copy(GS[:, :], GT[:, :, :].rearrange("p t e -> p (t e)")[
                        :, bass.ds(b * NT * NE, NT * NE)]).then_inc(e_gs, 1)
                    v.wait_ge(e_gs, b + 1)
                    scale(0)
                    scale(1)
                    for e in range(NE):
                        b2 = row("b2")[:, e * D:(e + 1) * D]
                        for i in range(NT):
                            gate = GS[:, i * NE + e:i * NE + e + 1]
                            if e == 0:
                                ins = nc.vector.tensor_scalar(Y[:, i, :], b2, gate, None, ALU.mult)
                            else:
                                ins = nc.vector.scalar_tensor_tensor(out=Y[:, i, :], in0=b2, scalar=gate,
                                                                     in1=Y[:, i, :], op0=ALU.mult, op1=ALU.add)
                        ins.then_inc(e_acc, 1)
                        v.wait_ge(e_acc, b * 2 * NE + e + 1)
                    for e in range(NE):
                        if e + 2 < NE:
                            scale(e + 2)
                        add(e)
                    layer_norm(v, lambda i: Y[:, i, :], lambda i: Y[:, i, :], 1e-5, e_ln, b * LN_LINKS)
                    xb = X[:, bass.ds(b * T, T)]
                    nc.vector.tensor_tensor(xb, xb, Y[:, :, :].rearrange("p i d -> p (i d)"),
                                            ALU.add).then_inc(e_x, 1)

            @block.tensor
            def _(pe):
                pe.wait_ge(loaded_mw, 32)

                def hidden(b, e):
                    pe.wait_ge(e_ze, b * NE + e + 1)
                    for k in range(HB):
                        if e:
                            pe.wait_ge(e_h, b * NE * HB + (e - 1) * HB + k + 1)
                        pe.matmul(PB[k // 2][:, (k % 2) * 512:(k % 2 + 1) * 512],
                                  W1[:, e * HID + k * 128:e * HID + (k + 1) * 128], ZE[e % 2],
                                  start=True, stop=True).then_inc(e_h_ps, 1)

                with pe.Fori(0, NB) as b:
                    hidden(b, 0)
                    for e in range(NE):
                        if e + 1 < NE:
                            hidden(b, e + 1)
                        pe.wait_ge(e_h, b * NE * HB + (e + 1) * HB)
                        if e >= 2:
                            pe.wait_ge(e_acc, b * 2 * NE + NE + e - 1)
                        for i in range(NT):
                            for k in range(HB):
                                m = pe.matmul(PA[e % 2][:, i * 128:(i + 1) * 128],
                                              HT[:, e % 2, k, i * 128:(i + 1) * 128],
                                              W2[:, (e * HB + k) * D:(e * HB + k + 1) * D],
                                              start=(k == 0), stop=(k == HB - 1))
                        m.then_inc(e_y_ps, 1)

            @block.scalar
            def _(act):
                with act.Fori(0, NB) as b:
                    for e in range(NE):
                        for k in range(HB):
                            if e >= 2 and k == 0:
                                act.wait_ge(e_y_ps, b * NE + e - 1)
                            act.wait_ge(e_h_ps, b * NE * HB + e * HB + k + 1)
                            nc.scalar.activation(HT[:, e % 2, k, :], PB[k // 2][:, (k % 2) * 512:(k % 2 + 1) * 512],
                                                 ACT.Gelu, bias=w("b1")[:, e * HB + k:e * HB + k + 1]).then_inc(e_h, 1)

            @block.gpsimd
            def _(pool):
                pool.wait_ge(e_x, NB)
                pool.memset(ops[:, :], 0.0).then_inc(consts, 1)
                pool.wait_ge(consts, CONSTS + 1)
                pool.memset(KO[MAX_ROW:MAX_ROW + MAX_PARTS], 1.0).then_inc(consts, 1)
                pool.wait_ge(consts, CONSTS + 2)

        second = attention("a2", True, NG, "wq2", "wk2", "wv2", "wo2", None, HD ** -0.5, 1.0, (e_x, NB), True)

        XS = arena[:, 0:T + 1]
        MU = arena[:, 2 * T:2 * T + 2]
        f_const, f_ln, f_xs_ps, f_xs, f_mix, f_k_ps, f_k, f_k2, f_out_ps, f_sig, f_gated, f_post, f_x = (
            sem(n) for n in ("f_const", "f_ln", "f_xs_ps", "f_xs", "f_mix", "f_k_ps", "f_k", "f_k2", "f_out_ps",
                             "f_sig", "f_gated", "f_post", "f_x"))
        with nc.Block() as block:
            @block.vector
            def _(v):
                v.wait_ge(*second)
                nc.vector.memset(XS[:, 0:1], 0.0).then_inc(f_const, 1)
                for k, name in enumerate(("mu_r", "mu_k")):
                    nc.vector.tensor_scalar(MU[:, k:k + 1], w(name), -1.0, 1.0, ALU.mult,
                                            ALU.add).then_inc(f_const, 1)
                v.wait_ge(f_const, 3)
                with v.Fori(0, NB) as b:
                    layer_norm(v, lambda i: xcols(b, i), lambda i: XN[:, i, :], 1e-5, f_ln, b * LN_LINKS)
                    v.wait_ge(f_xs, b + 1)
                    for k, name in enumerate(("mu_r", "mu_k")):
                        nc.vector.tensor_scalar(QS[:, k, :], XS[:, 0:T], MU[:, k:k + 1], None,
                                                ALU.mult).then_inc(f_mix, 1)
                    v.wait_ge(f_mix, b * 4 + 2)
                    for k, name in enumerate(("mu_r", "mu_k")):
                        nc.vector.scalar_tensor_tensor(out=QS[:, k, :], in0=XS[:, 1:T + 1], scalar=w(name),
                                                       in1=QS[:, k, :], op0=ALU.mult, op1=ALU.add).then_inc(f_mix, 1)
                    v.wait_ge(f_k, b + 1)
                    nc.vector.tensor_tensor(OT[:, :], OT[:, :], OT[:, :], ALU.mult).then_inc(f_k2, 1)
                    v.wait_ge(f_sig, b + 1)
                    v.wait_ge(f_out_ps, b + 1)
                    nc.vector.tensor_tensor(Y[:, :, :].rearrange("p i d -> p (i d)"), PA[1][:, :], XOT[:, :],
                                            ALU.mult).then_inc(f_gated, 1)
                    v.wait_ge(f_gated, b + 1)
                    layer_norm(v, lambda i: Y[:, i, :], lambda i: Y[:, i, :], 1e-5, f_post, b * LN_LINKS)
                    xb = X[:, bass.ds(b * T, T)]
                    nc.vector.tensor_tensor(xb, xb, Y[:, :, :].rearrange("p i d -> p (i d)"),
                                            ALU.add).then_inc(f_x, 1)

            @block.tensor
            def _(pe):
                with pe.Fori(0, NB) as b:
                    pe.wait_ge(f_ln, (b + 1) * LN_LINKS)
                    for i in range(NT):
                        m = pe.transpose(PM[:, i * 128:(i + 1) * 128], XN[:, i, :], ident)
                    m.then_inc(f_xs_ps, 1)
                    pe.wait_ge(f_mix, b * 4 + 4)
                    pe.matmul(PA[0][:, :], w("wkk"), QS[:, 1, :], start=True, stop=True).then_inc(f_k_ps, 1)
                    for i in range(NT):
                        m = pe.matmul(PB[0][:, i * 128:(i + 1) * 128], QS[:, 0, i * 128:(i + 1) * 128], w("wr"),
                                      start=True, stop=True)
                    m.then_inc(f_k_ps, 1)
                    pe.wait_ge(f_k2, b + 1)
                    for i in range(NT):
                        m = pe.matmul(PA[1][:, i * 128:(i + 1) * 128], OT[:, i * 128:(i + 1) * 128], w("wvv"),
                                      start=True, stop=True)
                    m.then_inc(f_out_ps, 1)

            @block.scalar
            def _(act):
                act.wait_ge(f_const, 3)
                with act.Fori(0, NB) as b:
                    act.wait_ge(f_xs_ps, b + 1)
                    nc.scalar.activation(XS[:, 1:T + 1], PM[:, :], ACT.Copy).then_inc(f_xs, 1)
                    act.wait_ge(f_k_ps, b * 2 + 1)
                    nc.scalar.activation(OT[:, :], PA[0][:, :], ACT.Relu).then_inc(f_k, 1)
                    act.wait_ge(f_k_ps, b * 2 + 2)
                    nc.scalar.activation(XOT[:, :], PB[0][:, 0:T], ACT.Sigmoid).then_inc(f_sig, 1)

            @block.sync
            def _(sp):
                with sp.Fori(0, NB) as b:
                    sp.wait_ge(f_x, b + 1)
                    sp.dma_start(out[bass.ds(b, 1)].rearrange("b (i p) d -> p (b i) d", p=128),
                                 X[:, bass.ds(b * T, T)].rearrange("p (c d) -> p c d", d=D)).then_inc(all_out, 16)
                sp.wait_ge(all_out, 16 * NB)


def kernel(**inputs):
    import numpy as _np
    import concourse.bacc as _bacc
    from concourse import mybir as _mybir
    from concourse.bass_utils import run_bass_kernel_spmd as _run

    a = {k: _np.asarray(v) for k, v in inputs.items()}
    columns = {
        "wq1": a["L0_attn_Wq"].T, "wk1": a["L0_attn_Wk"].T, "wv1": a["L0_attn_Wv"].T, "wu1": a["L0_attn_Wu"].T,
        "wq2": a["L1_attn_W_q"].T, "wk2": a["L1_attn_W_k"].T, "wv2": a["L1_attn_W_v"].T, "wo2": a["L1_attn_W_o"].T,
        "wr": a["L1_ffn_W_r"].T, "wkk": a["L1_ffn_W_k"].T, "wvv": a["L1_ffn_W_v"].T,
        "ident": _np.eye(128, dtype=_np.float32), "router_w": a["L0_ffn_router_w"].T,
        "router_s": a["L0_ffn_router_ln_scale"][:, None], "router_t": a["L0_ffn_router_ln_bias"][:, None],
        "expert_s": a["L0_ffn_expert_ln_scale"].T, "expert_t": a["L0_ffn_expert_ln_bias"].T,
        "b1": a["L0_ffn_b1"].reshape(NE * HB, 128).T,
        "mu_r": a["L1_ffn_mu_r"][:, None], "mu_k": a["L1_ffn_mu_k"][:, None],
    }
    rows = {"bu": a["L0_attn_bu"], "b2": a["L0_ffn_b2"].reshape(-1), "router_b": a["L0_ffn_router_b"],
            "earlier": _np.tril(_np.ones((NE, NE), dtype=_np.float32), k=-1).reshape(-1)}
    half = D // 2
    angle = (_np.arange(T, dtype=_np.float32)[:, None]
             * (1.0 / 10000.0 ** (_np.arange(half, dtype=_np.float32) / half)).astype(_np.float32)[None, :])
    arrays = {
        "x_dram": _np.ascontiguousarray(a["L0_attn_x"]),
        "weights_dram": _np.ascontiguousarray(_np.concatenate([columns[n] for n, _ in WCOLS], axis=1)),
        "rows_dram": _np.ascontiguousarray(_np.concatenate([rows[n] for n, _ in RCOLS])),
        "w1_dram": _np.ascontiguousarray(a["L0_ffn_w1"].transpose(2, 0, 1).reshape(D, NE * HID)),
        "w2_dram": _np.ascontiguousarray(a["L0_ffn_w2"].reshape(NE, D, HB, 128).transpose(3, 0, 2, 1)
                                         .reshape(128, NE * HB * D)),
        "rope_dram": _np.concatenate([_np.cos(angle), _np.sin(angle)], axis=1).astype(_np.float32),
        "mask_dram": _np.triu(_np.full((128, 128), -1e9, dtype=_np.float32), k=1),
    }
    nc = _bacc.Bacc("TRN2", target_bir_lowering=False, num_devices=1)
    args = [nc.dram_tensor(n, v.shape, _mybir.dt.from_np(v.dtype), kind="ExternalInput").ap()
            for n, v in arrays.items()]
    args.append(nc.dram_tensor("out_dram", (NB, T, D), _mybir.dt.float32, kind="ExternalOutput").ap())
    build(nc, *args)
    r = _run(nc, [arrays], core_ids=[0])
    return r.results[0]["out_dram"]
```

```python
from contextlib import ExitStack

import numpy as np

import concourse.bass as bass
from concourse import mybir

F32 = mybir.dt.float32
BF16 = mybir.dt.bfloat16
F32R = mybir.dt.float32r
ALU = mybir.AluOpType
ACT = mybir.ActivationFunctionType
AX = mybir.AxisListType

NB = 8
T = 512
D = 128
NT = T // 128
NH = 16
HD = D // NH
HG = 4
NG = NH // HG
UNITS = NG * NT
NE = 8
HID = 512
HB = HID // 128
SPLITS = 3
TERM_ROWS = SPLITS * SPLITS * HD
MAX_ROW = 96
MAX_PARTS = 2
ROWS = MAX_ROW + MAX_PARTS
LOADED_W = 64
CONSTS = 6

WCOLS = [("wq1", D), ("wk1", D), ("wv1", D), ("wu1", D), ("wq2", D), ("wk2", NG * HD), ("wv2", NG * HD),
         ("wo2", D), ("wr", D), ("wkk", D), ("wvv", D), ("ident", D), ("router_w", NE),
         ("router_s", 1), ("router_t", 1), ("expert_s", NE), ("expert_t", NE), ("b1", NE * HB), ("b2", NE),
         ("mu_r", 1), ("mu_k", 1)]
WAT, WN = {}, 0
for _name, _n in WCOLS:
    WAT[_name] = (WN, WN + _n)
    WN += _n
RCOLS = [("bu", D), ("router_b", NE), ("earlier", NE * NE)]
RAT, RN = {}, 0
for _name, _n in RCOLS:
    RAT[_name] = (RN, RN + _n)
    RN += _n

MISC = {2: ("oT3", "finish"), 3: ("xoT", "finish"), 4: ("xT", "project"), 5: ("oT0", "attend"),
        6: ("q", "project"), 7: ("k", "project"), 8: ("m3", "attend"), 9: ("out", "finish"),
        10: ("oT1", "attend"), 11: ("v", "score"), 12: ("m0", "score"), 13: ("m1", "score"),
        14: ("m2", "score"), 15: ("oT2", "attend")}
UNIT_OF = {item: u for u, (item, _) in MISC.items()}
FIRST_STEP, LAST_STEP = -2, NB
FULL = (1, NB - 3)


def stages(b):
    s = set()
    if b + 2 < NB:
        s.add("project")
    if 0 <= b + 1 < NB:
        s.add("score")
    if 0 <= b < NB:
        s.add("attend")
    if 0 <= b - 1:
        s.add("finish")
    return s


def misc_count(b, b_int, unit):
    st = stages(b_int)
    n = sum(1 for u in MISC if u <= unit and MISC[u][1] in st)
    n += sum(1 for s in range(FIRST_STEP, b_int) for u in MISC if MISC[u][1] in stages(s))
    return (b - b_int) * len(MISC) + n if not isinstance(b, int) else n


def run_steps(eng, step):
    for b in range(FIRST_STEP, FULL[0]):
        step(b, b)
    with eng.Fori(FULL[0], FULL[1], 2) as i:
        step(i, FULL[0])
        step(i + 1, FULL[0] + 1)
    for b in range(FULL[1], LAST_STEP + 1):
        step(b, b)


def run_pipeline(eng, depth, step):
    for s in range(depth):
        step(s, s)
    with eng.Fori(depth, NB - 1, 2) as i:
        step(i, depth)
        step(i + 1, depth + 1)
    for s in range(NB, NB + depth):
        step(s, s)


def has_work(s_int, k):
    return 0 <= s_int - k < NB


def build(nc, x_in, weights, rows, w1, w2, rope, mask, fill, out):
    with ExitStack() as ctx:
        def sb(name, shape, dt=F32):
            return ctx.enter_context(nc.sbuf_tensor(name, shape, dt))

        def psum(name, shape):
            return ctx.enter_context(nc.psum_tensor(name, shape, F32))

        def sem(name):
            return ctx.enter_context(nc.semaphore(name))

        X = sb("X", [128, NB * T])
        w_at = nc.sbuf_base
        W1 = sb("W1", [128, NE * HID])
        W2 = sb("W2", [128, NE * HB * D])
        ops_at = nc.sbuf_base
        ops = sb("ops", [128, 2 * 2 * NH * T], BF16)
        vo_at = nc.sbuf_base
        VO = sb("VO", [128, 2, NT, NH, 32])
        W = sb("W", [128, WN])
        R = sb("R", [128, RN])
        ident_b = sb("ident_b", [128, 128], BF16)
        mask_b = sb("mask_b", [128, 128], BF16)
        rope_t = sb("rope_t", [128, NT, 2, D // 2])
        stat = sb("stat", [128, 2, NT, 8])
        mv = sb("mv", [128, 2, NT, 2])
        ve = sb("ve", [128, 2, NT])
        rstd = sb("rstd", [128, 2, NT])
        eps5 = sb("eps5", [128, 1])
        eps6 = sb("eps6", [128, 1])
        minus_half = sb("minus_half", [128, 1])
        carry = sb("carry", [128, 2])
        QO = ops[:, 0:2 * NH * T].rearrange("p (c h t) -> p c h t", c=2, h=NH)
        KO = ops[:, 2 * NH * T:].rearrange("p (c h t) -> p c h t", c=2, h=NH)
        arena = sb("arena", [128, 4 * HG * T])
        P = arena[:, :].rearrange("p (r h t) -> p r h t", r=4, h=HG)
        XN = sb("XN", [128, NT, D])
        XR = sb("XR", [128, NT, D])
        RT = sb("RT", [128, 2, NT, D // 2])
        XNT = sb("XNT", [128, 2, T])
        QS = sb("QS", [128, 2, T])
        RES = sb("RES", [128, T])
        zero = sb("zero", [128, 1])
        SPL = sb("SPL", [128, 2, SPLITS, T], BF16)
        MX = sb("MX", [128, 2, NG, NT, HG])
        MR = sb("MR", [128, NT, HG])
        MS = sb("MS", [128, 2, NT, MAX_PARTS, HG], BF16)
        MT = sb("MT", [MAX_PARTS * HG, 2, T], BF16)
        OT = sb("OT", [128, T])
        RL = sb("RL", [128, NT, HG])
        XO = sb("XO", [128, NT, D])
        XOT = sb("XOT", [128, T])
        Y = sb("Y", [128, NT, D])

        PA = [psum("PA0", [128, 512]), psum("PA1", [128, 512])]
        PB = [psum("PB0", [128, 1024]), psum("PB1", [128, 1024])]
        PV = psum("PV", [128, 512])
        PM = psum("PM", [128, 512])
        PMb = PM[:, :].bitcast(BF16)

        scratch = {k: nc.dram_tensor(f"scratch_{k}", (2, SPLITS * HD, NH * T), BF16).ap() for k in ("q", "k")}

        def w(name):
            return W[:, WAT[name][0]:WAT[name][1]]

        def row(name):
            return R[:, RAT[name][0]:RAT[name][1]]

        ident = w("ident")
        loaded_x, loaded_w, loaded_mw = sem("loaded_x"), sem("loaded_w"), sem("loaded_mw")
        consts = sem("consts")
        cleared, filled = sem("cleared"), sem("filled")
        all_out = sem("all_out")

        def xcols(b, i):
            return X[:, bass.ds(b * T + i * D, D)]

        PRE, POST = 0, 1

        def stats_of(v, slot, src, chain, base):
            for i in range(NT):
                ins = nc.vector.bn_stats(stat[:, slot, i, 0:6], src(i))
            ins.then_inc(chain, 1)
            v.wait_ge(chain, base + 1)
            nc.vector.memset(stat[:, slot, 0, 6:7], 0.0)
            for i in range(NT):
                ins = nc.vector.bn_aggr(mv[:, slot, i, :], stat[:, slot, i, 0:6])
            ins.then_inc(chain, 1)

        def rstd_of(pool, slot, eps, stats, ready, chain, base):
            pool.wait_ge(stats, ready)
            pool.tensor_tensor(ve[:, slot, :], mv[:, slot, :, 1], eps[:, :].to_broadcast([128, NT]),
                               ALU.add).then_inc(chain, 1)
            pool.wait_ge(chain, base + 1)
            pool.tensor_tensor(rstd[:, slot, :], ve[:, slot, :], minus_half[:, :].to_broadcast([128, NT]),
                               ALU.pow).then_inc(chain, 1)

        def normalise(v, slot, src, dst, rstd_chain, ready, done):
            v.wait_ge(rstd_chain, ready)
            for i in range(NT):
                ins = nc.vector.tensor_scalar(dst(i), src(i), mv[:, slot, i, 0:1], rstd[:, slot, i:i + 1],
                                              ALU.subtract, ALU.mult)
            ins.then_inc(done, 1)

        VO_FLAT = VO[:, :, :, :, :].rearrange("p a b c d -> p (a b c d)")

        def clear_values(v, base):
            nc.vector.memset(VO_FLAT, 0.0).then_inc(cleared, 1)
            v.wait_ge(cleared, base + 1)
            nc.vector.memset(VO[:, :, :, :, HD:HD + 1], 1.0).then_inc(cleared, 1)
            v.wait_ge(cleared, base + 2)

        def fill_operands(sp):
            for k, o in enumerate((QO, KO)):
                sp.dma_start(o[TERM_ROWS:MAX_ROW].rearrange("p c h t -> p (c h t)").bitcast(F32),
                             fill[0:MAX_ROW - TERM_ROWS, :]).then_inc(filled, 16)
            sp.dma_start(KO[MAX_ROW:MAX_ROW + MAX_PARTS].rearrange("p c h t -> p (c h t)").bitcast(F32),
                         fill[MAX_ROW - TERM_ROWS:, :]).then_inc(filled, 16)
        FILLED = 48

        with nc.Block() as block:

            @block.sync
            def _(sp):
                sp.dma_start(X[:, 0:T].rearrange("p (i d) -> p i d", d=D),
                             x_in[0].rearrange("(i p) d -> p i d", p=128)).then_inc(loaded_x, 16)
                sp.dma_start(X[:, T:].rearrange("p (c d) -> p c d", d=D),
                             x_in[1:NB].rearrange("b (i p) d -> p (b i) d", p=128)).then_inc(loaded_x, 16)
                sp.dma_start(W[:, :], weights).then_inc(loaded_w, 16)
                sp.dma_start(R[:, :], rows.partition_broadcast(128)).then_inc(loaded_w, 16)
                sp.dma_start(rope_t[:, :, :, :].rearrange("p i c f -> p i (c f)"),
                             rope.rearrange("(i p) f -> p i f", p=128)).then_inc(loaded_w, 16)
                sp.dma_start(RES[:, 0:128], mask).then_inc(loaded_w, 16)
                fill_operands(sp)
                sp.wait_ge(filled, FILLED)
                sp.dma_start(W1[:, :], w1).then_inc(loaded_mw, 16)
                sp.dma_start(W2[:, :], w2).then_inc(loaded_mw, 16)


            @block.vector
            def _(v):
                clear_values(v, 0)

            @block.gpsimd
            def _(pool):
                for t, value in ((zero, 0.0), (eps5, 1e-5), (eps6, 1e-6), (minus_half, -0.5)):
                    pool.memset(t[:, :], value).then_inc(consts, 1)
                pool.wait_ge(loaded_w, LOADED_W)
                pool.tensor_copy(ident_b[:, :], ident).then_inc(consts, 1)
                pool.tensor_copy(mask_b[:, :], RES[:, 0:128]).then_inc(consts, 1)
                pool.wait_ge(consts, CONSTS)

        def attention(tag, causal, kv_heads, wq, wk, wv, wo, bias, q_scale, k_scale, before, roped):
            S = {n: sem(f"{tag}_{n}") for n in (
                "pre_stats", "pre_rstd", "pre_ln", "y_ready", "post_stats", "post_rstd", "post_ln", "xr_ready", "misc_full", "misc_free", "split", "q_scratch", "k_scratch",
                "a_full", "a_free", "m_chain", "m_split", "b_full", "p_ready", "pv_done",
                "ot_ready", "rl_ready", "x_done", "rope_chain")}
            qk_loaded = [sem(f"{tag}_qk_loaded{g}") for g in range(NG)]
            m_loaded = [sem(f"{tag}_m_loaded{g}") for g in range(NG)]
            MASKED = W1[:, 0:2 * T].rearrange("p (c t) -> p c t", c=2)
            mask_w = W1[:, 2 * T:3 * T]
            share = NH // kv_heads
            kg = HG // share
            KROWS = kv_heads * HD
            QK_DMAS = 8

            def keys(i):
                return (i + 1) * 128 if causal else T

            def q0(t):
                return t * 128 if causal else 0

            def misc_evict(eng, b, bi, u):
                eng.wait_ge(S["misc_full"], misc_count(b, bi, u))

            with nc.Block() as block:
                @block.tensor
                def _(pe):
                    pe.wait_ge(loaded_w, LOADED_W)
                    pe.wait_ge(consts, CONSTS)

                    def misc(b, bi, u):
                        item = MISC[u][0]
                        n = misc_count(b, bi, u)
                        if not (isinstance(n, int) and n == 1):
                            pe.wait_ge(S["misc_free"], n - 1)
                        if item == "xT":
                            pe.wait_ge(S["xr_ready"] if roped else S["pre_ln"], b + 3)
                            for i in range(NT):
                                m = pe.transpose(PM[:, i * 128:(i + 1) * 128], (XR if roped else XN)[:, i, :], ident)
                        elif item in ("q", "k"):
                            wt, n_out = (wq, D) if item == "q" else (wk, KROWS)
                            m = pe.matmul(PM[0:n_out, :], w(wt), XNT[:, bi % 2, :], start=True, stop=True)
                        elif item == "v":
                            for i in range(NT):
                                m = pe.matmul(PM[:, i * 128:i * 128 + KROWS], XNT[:, (bi + 1) % 2, i * 128:(i + 1) * 128],
                                              w(wv), start=True, stop=True)
                        elif item[0] == "m":
                            g = int(item[1])
                            mb = b if item == "m3" else b + 1
                            pe.wait_ge(S["m_split"], mb * NG + g + 1)
                            for i in range(NT):
                                m = pe.transpose(PMb[0:MAX_PARTS * HG, i * 128:(i + 1) * 128],
                                                 MS[:, g % 2, i, :, :].rearrange("p c h -> p (c h)"), ident_b[:, :])
                        elif item[0:2] == "oT":
                            g = int(item[2])
                            ob = b - 1 if g == NG - 1 else b
                            pe.wait_ge(S["ot_ready"], ob * NG + g + 1)
                            for i in range(NT):
                                m = pe.transpose(PM[:, i * 128:(i + 1) * 128], OT[:, i * 128:(i + 1) * 128], ident)
                        elif item == "xoT":
                            for i in range(NT):
                                m = pe.transpose(PM[:, i * 128:(i + 1) * 128], XO[:, i, :], ident)
                        else:
                            for i in range(NT):
                                m = pe.matmul(PM[:, i * 128:(i + 1) * 128], XOT[:, i * 128:(i + 1) * 128], w(wo),
                                              start=True, stop=True)
                        m.then_inc(S["misc_full"], 1)

                    def values(b, bi, u):
                        g, t = divmod(u, NT)
                        pe.wait_ge(S["p_ready"], (b * UNITS + u + 1) * 2)
                        if t == 0 and not (isinstance(b, int) and b == 0 and g == 0):
                            pe.wait_ge(S["ot_ready"], b * NG + g)
                        for j in range(HG):
                            kv = (g * HG + j) // share
                            m = pe.matmul(PV[32 * j:32 * j + 32, q0(t):T], VO[:, bi % 2, t, kv, :],
                                          P[:, u % 4, j, q0(t):T], start=(t == 0), stop=(t == NT - 1))
                        m.then_inc(S["pv_done"], 1)

                    def score_t(b, bi, u, half):
                        g, t = divmod(u, NT)
                        n = b * UNITS * 2 + u * 2 + half
                        if half == 0 and t == 0:
                            pe.wait_ge(m_loaded[g], (b + 1) * 16 * MAX_PARTS)
                        if not (isinstance(b, int) and b == 0 and u == 0):
                            pe.wait_ge(S["p_ready"], n - 1)
                        for j in range(2):
                            h = g * HG + half * 2 + j
                            kv = h // share
                            m = pe.matmul(PB[half][:, j * 512 + q0(t):j * 512 + T],
                                          KO[0:ROWS, bi % 2, kv, t * 128:(t + 1) * 128], QO[0:ROWS, bi % 2, h, q0(t):T],
                                          start=True, stop=not causal)
                            if causal:
                                at = j * 512 + q0(t)
                                m = pe.matmul(PB[half][:, at:at + 128], mask_b[:, :], ident_b[:, :],
                                              start=False, stop=True)
                        m.then_inc(S["b_full"], 1)

                    def score(b, bi, u, i):
                        kv = u // share
                        n = b * UNITS * NT + u * NT + i
                        if i == 0 and u % HG == 0:
                            pe.wait_ge(qk_loaded[u // HG], (b + 1) * 16 * QK_DMAS)
                        if not (isinstance(b, int) and b == 0 and u == 0 and i < 2):
                            pe.wait_ge(S["a_free"], n - 1)
                        m = pe.matmul(PA[i % 2][:, 0:keys(i)], QO[0:MAX_ROW, bi % 2, u, i * 128:(i + 1) * 128],
                                      KO[0:MAX_ROW, bi % 2, kv, 0:keys(i)], start=True, stop=True)
                        m.then_inc(S["a_full"], 1)

                    def step(b, bi):
                        st = stages(bi)
                        for u in range(UNITS):
                            if "score" in st:
                                score(b + 1, bi + 1, u, 0)
                            if "attend" in st:
                                score_t(b, bi, u, 0)
                            if "score" in st:
                                score(b + 1, bi + 1, u, 1)
                            if "attend" in st and u > 0:
                                values(b, bi, u - 1)
                            if "finish" in st and u == 0:
                                values(b - 1, bi - 1, UNITS - 1)
                            if "score" in st:
                                score(b + 1, bi + 1, u, 2)
                            if "attend" in st:
                                score_t(b, bi, u, 1)
                            if "score" in st:
                                score(b + 1, bi + 1, u, 3)
                            if u in MISC and MISC[u][1] in st:
                                misc(b, bi, u)
                    run_steps(pe, step)

                @block.scalar
                def _(act):
                    def evict(b, bi, u):
                        item, stage = MISC[u]
                        if stage not in stages(bi) or item not in ("xT", "q", "k", "v", "xoT"):
                            return
                        misc_evict(act, b, bi, u)
                        if item == "xT":
                            ins = nc.scalar.activation(XNT[:, bi % 2, :], PM[:, :], ACT.Copy)
                        elif item in ("q", "k"):
                            k = int(item == "k")
                            n_out = KROWS if k else D
                            if not (isinstance(b, int) and b == FIRST_STEP):
                                act.wait_ge(S["split"], (b + 1) * 8 + 4 * (k + 1))
                            ins = nc.scalar.activation(QS[0:n_out, k, :], PM[0:n_out, :], ACT.Copy,
                                                       scale=k_scale if k else q_scale)
                        elif item == "v":
                            ins = nc.scalar.activation(
                                VO[:, (bi + 1) % 2, :, 0:kv_heads, 0:HD],
                                PM[:, :].rearrange("p (i h d) -> p i h d", i=NT, d=HD)[:, :, 0:kv_heads, :], ACT.Copy)
                        else:
                            ins = nc.scalar.activation(XOT[:, :], PM[:, :], ACT.Copy)
                        ins.then_inc(S["misc_free"], 1)

                    def drain_group(b, bi, g, before_it):
                        act.wait_ge(S["pv_done"], b * UNITS + (g + 1) * NT)
                        if before_it is not None:
                            act.wait_ge(S["misc_free"], before_it)
                        nc.scalar.activation(OT[:, :], PV[:, :], ACT.Copy).then_inc(S["ot_ready"], 1)

                    def step(b, bi):
                        st = stages(bi)
                        for u in range(UNITS):
                            if "attend" in st:
                                g, t = divmod(u, NT)
                                for half in (0, 1):
                                    n = b * UNITS * 2 + u * 2 + half
                                    act.wait_ge(S["b_full"], n + 1)
                                    if half == 0 and not (isinstance(b, int) and b == 0 and u < 4):
                                        act.wait_ge(S["pv_done"], b * UNITS + u - 3)
                                    nc.scalar.activation(
                                        P[:, u % 4, 2 * half:2 * half + 2, q0(t):T],
                                        PB[half][:, :].rearrange("p (j s) -> p j s", j=2)[:, :, q0(t):T],
                                        ACT.Exp).then_inc(S["p_ready"], 1)
                                if t == 0 and g > 0:
                                    first = isinstance(b, int) and b == 0 and g == 1
                                    drain_group(b, bi, g - 1, None if first else
                                                misc_count(b, bi, UNIT_OF["oT3" if g == 1 else f"oT{g - 2}"]))
                            if "finish" in st and u == 0:
                                drain_group(b - 1, bi - 1, NG - 1, misc_count(b, bi, 0))
                            if u in MISC:
                                evict(b, bi, u)
                    run_steps(act, step)

                @block.gpsimd
                def _(pool):
                    def split(b, bi, k):
                        n = KROWS if k else D
                        src = QS[0:n, k, :]
                        pool.wait_ge(S["misc_free"], misc_count(b, bi, UNIT_OF["k" if k else "q"]))
                        if not (isinstance(b, int) and b == FIRST_STEP):
                            pool.wait_ge(S["k_scratch" if k else "q_scratch"], (b + 2) * 16 * SPLITS)
                        base = (b + 2) * 8 + k * 4
                        cnt = [0]

                        def link(ins):
                            cnt[0] += 1
                            ins.then_inc(S["split"], 1)
                            pool.wait_ge(S["split"], base + cnt[0])
                        link(pool.tensor_tensor(SPL[0:n, k, 0, :], src, zero[0:n, :].to_broadcast([n, T]), ALU.add))
                        link(pool.tensor_tensor(RES[0:n, :], src, SPL[0:n, k, 0, :], ALU.subtract))
                        link(pool.tensor_tensor(SPL[0:n, k, 1, :], RES[0:n, :], zero[0:n, :].to_broadcast([n, T]), ALU.add))
                        link(pool.tensor_tensor(SPL[0:n, k, 2, :], RES[0:n, :], SPL[0:n, k, 1, :], ALU.subtract))

                    def split_max(b, bi, g, read_before):
                        n = b * NG + g
                        pool.wait_ge(S["a_free"], (n + 1) * HG * NT)
                        if not (isinstance(b, int) and b == 0 and g == 0):
                            pool.wait_ge(S["m_split"], n)
                        if read_before is not None:
                            pool.wait_ge(S["misc_free"], read_before)
                        zeros_m = zero[:, :].unsqueeze(2).to_broadcast([128, NT, HG])
                        mx = MX[:, bi % 2, g, :, :]
                        pool.tensor_tensor(MS[:, g % 2, :, 0, :], zeros_m, mx, ALU.subtract).then_inc(S["m_chain"], 1)
                        pool.tensor_tensor(MR[:, :, :], zeros_m, mx, ALU.subtract).then_inc(S["m_chain"], 1)
                        pool.wait_ge(S["m_chain"], n * 2 + 2)
                        pool.tensor_tensor(MS[:, g % 2, :, 1, :], MR[:, :, :], MS[:, g % 2, :, 0, :],
                                           ALU.subtract).then_inc(S["m_split"], 1)

                    def rotate(b, bi):
                        pool.wait_ge(S["pre_ln"], b + 3)
                        if not (isinstance(b, int) and b == FIRST_STEP):
                            pool.wait_ge(S["misc_free"], misc_count(b, bi, 0))
                        xe = XN[:, :, :].rearrange("p i (f e) -> p i f e", e=2)[:, :, :, 0]
                        xo = XN[:, :, :].rearrange("p i (f e) -> p i f e", e=2)[:, :, :, 1]
                        cos, sin = rope_t[:, :, 0, :], rope_t[:, :, 1, :]
                        H = D // 2
                        base = (b + 2) * 5

                        pool.tensor_tensor(RT[:, 0], xe, cos, ALU.mult).then_inc(S["rope_chain"], 1)
                        pool.tensor_tensor(RT[:, 1], xo, sin, ALU.mult).then_inc(S["rope_chain"], 1)
                        pool.wait_ge(S["rope_chain"], base + 2)
                        pool.tensor_tensor(XR[:, :, 0:H], RT[:, 0], RT[:, 1], ALU.subtract).then_inc(S["rope_chain"], 1)
                        pool.wait_ge(S["rope_chain"], base + 3)
                        pool.tensor_tensor(RT[:, 0], xe, sin, ALU.mult).then_inc(S["rope_chain"], 1)
                        pool.tensor_tensor(RT[:, 1], xo, cos, ALU.mult).then_inc(S["rope_chain"], 1)
                        pool.wait_ge(S["rope_chain"], base + 5)
                        pool.tensor_tensor(XR[:, :, H:D], RT[:, 0], RT[:, 1], ALU.add).then_inc(S["xr_ready"], 1)

                    def step(b, bi):
                        st = stages(bi)
                        for u in range(UNITS):
                            if u == 0 and "project" in st:
                                rstd_of(pool, PRE, eps5, S["pre_stats"], (b + 3) * 2, S["pre_rstd"], (b + 2) * 2)
                            if u == 2 and "project" in st and roped:
                                rotate(b, bi)
                            if u == 1 and "attend" in st:
                                split_max(b, bi, NG - 1, misc_count(b, bi, 0))
                            if u == 5 and "score" in st:
                                early = isinstance(b, int) and b == -1
                                split_max(b + 1, bi + 1, 0, None if early else misc_count(b, bi, 0))
                            if u == 10 and "score" in st:
                                early = isinstance(b, int) and b == -1
                                split_max(b + 1, bi + 1, 1, None if early else misc_count(b, bi, UNIT_OF["m3"]))
                            if u == 13 and "score" in st:
                                split_max(b + 1, bi + 1, 2, misc_count(b, bi, UNIT_OF["m0"]))
                            if u in (7, 8) and "project" in st:
                                split(b, bi, int(u == 8))
                            if u == 11 and "finish" in st:
                                rstd_of(pool, POST, eps5, S["post_stats"], b * 2, S["post_rstd"], (b - 1) * 2)
                    run_steps(pool, step)

                @block.vector
                def _(v):
                    v.wait_ge(loaded_w, LOADED_W)
                    if before:
                        v.wait_ge(*before)
                    else:
                        v.wait_ge(loaded_x, 32)

                    def pre(b, bi):
                        if not (isinstance(b, int) and b == FIRST_STEP):
                            v.wait_ge(S["xr_ready"] if roped else S["misc_free"],
                                      b + 2 if roped else misc_count(b, bi, 0))
                        normalise(v, PRE, lambda i: xcols(b + 2, i), lambda i: XN[:, i, :], S["pre_rstd"],
                                  (b + 3) * 2, S["pre_ln"])

                    def maxima(b, bi, u, half):
                        for i in (2 * half, 2 * half + 1):
                            v.wait_ge(S["a_full"], b * UNITS * NT + u * NT + i + 1)
                            mx = MX[:, bi % 2, u // HG, i, u % HG:u % HG + 1]
                            if causal:
                                nc.vector.memset(carry[:, i % 2:i % 2 + 1], 0.0)
                                ins = nc.vector.tensor_tensor_reduce(
                                    out=MASKED[:, i % 2, 0:keys(i)], in0=PA[i % 2][:, 0:keys(i)],
                                    in1=mask_w[:, T - keys(i):T], scale=1.0, scalar=-3e38, op0=ALU.add, op1=ALU.max,
                                    accum_out=mx)
                            else:
                                ins = nc.vector.tensor_reduce(mx, PA[i % 2][:, 0:keys(i)], AX.X, ALU.max)
                            ins.then_inc(S["a_free"], 1)

                    def divide(b, bi, u, g, ob):
                        misc_evict(v, b, bi, u)
                        o = PM[:, :].rearrange("p (i h c) -> p i h c", i=NT, h=HG)
                        n = ob * NG + g
                        nc.vector.reciprocal(RL[:, :, :], o[:, :, :, HD]).then_inc(S["rl_ready"], 1)
                        v.wait_ge(S["rl_ready"], n + 1)
                        nc.vector.tensor_tensor(
                            XO[:, :, g * HG * HD:(g + 1) * HG * HD].rearrange("p i (h d) -> p i h d", d=HD),
                            o[:, :, :, 0:HD], RL[:, :, :].unsqueeze(3).to_broadcast([128, NT, HG, HD]),
                            ALU.mult).then_inc(S["misc_free"], 1)

                    def post(b, bi, u):
                        ob = b - 1
                        misc_evict(v, b, bi, u)
                        pm = PM[:, :].rearrange("p (i d) -> p i d", i=NT)
                        if bias:
                            ins = nc.vector.tensor_tensor(
                                Y[:, :, :], pm, row(bias).unsqueeze(1).to_broadcast([128, NT, D]), ALU.add)
                        else:
                            ins = nc.vector.tensor_copy(Y[:, :, :], pm)
                        ins.then_inc(S["misc_free"], 1)
                        v.wait_ge(S["misc_free"], misc_count(b, bi, u))
                        stats_of(v, POST, lambda i: Y[:, i, :], S["post_stats"], ob * 2)

                    def add(b):
                        ob = b - 1
                        normalise(v, POST, lambda i: Y[:, i, :], lambda i: Y[:, i, :], S["post_rstd"],
                                  (ob + 1) * 2, S["post_ln"])
                        v.wait_ge(S["post_ln"], ob + 1)
                        xb = X[:, bass.ds(ob * T, T)]
                        nc.vector.tensor_tensor(xb, xb, Y[:, :, :].rearrange("p i d -> p (i d)"),
                                                ALU.add).then_inc(S["x_done"], 1)

                    def read_item(b, bi, u):
                        item, stage = MISC[u]
                        if stage not in stages(bi):
                            return
                        if item[0:2] == "oT":
                            g = int(item[2])
                            divide(b, bi, u, g, b - 1 if g == NG - 1 else b)
                        elif item[0] == "m":
                            misc_evict(v, b, bi, u)
                            g = int(item[1])
                            mb = b if item == "m3" else b + 1
                            n = mb * NG + g
                            if not (isinstance(mb, int) and mb == 0 and g < 2):
                                v.wait_ge(m_loaded[(g + 2) % NG], (mb + 1 if g >= 2 else mb) * 16 * MAX_PARTS)
                            nc.vector.tensor_copy(MT[:, g % 2, :], PMb[0:MAX_PARTS * HG, 0:T]).then_inc(S["misc_free"], 1)
                        elif item == "out":
                            post(b, bi, u)

                    def step(b, bi):
                        st = stages(bi)
                        for u in range(UNITS):
                            if u == 0 and "project" in st:
                                stats_of(v, PRE, lambda i: xcols(b + 2, i), S["pre_stats"], (b + 2) * 2)
                            if "score" in st:
                                maxima(b + 1, bi + 1, u, 0)
                            if u == 2 and "project" in st:
                                pre(b, bi)
                            if u == 13 and "finish" in st:
                                add(b)
                            if u - 1 in MISC:
                                read_item(b, bi, u - 1)
                            if "score" in st:
                                maxima(b + 1, bi + 1, u, 1)
                        read_item(b, bi, UNITS - 1)
                    run_steps(v, step)
                    v.wait_ge(S["x_done"], NB)

                @block.sync
                def _(sp):
                    def to_scratch(b, bi, k):
                        sp.wait_ge(S["split"], (b + 2) * 8 + 4 * (k + 1))
                        heads = kv_heads if k else NH
                        for s in range(SPLITS):
                            dst = scratch["k" if k else "q"][bi % 2, s * HD:(s + 1) * HD, 0:heads * T]
                            sp.dma_start(dst.rearrange("d (h t) -> h d t", h=heads),
                                         SPL[0:heads * HD, k, s, :]).then_inc(S["k_scratch" if k else "q_scratch"], 16)

                    def load_group(b, bi, g):
                        sp.wait_ge(S["q_scratch"], (b + 3) * 16 * SPLITS)
                        sp.wait_ge(S["k_scratch"], (b + 3) * 16 * SPLITS)
                        if "attend" in stages(bi):
                            sp.wait_ge(S["b_full"], (b * UNITS + (g + 1) * NT) * 2)
                        sk, sq = scratch["k"][bi % 2], scratch["q"][bi % 2]
                        n = SPLITS * HD
                        kc = slice(g * kg * T, (g + 1) * kg * T)
                        qc = slice(g * HG * T, (g + 1) * HG * T)
                        kd = KO[:, bi % 2].rearrange("p h t -> p (h t)")
                        qd = QO[:, bi % 2].rearrange("p h t -> p (h t)")
                        for s in range(SPLITS):
                            sp.dma_start(kd[n * s:n * (s + 1), kc], sk[:, kc]).then_inc(qk_loaded[g], 16)
                            cut = s * HD
                            sp.dma_start(qd[n * s:n * (s + 1) - cut, qc], sq[cut:n, qc]).then_inc(qk_loaded[g], 16)
                            if s:
                                sp.dma_start(qd[n * (s + 1) - cut:n * (s + 1), qc], sq[0:cut, qc]).then_inc(qk_loaded[g], 16)

                    def load_max(mb, mbi, g, item):
                        sp.wait_ge(S["misc_free"], item)
                        for c in range(MAX_PARTS):
                            sp.dma_start(QO[MAX_ROW + c:MAX_ROW + c + 1, mbi % 2, g * HG:(g + 1) * HG, :],
                                         MT[c * HG:(c + 1) * HG, g % 2, :]).then_inc(m_loaded[g], 16)

                    sp.wait_ge(consts, CONSTS)

                    def step(b, bi):
                        st = stages(bi)
                        if "project" in st:
                            to_scratch(b, bi, 0)
                            to_scratch(b, bi, 1)
                        if "attend" in st:
                            load_max(b, bi, NG - 1, misc_count(b, bi, UNIT_OF["m3"]))
                        if "project" in st:
                            load_group(b, bi, 0)
                            load_group(b, bi, 1)
                        if "score" in st:
                            load_max(b + 1, bi + 1, 0, misc_count(b, bi, UNIT_OF["m0"]))
                            load_max(b + 1, bi + 1, 1, misc_count(b, bi, UNIT_OF["m1"]))
                        if "project" in st:
                            load_group(b, bi, 2)
                        if "score" in st:
                            load_max(b + 1, bi + 1, 2, misc_count(b, bi, UNIT_OF["m2"]))
                        if "project" in st:
                            load_group(b, bi, 3)
                    run_steps(sp, step)
            return S["x_done"], NB

        first = attention("a1", False, NH, "wq1", "wk1", "wv1", "wu1", "bu", 128.0 ** -0.25, 128.0 ** -0.25,
                          None, False)

        TB = NB * NT

        def cols(at, shape, dt=F32):
            n = int(np.prod(shape))
            names = "abc"[:len(shape)]
            ap = arena[:, at:at + n]
            if len(shape) == 1:
                return ap
            return ap.rearrange(f"p ({' '.join(names)}) -> p {' '.join(names)}",
                                **{names[k]: shape[k] for k in range(1, len(shape))})

        ZT = cols(0, [NB * T])
        LG = cols(NB * T, [TB, NE])
        GT = cols(NB * T + TB * NE, [TB, NE])
        TOP = cols(NB * T + 2 * TB * NE, [TB])
        GSB = cols(NB * T + 3 * TB * NE, [2 * 128])
        CMP = VO_FLAT[:, 0:TB * NE * NE].rearrange("p (t e j) -> p t e j", e=NE, j=NE)
        EQ = VO_FLAT[:, TB * NE * NE:2 * TB * NE * NE].rearrange("p (t e j) -> p t e j", e=NE, j=NE)
        gates_dram = nc.dram_tensor("gates", (NE, NB * T), F32).ap()

        def at(name, shape, offset):
            return nc.alloc_sbuf_tensor_at(name, shape, F32R, offset=offset)
        W1H, W1L = at("W1H", [128, NE * HID], ops_at), at("W1L", [128, NE * HID], ops_at + 4 * NE * HID)
        W2H = at("W2H", [128, NE * HID], ops_at + 8 * NE * HID)
        W2L = at("W2L", [128, NE * HID], ops_at + 12 * NE * HID)

        r_stats1, r_rstd1, r_ln1, r_stats2, r_rstd2, r_ln2, r_zt_ps, r_zt, r_zr, r_lg_ps, r_lg = (sem(n) for n in (
            "r_stats1", "r_rstd1", "r_ln1", "r_stats2", "r_rstd2", "r_ln2", "r_zt_ps", "r_zt", "r_zr", "r_lg_ps",
            "r_lg"))
        r_soft, r_exp, r_gates = sem("r_soft"), sem("r_exp"), sem("r_gates")
        g_ps, g_sb, g_out, w_high, w_low = (sem(n) for n in ("g_ps", "g_sb", "g_out", "w_high", "w_low"))
        ZRB = [XNT[:, 0, :], XNT[:, 1, :]]

        with nc.Block() as block:
            @block.vector
            def _(v):
                v.wait_ge(*first)

                def step(s, si):
                    if has_work(si, 4):
                        b = s - 4
                        v.wait_ge(r_lg_ps, b + 1)
                        nc.vector.tensor_tensor(
                            LG.rearrange("p t e -> p (t e)")[:, bass.ds(b * NT * NE, NT * NE)]
                            .rearrange("p (t e) -> p t e", e=NE),
                            PB[si % 2][:, 0:NT * NE].rearrange("p (t e) -> p t e", e=NE),
                            row("router_b").unsqueeze(1).to_broadcast([128, NT, NE]), ALU.add).then_inc(r_lg, 1)
                    if has_work(si, 2):
                        b = s - 2
                        if not (isinstance(s, int) and s == 2):
                            v.wait_ge(r_zt_ps, b)
                        normalise(v, POST, lambda i: XN[:, i, :], lambda i: Y[:, i, :], r_rstd2, (b + 1) * 2, r_ln2)
                    if has_work(si, 1):
                        b = s - 1
                        if not (isinstance(s, int) and s == 1):
                            v.wait_ge(r_ln2, b)
                        normalise(v, PRE, lambda i: xcols(b, i), lambda i: XN[:, i, :], r_rstd1, (b + 1) * 2, r_ln1)
                        v.wait_ge(r_ln1, b + 1)
                        stats_of(v, POST, lambda i: XN[:, i, :], r_stats2, b * 2)
                    if has_work(si, 0):
                        if not (isinstance(s, int) and s == 0):
                            v.wait_ge(r_ln1, s)
                        stats_of(v, PRE, lambda i: xcols(s, i), r_stats1, s * 2)
                run_pipeline(v, 4, step)

                v.wait_ge(r_lg, NB)
                n = [0]

                def link(ins):
                    n[0] += 1
                    ins.then_inc(r_soft, 1)
                    v.wait_ge(r_soft, n[0])

                def over_e(ap):
                    return ap.unsqueeze(2).to_broadcast([128, TB, NE])
                link(nc.vector.tensor_reduce(TOP, LG, AX.X, ALU.max))
                link(nc.vector.tensor_tensor(LG, LG, over_e(TOP), ALU.subtract))
                v.wait_ge(r_exp, 1)
                link(nc.vector.tensor_reduce(TOP, LG, AX.X, ALU.add))
                link(nc.vector.reciprocal(TOP, TOP))
                link(nc.vector.tensor_tensor(LG, LG, over_e(TOP), ALU.mult))
                pj = LG.unsqueeze(2).to_broadcast([128, TB, NE, NE])
                pe_ = LG.unsqueeze(3).to_broadcast([128, TB, NE, NE])
                earlier = row("earlier").rearrange("p (e j) -> p e j", j=NE).unsqueeze(1).to_broadcast([128, TB, NE, NE])
                link(nc.vector.tensor_tensor(EQ, pj, pe_, ALU.is_equal))
                link(nc.vector.tensor_tensor(EQ, EQ, earlier, ALU.mult))
                link(nc.vector.tensor_tensor(CMP, pj, pe_, ALU.is_gt))
                link(nc.vector.tensor_tensor(CMP, CMP, EQ, ALU.add))
                link(nc.vector.tensor_reduce(GT, CMP, AX.X, ALU.add))
                link(nc.vector.scalar_tensor_tensor(out=GT, in0=GT, scalar=1.5, in1=LG,
                                                    op0=ALU.is_lt, op1=ALU.mult))
                link(nc.vector.tensor_reduce(TOP, GT, AX.X, ALU.add))
                link(nc.vector.reciprocal(TOP, TOP))
                nc.vector.tensor_tensor(GT, GT, over_e(TOP), ALU.mult).then_inc(r_gates, 1)
                v.wait_ge(g_ps, 1)
                nc.vector.tensor_copy(GSB, PA[0][:, 0:256]).then_inc(g_sb, 1)

            @block.gpsimd
            def _(pool):
                def step(s, si):
                    if has_work(si, 1):
                        b = s - 1
                        rstd_of(pool, POST, eps6, r_stats2, (b + 1) * 2, r_rstd2, b * 2)
                    if has_work(si, 0):
                        rstd_of(pool, PRE, eps5, r_stats1, (s + 1) * 2, r_rstd1, s * 2)
                run_pipeline(pool, 4, step)
                for k, (full, high, low) in enumerate(((W1, W1H, W1L), (W2, W2H, W2L))):
                    pool.wait_ge(w_high, k + 1)
                    pool.tensor_tensor(low[:, :], full[:, :], high[:, :].bitcast(F32),
                                       ALU.subtract).then_inc(w_low, 1)
                pool.wait_ge(w_low, 2)

            @block.tensor
            def _(pe):
                def step(s, si):
                    if has_work(si, 2):
                        b = s - 2
                        pe.wait_ge(r_ln2, b + 1)
                        if not (isinstance(s, int) and s < 4):
                            pe.wait_ge(r_zr, b - 1)
                        for i in range(NT):
                            m = pe.transpose(PA[si % 2][:, i * 128:(i + 1) * 128], Y[:, i, :], ident)
                        m.then_inc(r_zt_ps, 1)
                        pe.wait_ge(r_zr, b + 1)
                        if not (isinstance(s, int) and s < 4):
                            pe.wait_ge(r_lg, b - 1)
                        for i in range(NT):
                            m = pe.matmul(PB[si % 2][:, i * NE:(i + 1) * NE], ZRB[si % 2][:, i * 128:(i + 1) * 128],
                                          w("router_w"), start=True, stop=True)
                        m.then_inc(r_lg_ps, 1)
                run_pipeline(pe, 4, step)
                pe.wait_ge(r_gates, 1)
                gates = GT.rearrange("p t e -> p (t e)")
                for k in range(2):
                    m = pe.transpose(PA[0][:, k * 128:(k + 1) * 128], gates[:, k * 128:(k + 1) * 128], ident)
                m.then_inc(g_ps, 1)

            @block.scalar
            def _(act):
                act.wait_ge(loaded_mw, 32)

                def step(s, si):
                    if has_work(si, 2):
                        b = s - 2
                        act.wait_ge(r_zt_ps, b + 1)
                        nc.scalar.activation(ZT[:, bass.ds(b * T, T)], PA[si % 2][:, :], ACT.Copy).then_inc(r_zt, 1)
                        if not (isinstance(s, int) and s < 4):
                            act.wait_ge(r_lg_ps, b - 1)
                        nc.scalar.activation(ZRB[si % 2], PA[si % 2][:, :], ACT.Identity, bias=w("router_t"),
                                             scale=w("router_s")).then_inc(r_zr, 1)
                run_pipeline(act, 4, step)
                act.wait_ge(r_soft, 2)
                nc.scalar.activation(LG, LG, ACT.Exp).then_inc(r_exp, 1)
                nc.scalar.activation(W1H[:, :], W1[:, :], ACT.Copy).then_inc(w_high, 1)
                nc.scalar.activation(W2H[:, :], W2[:, :], ACT.Copy).then_inc(w_high, 1)

            @block.sync
            def _(sp):
                sp.wait_ge(g_sb, 1)
                half = NB * T // 2
                for k in range(2):
                    sp.dma_start(gates_dram[:, k * half:(k + 1) * half].rearrange("e (t p) -> t e p", p=128),
                                 GSB[:, k * 128:(k + 1) * 128]).then_inc(g_out, 16)
                sp.wait_ge(g_out, 32)

        HH, HL = at("HH", [128, 2, HB, T], w_at), at("HL", [128, 2, HB, T], w_at + 8 * HB * T)
        ZH, ZL = at("ZH", [128, 2, T], vo_at), at("ZL", [128, 2, T], vo_at + 8 * T)
        G = nc.alloc_sbuf_tensor_at("G", [128, 2, T], F32, offset=vo_at + 16 * T)
        ZF = nc.alloc_sbuf_tensor_at("ZF", [128, T], F32, offset=vo_at + 24 * T)
        AT = nc.alloc_sbuf_tensor_at("AT", [128, T], F32, offset=vo_at + 28 * T)
        H = cols(NB * T + 2 * TB * NE, [HB, T])
        YG = cols(NB * T + 2 * TB * NE + HB * T, [T])
        e_zf, e_zh, e_zl, e_h_ps, e_h, e_hh, e_hl, e_y_ps, e_yg, e_acc, e_t_ps, e_y = (sem(n) for n in (
            "e_zf", "e_zh", "e_zl", "e_h_ps", "e_h", "e_hh", "e_hl", "e_y_ps", "e_yg", "e_acc", "e_t_ps",
            "e_y"))
        e_stats, e_rstd, e_ln, e_x = sem("e_stats"), sem("e_rstd"), sem("e_ln"), sem("e_x")

        e_g = [sem("e_g0"), sem("e_g1")]
        PV2 = PA

        def unless_first(b, cond=True):
            return not (isinstance(b, int) and b == 0) and cond

        with nc.Block() as block:
            def per_batch(eng, body):
                body(0)
                with eng.Fori(1, NB) as b:
                    body(b)

            @block.vector
            def _(v):
                def tokens(b, e):
                    n = b * NE + e
                    if unless_first(n):
                        v.wait_ge(e_zl, n)
                    nc.vector.tensor_scalar(ZF[:, :], ZT[:, bass.ds(b * T, T)], w("expert_s")[:, e:e + 1],
                                            w("expert_t")[:, e:e + 1], ALU.mult, ALU.add).then_inc(e_zf, 1)

                def leftovers(b, e, k):
                    n = b * NE + e
                    if k == 0 and not (isinstance(n, int) and n < 2):
                        v.wait_ge(e_y_ps, n - 1)
                    v.wait_ge(e_hh, n * HB + k + 1)
                    nc.vector.tensor_tensor(HL[:, e % 2, k, :], H[:, k, :], HH[:, e % 2, k, :].bitcast(F32),
                                            ALU.subtract).then_inc(e_hl, 1)

                def gather(b, e):
                    n = b * NE + e
                    v.wait_ge(e_g[e % 2], (b * (NE // 2) + e // 2 + 1) * 16)
                    v.wait_ge(e_y_ps, n + 1)
                    dst = AT[:, :] if e == 0 else YG
                    if e == 0 and unless_first(b):
                        v.wait_ge(e_t_ps, b)
                    if e >= 2:
                        v.wait_ge(e_acc, b * (NE - 1) + e - 1)
                    nc.vector.scalar_tensor_tensor(out=dst, in0=PV2[e % 2][:, :], scalar=w("b2")[:, e:e + 1],
                                                   in1=G[:, e % 2, :], op0=ALU.add, op1=ALU.mult).then_inc(e_yg, 1)
                    if e:
                        v.wait_ge(e_yg, n + 1)
                        nc.vector.tensor_tensor(AT[:, :], AT[:, :], YG, ALU.add).then_inc(e_acc, 1)

                def finish(b):
                    v.wait_ge(e_t_ps, b + 1)
                    nc.vector.tensor_copy(Y[:, :, :].rearrange("p i d -> p (i d)"), PM[:, :]).then_inc(e_y, 1)
                    v.wait_ge(e_y, b + 1)
                    stats_of(v, POST, lambda i: Y[:, i, :], e_stats, b * 2)

                def add(b):
                    normalise(v, POST, lambda i: Y[:, i, :], lambda i: Y[:, i, :], e_rstd, (b + 1) * 2, e_ln)
                    v.wait_ge(e_ln, b + 1)
                    xb = X[:, bass.ds(b * T, T)]
                    nc.vector.tensor_tensor(xb, xb, Y[:, :, :].rearrange("p i d -> p (i d)"),
                                            ALU.add).then_inc(e_x, 1)

                def body(b, last=False):
                    for e in range(NE):
                        for k in range(HB):
                            leftovers(b, e, k)
                            if k == 0:
                                if e + 2 < NE:
                                    tokens(b, e + 2)
                                elif not last:
                                    tokens(b + 1, e + 2 - NE)
                            if k == 1 and e >= 1:
                                gather(b, e - 1)
                            if k == 1 and e == 0 and unless_first(b):
                                gather(b - 1, NE - 1)
                            if k == 2 and e == 1 and unless_first(b):
                                finish(b - 1)
                            if k == 2 and e == 3 and unless_first(b):
                                add(b - 1)
                tokens(0, 0)
                tokens(0, 1)
                body(0)
                with v.Fori(1, NB - 1) as b:
                    body(b)
                body(NB - 1, last=True)
                gather(NB - 1, NE - 1)
                finish(NB - 1)
                add(NB - 1)
                v.wait_ge(e_x, NB)

            @block.gpsimd
            def _(pool):
                def split_tokens(b, e):
                    n = b * NE + e
                    pool.wait_ge(e_zf, n + 1)
                    if not (isinstance(n, int) and n < 2):
                        pool.wait_ge(e_h_ps, (n - 1) * HB)
                    pool.tensor_tensor(ZH[:, e % 2, :], ZF[:, :], zero[:, :].to_broadcast([128, T]),
                                       ALU.add).then_inc(e_zh, 1)
                    pool.wait_ge(e_zh, n + 1)
                    pool.tensor_tensor(ZL[:, e % 2, :], ZF[:, :], ZH[:, e % 2, :].bitcast(F32),
                                       ALU.subtract).then_inc(e_zl, 1)

                def body(b, last=False):
                    for e in range(NE):
                        if e + 2 < NE:
                            split_tokens(b, e + 2)
                        elif not last:
                            split_tokens(b + 1, e + 2 - NE)
                        if e == 1 and unless_first(b):
                            rstd_of(pool, POST, eps5, e_stats, b * 2, e_rstd, (b - 1) * 2)
                split_tokens(0, 0)
                split_tokens(0, 1)
                body(0)
                with pool.Fori(1, NB - 1) as b:
                    body(b)
                body(NB - 1, last=True)
                rstd_of(pool, POST, eps5, e_stats, NB * 2, e_rstd, (NB - 1) * 2)

            @block.tensor
            def _(pe):
                def three(out, weights, tokens, start, stop):
                    (wh, wl), (th, tl) = weights, tokens
                    pe.matmul(out, wh, th, start=start, stop=False)
                    pe.matmul(out, wh, tl, start=False, stop=False)
                    return pe.matmul(out, wl, th, start=False, stop=stop)

                def hidden(b, e):
                    n = b * NE + e
                    pe.wait_ge(e_zl, n + 1)
                    for k in range(HB):
                        if unless_first(n):
                            pe.wait_ge(e_hh, (n - 1) * HB + k + 1)
                        c = slice(e * HID + k * 128, e * HID + (k + 1) * 128)
                        three(PB[k // 2][:, (k % 2) * 512:(k % 2 + 1) * 512], (W1H[:, c], W1L[:, c]),
                              (ZH[:, e % 2, :], ZL[:, e % 2, :]), True, True).then_inc(e_h_ps, 1)

                def output(b, e):
                    n = b * NE + e
                    if not (isinstance(n, int) and n < 2):
                        pe.wait_ge(e_yg, n - 1)
                    for k in range(HB):
                        pe.wait_ge(e_hl, n * HB + k + 1)
                        c = slice((e * HB + k) * D, (e * HB + k + 1) * D)
                        m = three(PV2[e % 2][:, :], (W2H[:, c], W2L[:, c]), (HH[:, e % 2, k, :], HL[:, e % 2, k, :]),
                                  k == 0, k == HB - 1)
                    m.then_inc(e_y_ps, 1)

                def back(b):
                    pe.wait_ge(e_yg, (b + 1) * NE)
                    pe.wait_ge(e_acc, (b + 1) * (NE - 1))
                    if unless_first(b):
                        pe.wait_ge(e_y, b)
                    for i in range(NT):
                        m = pe.transpose(PM[:, i * 128:(i + 1) * 128], AT[:, i * 128:(i + 1) * 128], ident)
                    m.then_inc(e_t_ps, 1)

                def body(b, last=False):
                    for e in range(NE):
                        if e + 1 < NE:
                            hidden(b, e + 1)
                        elif not last:
                            hidden(b + 1, 0)
                        output(b, e)
                        if e == 0 and unless_first(b):
                            back(b - 1)
                hidden(0, 0)
                body(0)
                with pe.Fori(1, NB - 1) as b:
                    body(b)
                body(NB - 1, last=True)
                back(NB - 1)

            @block.scalar
            def _(act):
                def body(b, last=False):
                    for e in range(NE):
                        n = b * NE + e
                        for k in range(HB):
                            act.wait_ge(e_h_ps, n * HB + k + 1)
                            if unless_first(n):
                                act.wait_ge(e_hl, (n - 1) * HB + k + 1)
                            nc.scalar.activation(H[:, k, :], PB[k // 2][:, (k % 2) * 512:(k % 2 + 1) * 512],
                                                 ACT.Gelu, bias=w("b1")[:, e * HB + k:e * HB + k + 1]).then_inc(e_h, 1)
                            if k == 0 and not (isinstance(n, int) and n < 2):
                                act.wait_ge(e_y_ps, n - 1)
                            nc.scalar.activation(HH[:, e % 2, k, :], PB[k // 2][:, (k % 2) * 512:(k % 2 + 1) * 512],
                                                 ACT.Gelu, bias=w("b1")[:, e * HB + k:e * HB + k + 1]).then_inc(e_hh, 1)
                body(0)
                with act.Fori(1, NB - 1) as b:
                    body(b)
                body(NB - 1, last=True)

            @block.sync
            def _(sp):
                def body(b):
                    for e in range(NE):
                        n = b * NE + e
                        if not (isinstance(n, int) and n < 2):
                            sp.wait_ge(e_yg, n - 1)
                        sp.dma_start(G[:, e % 2, :], gates_dram[e, bass.ds(b * T, T)].partition_broadcast(128)
                                     ).then_inc(e_g[e % 2], 16)
                per_batch(sp, body)

        with nc.Block() as block:
            @block.sync
            def _(sp):
                sp.wait_ge(e_x, NB)
                fill_operands(sp)
                sp.wait_ge(filled, 2 * FILLED)

            @block.vector
            def _(v):
                clear_values(v, 2)
                nc.vector.memset(W1[:, 2 * T:3 * T - 128], 0.0).then_inc(cleared, 1)
                nc.vector.tensor_copy(W1[:, 3 * T - 128:3 * T], mask_b[:, :]).then_inc(cleared, 1)
                v.wait_ge(cleared, 6)

        second = attention("a2", True, NG, "wq2", "wk2", "wv2", "wo2", None, HD ** -0.5, 1.0, (e_x, NB), True)

        XS = cols(0, [T + 2])
        XM = cols(1032, [2, 2, T])
        KA = cols(1032 + 4 * T, [2, T])
        SG = cols(1032 + 6 * T, [2, T])
        YO = cols(1032 + 8 * T, [2, NT, D])
        MU = cols(1032 + 10 * T, [2])
        PR = cols(1032 + 11 * T, [2, T])
        f_const, f_stats, f_rstd, f_ln, f_xs_ps, f_xs, f_mix, f_k_ps, f_r_ps, f_k, f_k2, f_out_ps, f_sig, f_gated = (
            sem(n) for n in ("f_const", "f_stats", "f_rstd", "f_ln", "f_xs_ps", "f_xs", "f_mix", "f_k_ps", "f_r_ps",
                             "f_k", "f_k2", "f_out_ps", "f_sig", "f_gated"))
        f_prev = sem("f_prev")
        f_stats2, f_rstd2, f_ln2, f_x = sem("f_stats2"), sem("f_rstd2"), sem("f_ln2"), sem("f_x")
        with nc.Block() as block:
            @block.vector
            def _(v):
                v.wait_ge(*second)
                nc.vector.memset(XS[:, 0:2], 0.0).then_inc(f_const, 1)
                for k, name in enumerate(("mu_r", "mu_k")):
                    nc.vector.tensor_scalar(MU[:, k:k + 1], w(name), -1.0, 1.0, ALU.mult,
                                            ALU.add).then_inc(f_const, 1)
                v.wait_ge(f_const, 3)

                def step(s, si):
                    if has_work(si, 4):
                        b = s - 4
                        normalise(v, POST, lambda i: YO[:, si % 2, i, :], lambda i: YO[:, si % 2, i, :],
                                  f_rstd2, (b + 1) * 2, f_ln2)
                    if has_work(si, 3):
                        b = s - 3
                        v.wait_ge(f_sig, b + 1)
                        v.wait_ge(f_out_ps, b + 1)
                        if not (isinstance(s, int) and s < 5):
                            v.wait_ge(f_x, b - 1)
                        nc.vector.tensor_tensor(YO[:, (si + 1) % 2, :, :].rearrange("p i d -> p (i d)"),
                                                PA[1][:, :], SG[:, (si + 1) % 2, :], ALU.mult).then_inc(f_gated, 1)
                        v.wait_ge(f_gated, b + 1)
                        if not (isinstance(s, int) and s < 4):
                            v.wait_ge(f_ln2, b)
                        stats_of(v, POST, lambda i: YO[:, (si + 1) % 2, i, :], f_stats2, b * 2)
                    if has_work(si, 1):
                        b = s - 1
                        if not (isinstance(s, int) and s < 2):
                            v.wait_ge(f_xs_ps, b)
                        normalise(v, PRE, lambda i: xcols(b, i), lambda i: XN[:, i, :], f_rstd, (b + 1) * 2, f_ln)
                    if has_work(si, 2):
                        b = s - 2
                        v.wait_ge(f_k, b + 1)
                        nc.vector.tensor_tensor(KA[:, si % 2, :], KA[:, si % 2, :], KA[:, si % 2, :],
                                                ALU.mult).then_inc(f_k2, 1)
                    if has_work(si, 1):
                        b = s - 1
                        if not (isinstance(s, int) and s < 3):
                            v.wait_ge(f_r_ps, b - 1)
                        for k, name in enumerate(("mu_r", "mu_k")):
                            v.wait_ge(f_prev, b * 2 + k + 1)
                            nc.vector.scalar_tensor_tensor(
                                out=XM[:, (si + 1) % 2, k, :], in0=XS[:, 2:T + 2], scalar=w(name), in1=PR[:, k, :],
                                op0=ALU.mult, op1=ALU.add).then_inc(f_mix, 1)
                    if has_work(si, 0):
                        if not (isinstance(s, int) and s < 1):
                            v.wait_ge(f_ln, s)
                        stats_of(v, PRE, lambda i: xcols(s, i), f_stats, s * 2)
                run_pipeline(v, 4, step)

            @block.gpsimd
            def _(pool):
                pool.wait_ge(f_const, 3)

                def step(s, si):
                    if has_work(si, 4):
                        b = s - 4
                        pool.wait_ge(f_ln2, b + 1)
                        xb = X[:, bass.ds(b * T, T)]
                        pool.tensor_tensor(xb, xb, YO[:, si % 2, :, :].rearrange("p i d -> p (i d)"),
                                           ALU.add).then_inc(f_x, 1)
                    if has_work(si, 3):
                        b = s - 3
                        rstd_of(pool, POST, eps5, f_stats2, (b + 1) * 2, f_rstd2, b * 2)
                    if has_work(si, 0):
                        rstd_of(pool, PRE, eps5, f_stats, (s + 1) * 2, f_rstd, s * 2)
                run_pipeline(pool, 4, step)

            @block.tensor
            def _(pe):
                def step(s, si):
                    if has_work(si, 2):
                        b = s - 2
                        pe.wait_ge(f_mix, (b + 1) * 2)
                        if not (isinstance(s, int) and s < 3):
                            pe.wait_ge(f_k, b)
                        pe.matmul(PA[0][:, :], w("wkk"), XM[:, si % 2, 1, :], start=True, stop=True).then_inc(f_k_ps, 1)
                        if not (isinstance(s, int) and s < 3):
                            pe.wait_ge(f_sig, b)
                        for i in range(NT):
                            m = pe.matmul(PB[0][:, i * 128:(i + 1) * 128], XM[:, si % 2, 0, i * 128:(i + 1) * 128],
                                          w("wr"), start=True, stop=True)
                        m.then_inc(f_r_ps, 1)
                    if has_work(si, 1):
                        b = s - 1
                        pe.wait_ge(f_ln, b + 1)
                        if not (isinstance(s, int) and s < 2):
                            pe.wait_ge(f_xs, b)
                        for i in range(NT):
                            m = pe.transpose(PM[:, i * 128:(i + 1) * 128], XN[:, i, :], ident)
                        m.then_inc(f_xs_ps, 1)
                    if has_work(si, 2):
                        b = s - 2
                        pe.wait_ge(f_k2, b + 1)
                        if not (isinstance(s, int) and s < 3):
                            pe.wait_ge(f_gated, b)
                        for i in range(NT):
                            m = pe.matmul(PA[1][:, i * 128:(i + 1) * 128], KA[:, si % 2, i * 128:(i + 1) * 128],
                                          w("wvv"), start=True, stop=True)
                        m.then_inc(f_out_ps, 1)
                run_pipeline(pe, 4, step)

            @block.scalar
            def _(act):
                act.wait_ge(f_const, 3)

                def step(s, si):
                    if has_work(si, 2):
                        b = s - 2
                        act.wait_ge(f_k_ps, b + 1)
                        if not (isinstance(s, int) and s < 4):
                            act.wait_ge(f_out_ps, b - 1)
                        nc.scalar.activation(KA[:, si % 2, :], PA[0][:, :], ACT.Relu).then_inc(f_k, 1)
                        act.wait_ge(f_r_ps, b + 1)
                        if not (isinstance(s, int) and s < 4):
                            act.wait_ge(f_gated, b - 1)
                        nc.scalar.activation(SG[:, si % 2, :], PB[0][:, 0:T], ACT.Sigmoid).then_inc(f_sig, 1)
                    if has_work(si, 1):
                        b = s - 1
                        act.wait_ge(f_xs_ps, b + 1)
                        if not (isinstance(s, int) and s < 2):
                            act.wait_ge(f_mix, b * 2)
                        nc.scalar.activation(XS[:, 2:T + 2], PM[:, :], ACT.Copy).then_inc(f_xs, 1)
                        act.wait_ge(f_xs, b + 1)
                        for k in range(2):
                            nc.scalar.activation(PR[:, k, :], XS[:, 1:T + 1], ACT.Identity,
                                                 scale=MU[:, k:k + 1]).then_inc(f_prev, 1)
                run_pipeline(act, 4, step)

            @block.sync
            def _(sp):
                with sp.Fori(0, NB) as b:
                    sp.wait_ge(f_x, b + 1)
                    sp.dma_start(out[bass.ds(b, 1)].rearrange("b (i p) d -> p (b i) d", p=128),
                                 X[:, bass.ds(b * T, T)].rearrange("p (c d) -> p c d", d=D)).then_inc(all_out, 16)
                sp.wait_ge(all_out, 16 * NB)


def kernel(**inputs):
    import numpy as _np
    import concourse.bacc as _bacc
    from concourse import mybir as _mybir
    from concourse.bass_utils import run_bass_kernel_spmd as _run

    a = {k: _np.asarray(v) for k, v in inputs.items()}
    columns = {
        "wq1": a["L0_attn_Wq"].T, "wk1": a["L0_attn_Wk"].T, "wv1": a["L0_attn_Wv"].T, "wu1": a["L0_attn_Wu"].T,
        "wq2": a["L1_attn_W_q"].T, "wk2": a["L1_attn_W_k"].T, "wv2": a["L1_attn_W_v"].T, "wo2": a["L1_attn_W_o"].T,
        "wr": a["L1_ffn_W_r"].T, "wkk": a["L1_ffn_W_k"].T, "wvv": a["L1_ffn_W_v"].T,
        "ident": _np.eye(128, dtype=_np.float32), "router_w": a["L0_ffn_router_w"].T,
        "router_s": a["L0_ffn_router_ln_scale"][:, None], "router_t": a["L0_ffn_router_ln_bias"][:, None],
        "b2": a["L0_ffn_b2"].T, "expert_s": a["L0_ffn_expert_ln_scale"].T, "expert_t": a["L0_ffn_expert_ln_bias"].T,
        "b1": a["L0_ffn_b1"].reshape(NE * HB, 128).T,
        "mu_r": a["L1_ffn_mu_r"][:, None], "mu_k": a["L1_ffn_mu_k"][:, None],
    }
    rows = {"bu": a["L0_attn_bu"], "router_b": a["L0_ffn_router_b"],
            "earlier": _np.tril(_np.ones((NE, NE), dtype=_np.float32), k=-1).reshape(-1)}
    half = D // 2
    angle = (_np.arange(T, dtype=_np.float32)[:, None]
             * (1.0 / 10000.0 ** (_np.arange(half, dtype=_np.float32) / half)).astype(_np.float32)[None, :])
    arrays = {
        "x_dram": _np.ascontiguousarray(a["L0_attn_x"]),
        "weights_dram": _np.ascontiguousarray(_np.concatenate([columns[n] for n, _ in WCOLS], axis=1)),
        "rows_dram": _np.ascontiguousarray(_np.concatenate([rows[n] for n, _ in RCOLS])),
        "w1_dram": _np.ascontiguousarray(a["L0_ffn_w1"].transpose(2, 0, 1).reshape(D, NE * HID)),
        "w2_dram": _np.ascontiguousarray(a["L0_ffn_w2"].reshape(NE, D, HB, 128).transpose(3, 0, 2, 1)
                                         .reshape(128, NE * HB * D)),
        "rope_dram": _np.concatenate([_np.cos(angle), _np.sin(angle)], axis=1).astype(_np.float32),
        "mask_dram": _np.triu(_np.full((128, 128), -1e9, dtype=_np.float32), k=1),
        "fill_dram": _np.concatenate([_np.zeros((MAX_ROW - TERM_ROWS, NH * T), _np.uint32),
                                      _np.full((MAX_PARTS, NH * T), 0x3F803F80, _np.uint32)]).view(_np.float32),
    }
    nc = _bacc.Bacc("TRN2", target_bir_lowering=False, num_devices=1)
    args = [nc.dram_tensor(n, v.shape, _mybir.dt.from_np(v.dtype), kind="ExternalInput").ap()
            for n, v in arrays.items()]
    args.append(nc.dram_tensor("out_dram", (NB, T, D), _mybir.dt.float32, kind="ExternalOutput").ap())
    build(nc, *args)
    r = _run(nc, [arrays], core_ids=[0])
    return r.results[0]["out_dram"]
```

```python
from contextlib import ExitStack

import numpy as np

import concourse.bass as bass
from concourse import mybir

F32 = mybir.dt.float32
BF16 = mybir.dt.bfloat16
F32R = mybir.dt.float32r
ALU = mybir.AluOpType
ACT = mybir.ActivationFunctionType
AX = mybir.AxisListType

NB = 8
T = 512
D = 128
NT = T // 128
NH = 16
HD = D // NH
HG = 4
NG = NH // HG
UNITS = NG * NT
NE = 8
HID = 512
HB = HID // 128
SPLITS = 3
TERM_ROWS = SPLITS * SPLITS * HD
MAX_ROW = 96
MAX_PARTS = 2
ROWS = MAX_ROW + MAX_PARTS
TABLES = 32
CONSTS = 6

WCOLS = [("wq1", D), ("wk1", D), ("wv1", D), ("wu1", D), ("wq2", D), ("wk2", NG * HD), ("wv2", NG * HD),
         ("wo2", D), ("wr", D), ("wkk", D), ("wvv", D), ("ident", D), ("mask", 128), ("router_w", NE),
         ("router_s", 1), ("router_t", 1), ("expert_s", NE), ("expert_t", NE), ("b1", NE * HB), ("b2", NE),
         ("mu_r", 1), ("mu_k", 1)]
WAT, WN = {}, 0
for _name, _n in WCOLS:
    WAT[_name] = (WN, WN + _n)
    WN += _n
RCOLS = [("bu", D), ("router_b", NE), ("order", NE)]
RAT, RN = {}, 0
for _name, _n in RCOLS:
    RAT[_name] = (RN, RN + _n)
    RN += _n

ROUTE_AT = {(NB - 1, 2): 0, (NB - 1, 6): 1, (NB - 1, 9): 2, (NB - 1, 11): 3, (NB - 1, 13): 4, (NB - 1, 15): 5,
            (NB, 5): 6}
ROUTE_BESIDE = {1: 8, 2: 9, 3: 10, 4: 11}
GATE_LINKS = 20
MIX_AT = {(NB - 1, 2): 0, (NB - 1, 7): 1, (NB - 1, 11): 2, (NB - 1, 15): 3, (NB, 4): 4, (NB, 8): 5}
MIX_STEPS = NB + 4
PIECES = 4
PIECE = NE * HID // PIECES
W1_HIGH_AT = {(NB - 1, 2 + 3 * k): k for k in range(PIECES)}
W1_LOW_AT = {(NB - 1, 4 + 3 * k): k for k in range(PIECES)}
TOKENS_AT = {(NB, 5): 0, (NB, 12): 1}
W2_HIGH_AT = {(NB, 8 + k): k for k in range(PIECES)}

BESIDE = {0: ((-2, 0), (-2, 1)), 1: ((-2, 2), (-2, 3)), 2: ((-2, 4), (-2, 5)), 3: ((-2, 6), (-2, 7), (-2, 8)),
          4: ((-2, 9), (-2, 10)), 5: ((-2, 11),), 6: ((-1, 0), (-1, 1)), 7: ((-1, 2), (-1, 3))}
FIRST_UNIT = 4

MISC = {1: ("m1", "attend"), 2: ("oT3", "finish"), 3: ("xoT", "finish"), 4: ("xT", "project"), 5: ("m2", "attend"),
        6: ("out", "finish"), 7: ("oT0", "attend"), 8: ("q", "project"), 9: ("m3", "attend"), 10: ("k", "project"),
        11: ("oT1", "attend"), 12: ("v", "prepare"), 13: ("m0", "prepare"), 14: ("oT2", "attend")}
LEAD = 8
UNIT_OF = {item: u for u, (item, _) in MISC.items()}
FIRST_STEP, LAST_STEP = -2, NB
FULL = (1, NB - 3)


def stages(b):
    s = set()
    if b + 2 < NB:
        s.add("project")
    if 0 <= b + 1 < NB:
        s.add("prepare")
    if 0 <= b < NB:
        s.add("attend")
    if 0 <= b - 1:
        s.add("finish")
    return s


def units_before(b, u, n):
    return (b, u - n) if u >= n else (b - 1, u - n + UNITS)


def score_unit(b, b_int, u):
    ahead = u >= UNITS - LEAD
    if not 0 <= b_int + ahead < NB:
        return None
    return b + ahead, b_int + ahead, (u + LEAD) % UNITS


def misc_count(b, b_int, unit):
    st = stages(b_int)
    n = sum(1 for u in MISC if u <= unit and MISC[u][1] in st)
    n += sum(1 for s in range(FIRST_STEP, b_int) for u in MISC if MISC[u][1] in stages(s))
    return (b - b_int) * len(MISC) + n if not isinstance(b, int) else n


def run_steps(eng, first, unit, after=None, first_unit=0):
    def step(b, bi, from_unit=0):
        for u in range(from_unit, UNITS):
            unit(b, bi, u)
    for b in range(first, FULL[0]):
        step(b, b, first_unit if b == first else 0)
    with eng.Fori(FULL[0], FULL[1], 2) as i:
        step(i, FULL[0])
        step(i + 1, FULL[0] + 1)
    for b in range(FULL[1], LAST_STEP + 1):
        for u in range(UNITS):
            unit(b, b, u)
            if after:
                after(b, u)


def has_work(s_int, k):
    return 0 <= s_int - k < NB


def build(nc, x_in, weights, rows, w1, w2, rope, fill, out):
    with ExitStack() as ctx:
        def sb(name, shape, dt=F32):
            return ctx.enter_context(nc.sbuf_tensor(name, shape, dt))

        def psum(name, shape):
            return ctx.enter_context(nc.psum_tensor(name, shape, F32))

        def sem(name):
            return ctx.enter_context(nc.semaphore(name))

        X = sb("X", [128, NB * T])
        w_at = nc.sbuf_base
        W1 = sb("W1", [128, NE * HID])
        W2 = sb("W2", [128, NE * HB * D])
        ops_at = nc.sbuf_base
        ops = sb("ops", [128, 2 * 2 * NH * T], BF16)
        vo_at = nc.sbuf_base
        VO = sb("VO", [128, 2, NT, NH, 32])
        arena_at = nc.sbuf_base
        arena = sb("arena", [128, 4 * HG * T])
        W = sb("W", [128, WN])
        R = sb("R", [128, RN])
        ident_b = sb("ident_b", [128, 128], BF16)
        mask_b = sb("mask_b", [128, 128], BF16)
        rope_t = sb("rope_t", [128, NT, 2, D // 2])
        stat = sb("stat", [128, 3, NT, 8])
        mv = sb("mv", [128, 3, NT, 2])
        ve = sb("ve", [128, 3, NT])
        rstd = sb("rstd", [128, 3, NT])
        eps5 = sb("eps5", [128, 1])
        eps6 = sb("eps6", [128, 1])
        minus_half = sb("minus_half", [128, 1])
        carry = sb("carry", [128, 2])
        MU = sb("MU", [128, 2])
        QO = ops[:, 0:2 * NH * T].rearrange("p (c h t) -> p c h t", c=2, h=NH)
        KO = ops[:, 2 * NH * T:].rearrange("p (c h t) -> p c h t", c=2, h=NH)
        P = arena[:, :].rearrange("p (r h t) -> p r h t", r=4, h=HG)
        XN = sb("XN", [128, NT, D])
        XR = sb("XR", [128, NT, D])
        RT = sb("RT", [128, 2, NT, D // 2])
        XNT = sb("XNT", [128, 2, T])
        QS = sb("QS", [128, 2, T])
        RES = sb("RES", [128, T])
        zero = sb("zero", [128, 1])
        SPL = sb("SPL", [128, 2, SPLITS, T], BF16)
        MX = sb("MX", [128, 2, NG, NT, HG])
        MR = sb("MR", [128, NT, HG])
        MS = sb("MS", [128, 2, NT, MAX_PARTS, HG], BF16)
        MT = sb("MT", [MAX_PARTS * HG, 2, T], BF16)
        OT = sb("OT", [128, T])
        RL = sb("RL", [128, NT, HG])
        XO = sb("XO", [128, NT, D])
        XOT = sb("XOT", [128, T])
        Y = sb("Y", [128, NT, D])

        PA = [psum("PA0", [128, 512]), psum("PA1", [128, 512])]
        PB = [psum("PB0", [128, 1024]), psum("PB1", [128, 1024])]
        PV = psum("PV", [128, 512])
        PM = psum("PM", [128, 512])
        PMb = PM[:, :].bitcast(BF16)

        scratch = {k: nc.dram_tensor(f"scratch_{k}", (2, SPLITS * HD, NH * T), BF16).ap() for k in ("q", "k")}

        def w(name):
            return W[:, WAT[name][0]:WAT[name][1]]

        def row(name):
            return R[:, RAT[name][0]:RAT[name][1]]

        ident = w("ident")
        loaded_x0, loaded_x, loaded_w, loaded_tables, loaded_mw = (
            sem(n) for n in ("loaded_x0", "loaded_x", "loaded_w", "loaded_tables", "loaded_mw"))
        consts = sem("consts")
        cleared, filled, masks = sem("cleared"), sem("filled"), sem("masks")
        all_out = sem("all_out")

        def xcols(b, i):
            return X[:, bass.ds(b * T + i * D, D)]

        PRE, POST, AGAIN = 0, 1, 2

        def stats_tile(slot, src, chain, i):
            ins = nc.vector.bn_stats(stat[:, slot, i, 0:6], src(i))
            if i == NT - 1:
                ins.then_inc(chain, 1)

        def aggregate(v, slot, chain, base):
            v.wait_ge(chain, base + 1)
            nc.vector.memset(stat[:, slot, 0, 6:7], 0.0)
            for i in range(NT):
                ins = nc.vector.bn_aggr(mv[:, slot, i, :], stat[:, slot, i, 0:6])
            ins.then_inc(chain, 1)

        def stats_of(v, slot, src, chain, base):
            for i in range(NT):
                stats_tile(slot, src, chain, i)
            aggregate(v, slot, chain, base)

        def rstd_of(pool, slot, eps, stats, ready, chain, base):
            pool.wait_ge(stats, ready)
            pool.tensor_tensor(ve[:, slot, :], mv[:, slot, :, 1], eps[:, :].to_broadcast([128, NT]),
                               ALU.add).then_inc(chain, 1)
            pool.wait_ge(chain, base + 1)
            pool.tensor_tensor(rstd[:, slot, :], ve[:, slot, :], minus_half[:, :].to_broadcast([128, NT]),
                               ALU.pow).then_inc(chain, 1)

        def normalise_tile(slot, src, dst, done, i):
            ins = nc.vector.tensor_scalar(dst(i), src(i), mv[:, slot, i, 0:1], rstd[:, slot, i:i + 1],
                                          ALU.subtract, ALU.mult)
            if i == NT - 1:
                ins.then_inc(done, 1)

        def normalise(v, slot, src, dst, rstd_chain, ready, done):
            v.wait_ge(rstd_chain, ready)
            for i in range(NT):
                normalise_tile(slot, src, dst, done, i)

        VO_FLAT = VO[:, :, :, :, :].rearrange("p a b c d -> p (a b c d)")

        def clear_values(v, base):
            nc.vector.memset(VO_FLAT, 0.0).then_inc(cleared, 1)
            v.wait_ge(cleared, base + 1)
            nc.vector.memset(VO[:, :, :, :, HD:HD + 1], 1.0).then_inc(cleared, 1)
            v.wait_ge(cleared, base + 2)

        def fill_operands(sp):
            for k, o in enumerate((QO, KO)):
                sp.dma_start(o[TERM_ROWS:MAX_ROW].rearrange("p c h t -> p (c h t)").bitcast(F32),
                             fill[0:MAX_ROW - TERM_ROWS, :]).then_inc(filled, 16)
            sp.dma_start(KO[MAX_ROW:MAX_ROW + MAX_PARTS].rearrange("p c h t -> p (c h t)").bitcast(F32),
                         fill[MAX_ROW - TERM_ROWS:, :]).then_inc(filled, 16)
        FILLED, CLEARED = 48, 2

        def load_inputs(sp):
            sp.dma_start(X[:, 0:T].rearrange("p (i d) -> p i d", d=D),
                         x_in[0].rearrange("(i p) d -> p i d", p=128)).then_inc(loaded_x0, 16)
            sp.dma_start(W[:, :], weights).then_inc(loaded_w, 16)
            sp.dma_start(X[:, T:].rearrange("p (c d) -> p c d", d=D),
                         x_in[1:NB].rearrange("b (i p) d -> p (b i) d", p=128)).then_inc(loaded_x, 16)
            sp.dma_start(R[:, :], rows.partition_broadcast(128)).then_inc(loaded_tables, 16)
            sp.dma_start(rope_t[:, :, :, :].rearrange("p i c f -> p i (c f)"),
                         rope.rearrange("(i p) f -> p i f", p=128)).then_inc(loaded_tables, 16)
            fill_operands(sp)

        def make_constants(pool):
            for t, value in ((zero, 0.0), (eps5, 1e-5), (eps6, 1e-6), (minus_half, -0.5)):
                pool.memset(t[:, :], value).then_inc(consts, 1)
            pool.wait_ge(loaded_w, 16)
            pool.tensor_copy(ident_b[:, :], ident).then_inc(consts, 1)
            pool.tensor_copy(mask_b[:, :], w("mask")).then_inc(consts, 1)
            pool.wait_ge(consts, CONSTS)

        def attention(tag, causal, kv_heads, wq, wk, wv, wo, bias, q_scale, k_scale, roped, fills, clears):
            S = {n: sem(f"{tag}_{n}") for n in (
                "pre_stats", "pre_rstd", "pre_ln",
                "rope_chain", "xr_ready",
                "misc_full", "misc_free",
                "split", "q_scratch", "k_scratch",
                "a_full", "a_free",
                "m_chain", "m_split",
                "b_full", "p_ready", "pv_done",
                "ot_ready", "rl_ready",
                "post_stats", "post_rstd", "post_ln",
                "x_done")}
            qk_loaded = [sem(f"{tag}_qk_loaded{g}") for g in range(NG)]
            m_loaded = [sem(f"{tag}_m_loaded{g}") for g in range(NG)]
            MASKED = W1[:, 0:2 * T].rearrange("p (c t) -> p c t", c=2)
            mask_w = W1[:, 2 * T:3 * T]
            share = NH // kv_heads
            kg = HG // share
            KROWS = kv_heads * HD
            QK_DMAS = 8

            def keys(i):
                return (i + 1) * 128 if causal else T

            def q0(t):
                return t * 128 if causal else 0

            def misc_evict(eng, b, bi, u):
                eng.wait_ge(S["misc_full"], misc_count(b, bi, u))

            def split(eng, b, bi, k):
                n = KROWS if k else D
                src = QS[0:n, k, :]
                eng.wait_ge(S["misc_free"], misc_count(b, bi, UNIT_OF["k" if k else "q"]))
                if not (isinstance(b, int) and b == FIRST_STEP):
                    eng.wait_ge(S["k_scratch" if k else "q_scratch"], (b + 2) * 16 * SPLITS)
                base = (b + 2) * 8 + k * 4
                cnt = [0]

                def link(ins):
                    cnt[0] += 1
                    ins.then_inc(S["split"], 1)
                    eng.wait_ge(S["split"], base + cnt[0])
                link(eng.tensor_tensor(SPL[0:n, k, 0, :], src, zero[0:n, :].to_broadcast([n, T]), ALU.add))
                link(eng.tensor_tensor(RES[0:n, :], src, SPL[0:n, k, 0, :], ALU.subtract))
                link(eng.tensor_tensor(SPL[0:n, k, 1, :], RES[0:n, :], zero[0:n, :].to_broadcast([n, T]), ALU.add))
                link(eng.tensor_tensor(SPL[0:n, k, 2, :], RES[0:n, :], SPL[0:n, k, 1, :], ALU.subtract))

            def tensor(pe):
                def misc(b, bi, u):
                    item = MISC[u][0]
                    n = misc_count(b, bi, u)
                    if not (isinstance(n, int) and n == 1):
                        pe.wait_ge(S["misc_free"], n - 1)
                    if item == "xT":
                        pe.wait_ge(S["xr_ready"] if roped else S["pre_ln"], b + 3)
                        for i in range(NT):
                            m = pe.transpose(PM[:, i * 128:(i + 1) * 128], (XR if roped else XN)[:, i, :], ident)
                    elif item in ("q", "k"):
                        wt, n_out = (wq, D) if item == "q" else (wk, KROWS)
                        m = pe.matmul(PM[0:n_out, :], w(wt), XNT[:, bi % 2, :], start=True, stop=True)
                    elif item == "v":
                        for i in range(NT):
                            m = pe.matmul(PM[:, i * 128:i * 128 + KROWS], XNT[:, (bi + 1) % 2, i * 128:(i + 1) * 128],
                                          w(wv), start=True, stop=True)
                    elif item[0] == "m":
                        g = int(item[1])
                        mb = b + 1 if item == "m0" else b
                        pe.wait_ge(S["m_split"], mb * NG + g + 1)
                        for i in range(NT):
                            m = pe.transpose(PMb[0:MAX_PARTS * HG, i * 128:(i + 1) * 128],
                                             MS[:, g % 2, i, :, :].rearrange("p c h -> p (c h)"), ident_b[:, :])
                    elif item[0:2] == "oT":
                        g = int(item[2])
                        ob = b - 1 if g == NG - 1 else b
                        pe.wait_ge(S["ot_ready"], ob * NG + g + 1)
                        for i in range(NT):
                            m = pe.transpose(PM[:, i * 128:(i + 1) * 128], OT[:, i * 128:(i + 1) * 128], ident)
                    elif item == "xoT":
                        for i in range(NT):
                            m = pe.transpose(PM[:, i * 128:(i + 1) * 128], XO[:, i, :], ident)
                    else:
                        for i in range(NT):
                            m = pe.matmul(PM[:, i * 128:(i + 1) * 128], XOT[:, i * 128:(i + 1) * 128], w(wo),
                                          start=True, stop=True)
                    m.then_inc(S["misc_full"], 1)

                def values(b, bi, u):
                    g, t = divmod(u, NT)
                    pe.wait_ge(S["p_ready"], (b * UNITS + u + 1) * 2)
                    if t == 0 and not (isinstance(b, int) and b == 0 and g == 0):
                        pe.wait_ge(S["ot_ready"], b * NG + g)
                    for j in range(HG):
                        kv = (g * HG + j) // share
                        m = pe.matmul(PV[32 * j:32 * j + 32, q0(t):T], VO[:, bi % 2, t, kv, :],
                                      P[:, u % 4, j, q0(t):T], start=(t == 0), stop=(t == NT - 1))
                    m.then_inc(S["pv_done"], 1)

                def score_t(b, bi, u, half):
                    g, t = divmod(u, NT)
                    n = b * UNITS * 2 + u * 2 + half
                    if half == 0 and t == 0:
                        pe.wait_ge(m_loaded[g], (b + 1) * 16 * MAX_PARTS)
                    if not (isinstance(b, int) and b == 0 and u == 0):
                        pe.wait_ge(S["p_ready"], n - 1)
                    for j in range(2):
                        h = g * HG + half * 2 + j
                        kv = h // share
                        m = pe.matmul(PB[half][:, j * 512 + q0(t):j * 512 + T],
                                      KO[0:ROWS, bi % 2, kv, t * 128:(t + 1) * 128], QO[0:ROWS, bi % 2, h, q0(t):T],
                                      start=True, stop=not causal)
                        if causal:
                            at = j * 512 + q0(t)
                            m = pe.matmul(PB[half][:, at:at + 128], mask_b[:, :], ident_b[:, :],
                                          start=False, stop=True)
                    m.then_inc(S["b_full"], 1)

                def score(b, bi, u, j):
                    g, t = divmod(u, NT)
                    h, i = g * HG + j, NT - 1 - t
                    n = b * UNITS * NT + u * NT + j
                    if isinstance(b, int) and b == 0 and u == 0 and j == 0:
                        pe.wait_ge(filled, fills)
                    if j == 0 and t == 0:
                        pe.wait_ge(qk_loaded[g], (b + 1) * 16 * QK_DMAS)
                    if not (isinstance(b, int) and b == 0 and u == 0 and j < 2):
                        pe.wait_ge(S["a_free"], n - 1)
                    m = pe.matmul(PA[j % 2][:, 0:keys(i)], QO[0:MAX_ROW, bi % 2, h, i * 128:(i + 1) * 128],
                                  KO[0:MAX_ROW, bi % 2, h // share, 0:keys(i)], start=True, stop=True)
                    m.then_inc(S["a_full"], 1)

                def unit(b, bi, u):
                    st = stages(bi)
                    ahead = score_unit(b, bi, u)
                    if ahead:
                        score(*ahead, 0)
                    if "attend" in st:
                        score_t(b, bi, u, 0)
                    if ahead:
                        score(*ahead, 1)
                    if "attend" in st and u > 0:
                        values(b, bi, u - 1)
                    if "finish" in st and u == 0:
                        values(b - 1, bi - 1, UNITS - 1)
                    if ahead:
                        score(*ahead, 2)
                    if "attend" in st:
                        score_t(b, bi, u, 1)
                    if ahead:
                        score(*ahead, 3)
                    if u in MISC and MISC[u][1] in st:
                        misc(b, bi, u)
                return unit

            def scalar(act):
                def evict(b, bi, u):
                    item, stage = MISC[u]
                    if stage not in stages(bi) or item not in ("xT", "q", "k", "v", "xoT"):
                        return
                    misc_evict(act, b, bi, u)
                    if item == "xT":
                        ins = nc.scalar.activation(XNT[:, bi % 2, :], PM[:, :], ACT.Copy)
                    elif item in ("q", "k"):
                        k = int(item == "k")
                        n_out = KROWS if k else D
                        if not (isinstance(b, int) and b == FIRST_STEP):
                            act.wait_ge(S["split"], (b + 1) * 8 + 4 * (k + 1))
                        ins = nc.scalar.activation(QS[0:n_out, k, :], PM[0:n_out, :], ACT.Copy,
                                                   scale=k_scale if k else q_scale)
                    elif item == "v":
                        if isinstance(b, int) and b == -1:
                            act.wait_ge(cleared, clears)
                        ins = nc.scalar.activation(
                            VO[:, (bi + 1) % 2, :, 0:kv_heads, 0:HD],
                            PM[:, :].rearrange("p (i h d) -> p i h d", i=NT, d=HD)[:, :, 0:kv_heads, :], ACT.Copy)
                    else:
                        ins = nc.scalar.activation(XOT[:, :], PM[:, :], ACT.Copy)
                    ins.then_inc(S["misc_free"], 1)

                def drain_group(b, bi, g, before_it):
                    act.wait_ge(S["pv_done"], b * UNITS + (g + 1) * NT)
                    if before_it is not None:
                        act.wait_ge(S["misc_full"], before_it)
                    nc.scalar.activation(OT[:, :], PV[:, :], ACT.Copy).then_inc(S["ot_ready"], 1)

                def unit(b, bi, u):
                    st = stages(bi)
                    g, t = divmod(u, NT)
                    for half in (0, 1):
                        if "attend" in st:
                            n = b * UNITS * 2 + u * 2 + half
                            act.wait_ge(S["b_full"], n + 1)
                            if half == 0 and not (isinstance(b, int) and b == 0 and u < 4):
                                act.wait_ge(S["pv_done"], b * UNITS + u - 3)
                            nc.scalar.activation(
                                P[:, u % 4, 2 * half:2 * half + 2, q0(t):T],
                                PB[half][:, :].rearrange("p (j s) -> p j s", j=2)[:, :, q0(t):T],
                                ACT.Exp).then_inc(S["p_ready"], 1)
                        if half == 0 and "attend" in st and t == 0 and g > 0:
                            first = isinstance(b, int) and b == 0 and g == 1
                            drain_group(b, bi, g - 1, None if first else
                                        misc_count(b, bi, UNIT_OF["oT3" if g == 1 else f"oT{g - 2}"]))
                        if half == 0 and "finish" in st and u == 0:
                            drain_group(b - 1, bi - 1, NG - 1, misc_count(b, bi, 0))
                    if u in MISC:
                        evict(b, bi, u)
                return unit

            def gpsimd(pool):
                def split_max(b, bi, g, read_before):
                    n = b * NG + g
                    pool.wait_ge(S["a_free"], (n + 1) * HG * NT)
                    if not (isinstance(b, int) and b == 0 and g == 0):
                        pool.wait_ge(S["m_split"], n)
                    if read_before is not None:
                        pool.wait_ge(S["misc_free"], read_before)
                    zeros_m = zero[:, :].unsqueeze(2).to_broadcast([128, NT, HG])
                    mx = MX[:, bi % 2, g, :, :]
                    pool.tensor_tensor(MS[:, g % 2, :, 0, :], zeros_m, mx, ALU.subtract).then_inc(S["m_chain"], 1)
                    pool.tensor_tensor(MR[:, :, :], zeros_m, mx, ALU.subtract).then_inc(S["m_chain"], 1)
                    pool.wait_ge(S["m_chain"], n * 2 + 2)
                    pool.tensor_tensor(MS[:, g % 2, :, 1, :], MR[:, :, :], MS[:, g % 2, :, 0, :],
                                       ALU.subtract).then_inc(S["m_split"], 1)

                def rotate(b, bi):
                    pool.wait_ge(S["pre_ln"], b + 3)
                    if not (isinstance(b, int) and b == FIRST_STEP):
                        pool.wait_ge(S["misc_free"], misc_count(b, bi, 0))
                    xe = XN[:, :, :].rearrange("p i (f e) -> p i f e", e=2)[:, :, :, 0]
                    xo = XN[:, :, :].rearrange("p i (f e) -> p i f e", e=2)[:, :, :, 1]
                    cos, sin = rope_t[:, :, 0, :], rope_t[:, :, 1, :]
                    H = D // 2
                    base = (b + 2) * 5

                    pool.tensor_tensor(RT[:, 0], xe, cos, ALU.mult).then_inc(S["rope_chain"], 1)
                    pool.tensor_tensor(RT[:, 1], xo, sin, ALU.mult).then_inc(S["rope_chain"], 1)
                    pool.wait_ge(S["rope_chain"], base + 2)
                    pool.tensor_tensor(XR[:, :, 0:H], RT[:, 0], RT[:, 1], ALU.subtract).then_inc(S["rope_chain"], 1)
                    pool.wait_ge(S["rope_chain"], base + 3)
                    pool.tensor_tensor(RT[:, 0], xe, sin, ALU.mult).then_inc(S["rope_chain"], 1)
                    pool.tensor_tensor(RT[:, 1], xo, cos, ALU.mult).then_inc(S["rope_chain"], 1)
                    pool.wait_ge(S["rope_chain"], base + 5)
                    pool.tensor_tensor(XR[:, :, H:D], RT[:, 0], RT[:, 1], ALU.add).then_inc(S["xr_ready"], 1)

                def unit(b, bi, u):
                    st = stages(bi)
                    if u == 0 and "attend" in st:
                        first = isinstance(b, int) and b == 0
                        split_max(b, bi, 1, None if first else misc_count(b, bi, 0))
                    if u == 1 and "project" in st:
                        rstd_of(pool, PRE, eps5, S["pre_stats"], (b + 3) * 2, S["pre_rstd"], (b + 2) * 2)
                    if u == 2 and "project" in st and roped:
                        rotate(b, bi)
                    if u == 4 and "attend" in st:
                        split_max(b, bi, 2, misc_count(b, bi, 0))
                    if u == 8 and "attend" in st:
                        split_max(b, bi, 3, misc_count(b, bi, UNIT_OF["m1"]))
                    if u == 8 and "finish" in st:
                        rstd_of(pool, POST, eps5, S["post_stats"], b * 2, S["post_rstd"], (b - 1) * 2)
                    if u in (9, 11) and "project" in st:
                        split(pool, b, bi, int(u == 11))
                    if u == 12 and "prepare" in st:
                        first = isinstance(b, int) and b == -1
                        split_max(b + 1, bi + 1, 0, None if first else misc_count(b, bi, UNIT_OF["m2"]))
                return unit

            def vector(v):
                def maximum(b, bi, u, j):
                    g, t = divmod(u, NT)
                    i = NT - 1 - t
                    v.wait_ge(S["a_full"], b * UNITS * NT + u * NT + j + 1)
                    mx = MX[:, bi % 2, g, i, j:j + 1]
                    if causal:
                        nc.vector.memset(carry[:, j % 2:j % 2 + 1], 0.0)
                        ins = nc.vector.tensor_tensor_reduce(
                            out=MASKED[:, j % 2, 0:keys(i)], in0=PA[j % 2][:, 0:keys(i)],
                            in1=mask_w[:, T - keys(i):T], scale=1.0, scalar=-3e38, op0=ALU.add, op1=ALU.max,
                            accum_out=mx)
                    else:
                        ins = nc.vector.tensor_reduce(mx, PA[j % 2][:, 0:keys(i)], AX.X, ALU.max)
                    ins.then_inc(S["a_free"], 1)

                def project(b, bi, u, i):
                    src = lambda i: xcols(b + 2, i)
                    if u == 0:
                        stats_tile(PRE, src, S["pre_stats"], i)
                    if u == 1 and i == 0:
                        aggregate(v, PRE, S["pre_stats"], (b + 2) * 2)
                    k = u * NT + i - 7
                    if 0 <= k < NT:
                        if k == 0:
                            if not (isinstance(b, int) and b == FIRST_STEP):
                                v.wait_ge(S["xr_ready"] if roped else S["misc_free"],
                                          b + 2 if roped else misc_count(b, bi, 0))
                            v.wait_ge(S["pre_rstd"], (b + 3) * 2)
                        normalise_tile(PRE, src, lambda i: XN[:, i, :], S["pre_ln"], k)

                def divide(b, bi, ob, g, part):
                    o = PM[:, :].rearrange("p (i h c) -> p i h c", i=NT, h=HG)
                    if part == 0:
                        nc.vector.reciprocal(RL[:, :, :], o[:, :, :, HD]).then_inc(S["rl_ready"], 1)
                    else:
                        v.wait_ge(S["rl_ready"], ob * NG + g + 1)
                        nc.vector.tensor_tensor(
                            XO[:, :, g * HG * HD:(g + 1) * HG * HD].rearrange("p i (h d) -> p i h d", d=HD),
                            o[:, :, :, 0:HD], RL[:, :, :].unsqueeze(3).to_broadcast([128, NT, HG, HD]),
                            ALU.mult).then_inc(S["misc_free"], 1)

                def read_item(b, bi, u, part):
                    item, stage = MISC[u]
                    if stage not in stages(bi):
                        return
                    if item[0:2] == "oT":
                        g = int(item[2])
                        if part == 0:
                            v.wait_ge(S["misc_full"], misc_count(b, bi, u))
                        divide(b, bi, b - 1 if g == NG - 1 else b, g, part)
                    elif item[0] == "m" and part == 0:
                        v.wait_ge(S["misc_full"], misc_count(b, bi, u))
                        g = int(item[1])
                        mb = b + 1 if item == "m0" else b
                        if not (isinstance(mb, int) and mb == 0 and g < 2):
                            v.wait_ge(m_loaded[(g + 2) % NG], (mb + 1 if g >= 2 else mb) * 16 * MAX_PARTS)
                        nc.vector.tensor_copy(MT[:, g % 2, :], PMb[0:MAX_PARTS * HG, 0:T]).then_inc(S["misc_free"], 1)
                    elif item == "out" and part == 0:
                        v.wait_ge(S["misc_full"], misc_count(b, bi, u))
                        pm = PM[:, :].rearrange("p (i d) -> p i d", i=NT)
                        if bias:
                            ins = nc.vector.tensor_tensor(
                                Y[:, :, :], pm, row(bias).unsqueeze(1).to_broadcast([128, NT, D]), ALU.add)
                        else:
                            ins = nc.vector.tensor_copy(Y[:, :, :], pm)
                        ins.then_inc(S["misc_free"], 1)

                def finish(b, bi, u, i):
                    y = lambda i: Y[:, i, :]
                    out_u = UNIT_OF["out"] + 1
                    k = (u - out_u) * NT + i
                    if 2 <= k < 2 + NT:
                        if k == 2:
                            v.wait_ge(S["misc_free"], misc_count(b, bi, UNIT_OF["out"]))
                        stats_tile(POST, y, S["post_stats"], k - 2)
                    if k == 3 + NT:
                        aggregate(v, POST, S["post_stats"], (b - 1) * 2)
                    if u == 10:
                        if i == 0:
                            v.wait_ge(S["post_rstd"], b * 2)
                        normalise_tile(POST, y, y, S["post_ln"], i)
                    if u == 11 and i == 0:
                        v.wait_ge(S["post_ln"], b)
                        xb = X[:, bass.ds((b - 1) * T, T)]
                        nc.vector.tensor_tensor(xb, xb, Y[:, :, :].rearrange("p i d -> p (i d)"),
                                                ALU.add).then_inc(S["x_done"], 1)

                def unit(b, bi, u):
                    st = stages(bi)
                    ahead = score_unit(b, bi, u)
                    for i in range(NT):
                        if ahead:
                            maximum(*ahead, i)
                        if "project" in st:
                            project(b, bi, u, i)
                        if u - 1 in MISC and i < 2:
                            read_item(b, bi, u - 1, i)
                        if "finish" in st:
                            finish(b, bi, u, i)
                return unit

            def sync(sp):
                def to_scratch(b, bi, k):
                    sp.wait_ge(S["split"], (b + 2) * 8 + 4 * (k + 1))
                    heads = kv_heads if k else NH
                    for s in range(SPLITS):
                        dst = scratch["k" if k else "q"][bi % 2, s * HD:(s + 1) * HD, 0:heads * T]
                        sp.dma_start(dst.rearrange("d (h t) -> h d t", h=heads),
                                     SPL[0:heads * HD, k, s, :]).then_inc(S["k_scratch" if k else "q_scratch"], 16)

                def load_group(b, bi, g):
                    if not (isinstance(b, int) and b == FIRST_STEP):
                        sp.wait_ge(S["a_free"], (b * UNITS + UNITS + g * NT + 1) * NT)
                    sp.wait_ge(S["q_scratch"], (b + 3) * 16 * SPLITS)
                    sp.wait_ge(S["k_scratch"], (b + 3) * 16 * SPLITS)
                    if "attend" in stages(bi):
                        sp.wait_ge(S["b_full"], (b * UNITS + (g + 1) * NT) * 2)
                    sk, sq = scratch["k"][bi % 2], scratch["q"][bi % 2]
                    n = SPLITS * HD
                    kc = slice(g * kg * T, (g + 1) * kg * T)
                    qc = slice(g * HG * T, (g + 1) * HG * T)
                    kd = KO[:, bi % 2].rearrange("p h t -> p (h t)")
                    qd = QO[:, bi % 2].rearrange("p h t -> p (h t)")
                    for s in range(SPLITS):
                        sp.dma_start(kd[n * s:n * (s + 1), kc], sk[:, kc]).then_inc(qk_loaded[g], 16)
                        cut = s * HD
                        sp.dma_start(qd[n * s:n * (s + 1) - cut, qc], sq[cut:n, qc]).then_inc(qk_loaded[g], 16)
                        if s:
                            sp.dma_start(qd[n * (s + 1) - cut:n * (s + 1), qc],
                                         sq[0:cut, qc]).then_inc(qk_loaded[g], 16)

                def load_max(mb, mbi, g, item):
                    sp.wait_ge(S["misc_free"], item)
                    for c in range(MAX_PARTS):
                        sp.dma_start(QO[MAX_ROW + c:MAX_ROW + c + 1, mbi % 2, g * HG:(g + 1) * HG, :],
                                     MT[c * HG:(c + 1) * HG, g % 2, :]).then_inc(m_loaded[g], 16)

                def unit(b, bi, u):
                    st = stages(bi)
                    if u in (UNIT_OF["m1"], UNIT_OF["m2"], UNIT_OF["m3"]) and "attend" in st:
                        load_max(b, bi, int(MISC[u][0][1]), misc_count(b, bi, u))
                    if u == UNIT_OF["m1"] and bi != FIRST_STEP and "project" in stages(bi - 1):
                        load_group(b - 1, bi - 1, 2)
                        load_group(b - 1, bi - 1, 3)
                    if u == UNIT_OF["v"] and "project" in st:
                        to_scratch(b, bi, 0)
                        to_scratch(b, bi, 1)
                    if u == UNITS - 1 and "prepare" in st:
                        load_max(b + 1, bi + 1, 0, misc_count(b, bi, UNIT_OF["m0"]))
                    if u == UNITS - 1 and "project" in st:
                        load_group(b, bi, 0)
                        load_group(b, bi, 1)
                return unit

            return S, tensor, scalar, gpsimd, vector, sync, split

        S1, tensor1, scalar1, gpsimd1, vector1, sync1, split1 = attention(
            "a1", False, NH, "wq1", "wk1", "wv1", "wu1", "bu", 128.0 ** -0.25, 128.0 ** -0.25, False, FILLED, CLEARED)
        TB = NB * NT

        def cols(at, shape, dt=F32):
            n = int(np.prod(shape))
            names = "abc"[:len(shape)]
            ap = arena[:, at:at + n]
            if len(shape) == 1:
                return ap
            return ap.rearrange(f"p ({' '.join(names)}) -> p {' '.join(names)}",
                                **{names[k]: shape[k] for k in range(1, len(shape))})

        def at(name, shape, offset, dt=F32R):
            return nc.alloc_sbuf_tensor_at(name, shape, dt, offset=offset)
        OPERAND = 2 * NH * T
        ZT = at("ZT", [128, NB * T], ops_at, F32)
        W1H = at("W1H", [128, NE * HID], ops_at + 2 * OPERAND)
        W2H = at("W2H", [128, NE * HID], ops_at + OPERAND)
        W1L, W2L = at("W1L", [128, NE * HID], w_at), at("W2L", [128, NE * HID], w_at + 4 * NE * HID)
        RT_FLAT = RT[:, :, :, :].rearrange("p a b c -> p (a b c)")
        LG = RT_FLAT[:, 0:TB * NE].rearrange("p (t e) -> p t e", e=NE)
        GT = RT_FLAT[:, TB * NE:2 * TB * NE].rearrange("p (t e) -> p t e", e=NE)
        SMALL = NB * T + HB * T + T
        HT = TB // 2
        TOP, TOP2, NUM = (cols(SMALL + k * HT, [HT]) for k in range(3))
        EQ, SEL, SEL2, REST = (cols(SMALL + (k + 1) * HT * NE, [HT, NE]) for k in range(4))
        GSB = cols(SMALL + 5 * HT * NE, [2 * 128])
        gates_dram = nc.dram_tensor("gates", (NE, NB * T), F32).ap()

        r_stats1, r_rstd1, r_ln1, r_stats2, r_rstd2, r_ln2, r_zt_ps, r_zt, r_zr, r_lg_ps, r_lg = (sem(n) for n in (
            "r_stats1", "r_rstd1", "r_ln1", "r_stats2", "r_rstd2", "r_ln2", "r_zt_ps", "r_zt", "r_zr", "r_lg_ps",
            "r_lg"))
        r_soft, r_exp, r_gates = sem("r_soft"), sem("r_exp"), sem("r_gates")
        g_ps, g_sb, g_out, w_high, w_low = (sem(n) for n in ("g_ps", "g_sb", "g_out", "w_high", "w_low"))
        ZRB = [XNT[:, 0, :], XNT[:, 1, :]]

        def route_bank(b):
            return (PA if b < 4 else (PV, PM))[b % 2]

        def route_vector(v, s):
            if has_work(s, 4):
                b = s - 4
                v.wait_ge(r_lg_ps, b + 1)
                nc.vector.tensor_tensor(
                    LG[:, b * NT:(b + 1) * NT, :], route_bank(b)[:, 0:NT * NE].rearrange("p (t e) -> p t e", e=NE),
                    row("router_b").unsqueeze(1).to_broadcast([128, NT, NE]), ALU.add).then_inc(r_lg, 1)
            if has_work(s, 2):
                b = s - 2
                if b:
                    v.wait_ge(r_zt_ps, b)
                normalise(v, AGAIN, lambda i: XN[:, i, :], lambda i: XR[:, i, :], r_rstd2, (b + 1) * 2, r_ln2)
            if has_work(s, 1):
                b = s - 1
                if b:
                    v.wait_ge(r_ln2, b)
                normalise(v, PRE, lambda i: xcols(b, i), lambda i: XN[:, i, :], r_rstd1, (b + 1) * 2, r_ln1)
                v.wait_ge(r_ln1, b + 1)
                stats_of(v, AGAIN, lambda i: XN[:, i, :], r_stats2, b * 2)
            if has_work(s, 0):
                v.wait_ge(S1["x_done"], s + 1)
                if s:
                    v.wait_ge(r_ln1, s)
                stats_of(v, PRE, lambda i: xcols(s, i), r_stats1, s * 2)

        def route_gpsimd(pool, s):
            if has_work(s, 1):
                b = s - 1
                rstd_of(pool, AGAIN, eps6, r_stats2, (b + 1) * 2, r_rstd2, b * 2)
            if has_work(s, 0):
                rstd_of(pool, PRE, eps5, r_stats1, (s + 1) * 2, r_rstd1, s * 2)

        def route_tensor(pe, s):
            if has_work(s, 3):
                b = s - 3
                pe.wait_ge(r_zr, b + 1)
                if b == 5:
                    pe.wait_ge(g_sb, 1)
                for i in range(NT):
                    m = pe.matmul(route_bank(b)[:, i * NE:(i + 1) * NE], ZRB[b % 2][:, i * 128:(i + 1) * 128],
                                  w("router_w"), start=True, stop=True)
                m.then_inc(r_lg_ps, 1)
            if has_work(s, 2):
                b = s - 2
                pe.wait_ge(r_ln2, b + 1)
                if b >= 2:
                    pe.wait_ge(r_lg, b - 1)
                for i in range(NT):
                    m = pe.transpose(route_bank(b)[:, i * 128:(i + 1) * 128], XR[:, i, :], ident)
                m.then_inc(r_zt_ps, 1)

        def route_scalar(act, s):
            if has_work(s, 2):
                b = s - 2
                act.wait_ge(r_zt_ps, b + 1)
                nc.scalar.activation(ZT[:, b * T:(b + 1) * T], route_bank(b)[:, :], ACT.Copy).then_inc(r_zt, 1)
                if b >= 2:
                    act.wait_ge(r_lg_ps, b - 1)
                nc.scalar.activation(ZRB[b % 2], route_bank(b)[:, :], ACT.Identity, bias=w("router_t"),
                                     scale=w("router_s")).then_inc(r_zr, 1)

        def weights_high(k, full, high):
            c = slice(k * PIECE, (k + 1) * PIECE)
            nc.scalar.activation(high[:, c], full[:, c], ACT.Copy).then_inc(w_high, 1)

        def weights_low(pool, k, full, high, low, ready):
            c = slice(k * PIECE, (k + 1) * PIECE)
            pool.wait_ge(w_high, ready)
            pool.tensor_tensor(low[:, c], full[:, c], high[:, c].bitcast(F32), ALU.subtract).then_inc(w_low, 1)

        def half_of(ap, half):
            return ap[:, half * HT:(half + 1) * HT]

        def gates_tensor(pe, half):
            pe.wait_ge(r_gates, half + 1)
            if half == 0:
                pe.wait_ge(r_zr, 6)
            c = TB * NE + half * 128
            pe.transpose(PM[:, 0:128], RT_FLAT[:, c:c + 128], ident).then_inc(g_ps, 1)

        def gates_scalar(act, half):
            act.wait_ge(r_soft, half * GATE_LINKS + 2)
            lg = half_of(LG, half)
            nc.scalar.activation(lg, lg, ACT.Exp).then_inc(r_exp, 1)

        def gates_sync(sp, half):
            sp.wait_ge(g_sb, half + 1)
            n = NB * T // 2
            sp.dma_start(gates_dram[:, half * n:(half + 1) * n].rearrange("e (t p) -> t e p", p=128),
                         GSB[:, half * 128:(half + 1) * 128]).then_inc(g_out, 16)
            sp.wait_ge(g_out, (half + 1) * 16)

        def gates_vector(v, half):
            LGH, GTH = half_of(LG, half), half_of(GT, half)
            v.wait_ge(r_lg, (half + 1) * NB // 2)
            n = [half * GATE_LINKS]

            def link(ins):
                n[0] += 1
                ins.then_inc(r_soft, 1)
                v.wait_ge(r_soft, n[0])

            def over_e(ap):
                return ap.unsqueeze(2).to_broadcast([128, HT, NE])
            link(nc.vector.tensor_reduce(TOP, LGH, AX.X, ALU.max))
            link(nc.vector.tensor_tensor(LGH, LGH, over_e(TOP), ALU.subtract))
            v.wait_ge(r_exp, half + 1)
            link(nc.vector.tensor_reduce(TOP, LGH, AX.X, ALU.add))
            link(nc.vector.reciprocal(TOP, TOP))
            link(nc.vector.tensor_tensor(LGH, LGH, over_e(TOP), ALU.mult))

            def highest(probs, top, sel):
                link(nc.vector.tensor_reduce(top, probs, AX.X, ALU.max))
                link(nc.vector.tensor_tensor(EQ, probs, over_e(top), ALU.is_equal))
                link(nc.vector.tensor_tensor(EQ, EQ, row("order").unsqueeze(1).to_broadcast([128, HT, NE]), ALU.mult))
                link(nc.vector.tensor_reduce(NUM, EQ, AX.X, ALU.max))
                link(nc.vector.tensor_tensor(sel, EQ, over_e(NUM), ALU.is_equal))
            highest(LGH, TOP, SEL)
            link(nc.vector.scalar_tensor_tensor(out=REST, in0=SEL, scalar=-2.0, in1=LGH, op0=ALU.mult, op1=ALU.add))
            highest(REST, TOP2, SEL2)
            link(nc.vector.tensor_tensor(SEL, SEL, SEL2, ALU.add))
            link(nc.vector.tensor_tensor(GTH, SEL, LGH, ALU.mult))
            link(nc.vector.tensor_tensor(TOP, TOP, TOP2, ALU.add))
            link(nc.vector.reciprocal(TOP, TOP))
            assert n[0] == (half + 1) * GATE_LINKS
            nc.vector.tensor_tensor(GTH, GTH, over_e(TOP), ALU.mult).then_inc(r_gates, 1)

        def gates_copy(v, half):
            v.wait_ge(g_ps, half + 1)
            nc.vector.tensor_copy(GSB[:, half * 128:(half + 1) * 128], PM[:, 0:128]).then_inc(g_sb, 1)

        def first_tensor(pe):
            pe.wait_ge(loaded_w, 16)
            pe.wait_ge(consts, CONSTS)

            def after(b, u):
                if units_before(b, u, 1) in ROUTE_AT:
                    route_tensor(pe, ROUTE_AT[units_before(b, u, 1)])
            run_steps(pe, FIRST_STEP, tensor1(pe), after)

        def first_scalar(act):
            def after(b, u):
                if units_before(b, u, 2) in ROUTE_AT:
                    route_scalar(act, ROUTE_AT[units_before(b, u, 2)])
                if (b, u) == (NB - 1, 0):
                    act.wait_ge(loaded_mw, 32)
                if (b, u) in W1_HIGH_AT:
                    weights_high(W1_HIGH_AT[b, u], W1, W1H)
                if (b, u) in W2_HIGH_AT:
                    weights_high(W2_HIGH_AT[b, u], W2, W2H)
            run_steps(act, FIRST_STEP, scalar1(act), after)

        def first_gpsimd(pool, split_tokens):
            make_constants(pool)
            unit = gpsimd1(pool)
            for u in range(4):
                unit(FIRST_STEP, FIRST_STEP, u)

            def after(b, u):
                if (b, u) in ROUTE_AT:
                    route_gpsimd(pool, ROUTE_AT[b, u])
                if (b, u) in W1_LOW_AT:
                    k = W1_LOW_AT[b, u]
                    weights_low(pool, k, W1, W1H, W1L, k + 1)
                if (b, u) in TOKENS_AT:
                    split_tokens(0, TOKENS_AT[b, u])
            run_steps(pool, FIRST_STEP + 1, unit, after)

        def first_vector(v, tokens):
            unit = vector1(v)
            v.wait_ge(loaded_x0, 16)
            v.wait_ge(loaded_w, 16)
            for u in range(4):
                unit(FIRST_STEP, FIRST_STEP, u)
            clear_values(v, 0)
            for k in (0, 1):
                split1(v, FIRST_STEP, FIRST_STEP, k)
            v.wait_ge(loaded_x, 16)
            v.wait_ge(loaded_tables, TABLES)

            def after(b, u):
                if (b, u) in ROUTE_AT:
                    route_vector(v, ROUTE_AT[b, u])
                if (b, u) in TOKENS_AT:
                    tokens(0, TOKENS_AT[b, u])
            run_steps(v, FIRST_STEP + 1, unit, after)

        def first_sync(sp):
            load_inputs(sp)
            unit = sync1(sp)
            for b in (FIRST_STEP, FIRST_STEP + 1):
                for u in range(UNITS):
                    unit(b, b, u)
            sp.dma_start(W1[:, :], w1).then_inc(loaded_mw, 16)
            sp.dma_start(W2[:, :], w2).then_inc(loaded_mw, 16)
            run_steps(sp, FIRST_STEP + 2, unit)

        HH, HL = at("HH", [128, 2, HB, T], ops_at + 3 * OPERAND), at("HL", [128, 2, HB, T], arena_at)
        ZH, ZL = at("ZH", [128, 2, T], vo_at), at("ZL", [128, 2, T], vo_at + 8 * T)
        G = at("G", [128, 2, T], vo_at + 16 * T, F32)
        ZF = at("ZF", [128, T], vo_at + 24 * T, F32)
        AT = at("AT", [128, T], vo_at + 28 * T, F32)
        H = cols(NB * T, [HB, T])
        YG = cols(NB * T + HB * T, [T])
        e_zf, e_zh, e_zl, e_h_ps, e_h, e_hh, e_hl, e_y_ps, e_yg, e_acc, e_t_ps, e_y = (sem(n) for n in (
            "e_zf", "e_zh", "e_zl", "e_h_ps", "e_h", "e_hh", "e_hl", "e_y_ps", "e_yg", "e_acc", "e_t_ps",
            "e_y"))
        e_stats, e_rstd, e_ln, e_x = sem("e_stats"), sem("e_rstd"), sem("e_ln"), sem("e_x")

        e_g = [sem("e_g0"), sem("e_g1")]
        PV2 = PA

        def unless_first(b):
            return not (isinstance(b, int) and b == 0)

        S2, tensor2, scalar2, gpsimd2, vector2, sync2, _ = attention(
            "a2", True, NG, "wq2", "wk2", "wv2", "wo2", None, HD ** -0.5, 1.0, True, 2 * FILLED, 2 * CLEARED)

        def beside(unit, e):
            for b, u in BESIDE[e]:
                unit(b, b, u)

        with nc.Block() as block:
            @block.vector
            def _(v):
                def tokens(b, e):
                    n = b * NE + e
                    if unless_first(n):
                        v.wait_ge(e_zl, n)
                    nc.vector.tensor_scalar(ZF[:, :], ZT[:, bass.ds(b * T, T)], w("expert_s")[:, e:e + 1],
                                            w("expert_t")[:, e:e + 1], ALU.mult, ALU.add).then_inc(e_zf, 1)

                def leftovers(b, e, k):
                    n = b * NE + e
                    if k == 0 and not (isinstance(n, int) and n < 2):
                        v.wait_ge(e_y_ps, n - 1)
                    v.wait_ge(e_hh, n * HB + k + 1)
                    nc.vector.tensor_tensor(HL[:, e % 2, k, :], H[:, k, :], HH[:, e % 2, k, :].bitcast(F32),
                                            ALU.subtract).then_inc(e_hl, 1)

                def gather(b, e):
                    n = b * NE + e
                    v.wait_ge(e_g[e % 2], (b * (NE // 2) + e // 2 + 1) * 16)
                    v.wait_ge(e_y_ps, n + 1)
                    dst = AT[:, :] if e == 0 else YG
                    if e == 0 and unless_first(b):
                        v.wait_ge(e_t_ps, b)
                    if e >= 2:
                        v.wait_ge(e_acc, b * (NE - 1) + e - 1)
                    nc.vector.scalar_tensor_tensor(out=dst, in0=PV2[e % 2][:, :], scalar=w("b2")[:, e:e + 1],
                                                   in1=G[:, e % 2, :], op0=ALU.add, op1=ALU.mult).then_inc(e_yg, 1)
                    if e:
                        v.wait_ge(e_yg, n + 1)
                        nc.vector.tensor_tensor(AT[:, :], AT[:, :], YG, ALU.add).then_inc(e_acc, 1)

                def finish(b):
                    v.wait_ge(e_t_ps, b + 1)
                    nc.vector.tensor_copy(Y[:, :, :].rearrange("p i d -> p (i d)"), PM[:, :]).then_inc(e_y, 1)
                    v.wait_ge(e_y, b + 1)
                    stats_of(v, POST, lambda i: Y[:, i, :], e_stats, b * 2)

                def add(b):
                    normalise(v, POST, lambda i: Y[:, i, :], lambda i: Y[:, i, :], e_rstd, (b + 1) * 2, e_ln)
                    v.wait_ge(e_ln, b + 1)
                    xb = X[:, bass.ds(b * T, T)]
                    nc.vector.tensor_tensor(xb, xb, Y[:, :, :].rearrange("p i d -> p (i d)"),
                                            ALU.add).then_inc(e_x, 1)

                def body(b, last=False):
                    for e in range(NE):
                        for k in range(HB):
                            leftovers(b, e, k)
                            if k == 0:
                                if e + 2 < NE:
                                    tokens(b, e + 2)
                                elif not last:
                                    tokens(b + 1, e + 2 - NE)
                            if k == (3 if isinstance(b, int) and b == 0 and e == 1 else 1) and e >= 1:
                                gather(b, e - 1)
                            if k == 1 and e == 0 and unless_first(b):
                                gather(b - 1, NE - 1)
                            if k == 2 and e == 1 and unless_first(b):
                                finish(b - 1)
                            if k == 2 and e == 3 and unless_first(b):
                                add(b - 1)
                        if isinstance(b, int) and b == 0:
                            if e == 0:
                                gates_vector(v, 0)
                                gates_copy(v, 0)
                            if e in ROUTE_BESIDE:
                                route_vector(v, ROUTE_BESIDE[e])
                            if e == 5:
                                gates_vector(v, 1)
                            if e == 6:
                                gates_copy(v, 1)
                        if last:
                            if e == 0:
                                v.wait_ge(e_x, 2)
                            beside(projection, e)
                projection = vector2(v)
                first_vector(v, tokens)
                route_vector(v, 7)
                body(0)
                with v.Fori(1, NB - 1) as b:
                    body(b)
                body(NB - 1, last=True)
                gather(NB - 1, NE - 1)
                finish(NB - 1)
                add(NB - 1)
                v.wait_ge(e_x, NB)

            @block.gpsimd
            def _(pool):
                def split_tokens(b, e):
                    n = b * NE + e
                    pool.wait_ge(e_zf, n + 1)
                    if not (isinstance(n, int) and n < 2):
                        pool.wait_ge(e_h_ps, (n - 1) * HB)
                    pool.tensor_tensor(ZH[:, e % 2, :], ZF[:, :], zero[:, :].to_broadcast([128, T]),
                                       ALU.add).then_inc(e_zh, 1)
                    pool.wait_ge(e_zh, n + 1)
                    pool.tensor_tensor(ZL[:, e % 2, :], ZF[:, :], ZH[:, e % 2, :].bitcast(F32),
                                       ALU.subtract).then_inc(e_zl, 1)

                def body(b, last=False):
                    for e in range(NE):
                        if e + 2 < NE:
                            split_tokens(b, e + 2)
                        elif not last:
                            split_tokens(b + 1, e + 2 - NE)
                        if e == 1 and unless_first(b):
                            rstd_of(pool, POST, eps5, e_stats, b * 2, e_rstd, (b - 1) * 2)
                        if isinstance(b, int) and b == 0 and e in ROUTE_BESIDE:
                            route_gpsimd(pool, ROUTE_BESIDE[e])
                        if last:
                            beside(projection, e)
                projection = gpsimd2(pool)
                first_gpsimd(pool, split_tokens)
                route_gpsimd(pool, 7)
                for k in range(PIECES):
                    weights_low(pool, k, W2, W2H, W2L, PIECES + k + 1)
                body(0)
                with pool.Fori(1, NB - 1) as b:
                    body(b)
                body(NB - 1, last=True)
                rstd_of(pool, POST, eps5, e_stats, NB * 2, e_rstd, (NB - 1) * 2)

            @block.tensor
            def _(pe):
                def three(out, weights, tokens, start, stop):
                    (wh, wl), (th, tl) = weights, tokens
                    pe.matmul(out, wh, th, start=start, stop=False)
                    pe.matmul(out, wh, tl, start=False, stop=False)
                    return pe.matmul(out, wl, th, start=False, stop=stop)

                def hidden(b, e):
                    n = b * NE + e
                    pe.wait_ge(e_zl, n + 1)
                    if isinstance(b, int) and b == 0:
                        pe.wait_ge(w_low, e * HID // PIECE + 1)
                    for k in range(HB):
                        if unless_first(n):
                            pe.wait_ge(e_hh, (n - 1) * HB + k + 1)
                        c = slice(e * HID + k * 128, e * HID + (k + 1) * 128)
                        three(PB[k // 2][:, (k % 2) * 512:(k % 2 + 1) * 512], (W1H[:, c], W1L[:, c]),
                              (ZH[:, e % 2, :], ZL[:, e % 2, :]), True, True).then_inc(e_h_ps, 1)

                def output(b, e):
                    n = b * NE + e
                    if not (isinstance(n, int) and n < 2):
                        pe.wait_ge(e_yg, n - 1)
                    else:
                        pe.wait_ge(r_lg, 4)
                    if isinstance(b, int) and b == 0:
                        pe.wait_ge(w_low, PIECES + e * HID // PIECE + 1)
                    for k in range(HB):
                        pe.wait_ge(e_hl, n * HB + k + 1)
                        c = slice((e * HB + k) * D, (e * HB + k + 1) * D)
                        m = three(PV2[e % 2][:, :], (W2H[:, c], W2L[:, c]), (HH[:, e % 2, k, :], HL[:, e % 2, k, :]),
                                  k == 0, k == HB - 1)
                    m.then_inc(e_y_ps, 1)

                def back(b):
                    pe.wait_ge(e_yg, (b + 1) * NE)
                    pe.wait_ge(e_acc, (b + 1) * (NE - 1))
                    if unless_first(b):
                        pe.wait_ge(e_y, b)
                    for i in range(NT):
                        m = pe.transpose(PM[:, i * 128:(i + 1) * 128], AT[:, i * 128:(i + 1) * 128], ident)
                    m.then_inc(e_t_ps, 1)

                def body(b, last=False):
                    for e in range(NE):
                        if e + 1 < NE:
                            hidden(b, e + 1)
                        elif not last:
                            hidden(b + 1, 0)
                        output(b, e)
                        if e == 0 and unless_first(b):
                            back(b - 1)
                        if isinstance(b, int) and b == 0:
                            if e == 0:
                                gates_tensor(pe, 0)
                            if e in ROUTE_BESIDE:
                                route_tensor(pe, ROUTE_BESIDE[e])
                            if e == 6:
                                gates_tensor(pe, 1)
                        if last:
                            if e == 2:
                                pe.wait_ge(e_y, NB - 1)
                            beside(projection, e)
                projection = tensor2(pe)
                first_tensor(pe)
                hidden(0, 0)
                route_tensor(pe, 7)
                body(0)
                with pe.Fori(1, NB - 1) as b:
                    body(b)
                body(NB - 1, last=True)
                pe.wait_ge(S2["misc_free"], misc_count(FIRST_STEP, FIRST_STEP, UNIT_OF["k"]))
                back(NB - 1)

            @block.scalar
            def _(act):
                def body(b, last=False):
                    for e in range(NE):
                        n = b * NE + e
                        for k in range(HB):
                            act.wait_ge(e_h_ps, n * HB + k + 1)
                            if unless_first(n):
                                act.wait_ge(e_hl, (n - 1) * HB + k + 1)
                            nc.scalar.activation(H[:, k, :], PB[k // 2][:, (k % 2) * 512:(k % 2 + 1) * 512],
                                                 ACT.Gelu, bias=w("b1")[:, e * HB + k:e * HB + k + 1]).then_inc(e_h, 1)
                            if k == 0 and not (isinstance(n, int) and n < 2):
                                act.wait_ge(e_y_ps, n - 1)
                            nc.scalar.activation(HH[:, e % 2, k, :], PB[k // 2][:, (k % 2) * 512:(k % 2 + 1) * 512],
                                                 ACT.Gelu, bias=w("b1")[:, e * HB + k:e * HB + k + 1]).then_inc(e_hh, 1)
                            if isinstance(b, int) and b == 0 and k == 2:
                                if e - 1 in ROUTE_BESIDE:
                                    route_scalar(act, ROUTE_BESIDE[e - 1])
                                if e == 6:
                                    gates_scalar(act, 1)
                            if last and e and k == 2:
                                beside(projection, e - 1)
                        if isinstance(b, int) and b == 0 and e == 0:
                            route_scalar(act, 7)
                            gates_scalar(act, 0)
                projection = scalar2(act)
                first_scalar(act)
                body(0)
                with act.Fori(1, NB - 1) as b:
                    body(b)
                body(NB - 1, last=True)

            @block.sync
            def _(sp):
                def body(b):
                    for e in range(NE):
                        n = b * NE + e
                        if not (isinstance(n, int) and n < 2):
                            sp.wait_ge(e_yg, n - 1)
                        sp.dma_start(G[:, e % 2, :], gates_dram[e, bass.ds(b * T, T)].partition_broadcast(128)
                                     ).then_inc(e_g[e % 2], 16)
                first_sync(sp)
                gates_sync(sp, 0)
                body(0)
                gates_sync(sp, 1)
                with sp.Fori(1, NB) as b:
                    body(b)
                sync2(sp)(FIRST_STEP, FIRST_STEP, UNIT_OF["v"])

        F = at("F", [128, 2 * NE * HID], w_at, F32)
        XM = F[:, 0:4 * T].rearrange("p (c k t) -> p c k t", c=2, k=2)
        KA = F[:, 4 * T:6 * T].rearrange("p (c t) -> p c t", c=2)
        SG = F[:, 6 * T:8 * T].rearrange("p (c t) -> p c t", c=2)
        YO = F[:, 8 * T:10 * T].rearrange("p (c i d) -> p c i d", c=2, i=NT)
        PR = F[:, 10 * T:12 * T].rearrange("p (k t) -> p k t", k=2)
        XS = F[:, 12 * T:13 * T + 2]
        f_const, f_stats, f_rstd, f_ln, f_xs_ps, f_xs, f_mix, f_k_ps, f_r_ps, f_k, f_k2, f_out_ps, f_sig, f_gated = (
            sem(n) for n in ("f_const", "f_stats", "f_rstd", "f_ln", "f_xs_ps", "f_xs", "f_mix", "f_k_ps", "f_r_ps",
                             "f_k", "f_k2", "f_out_ps", "f_sig", "f_gated"))
        f_prev = sem("f_prev")
        f_stats2, f_rstd2, f_ln2, f_x = sem("f_stats2"), sem("f_rstd2"), sem("f_ln2"), sem("f_x")

        def beside_attention(s):
            return s < len(MIX_AT)

        def xs_bank(b):
            return PA[0] if beside_attention(b + 1) else PM

        def r_bank(b):
            return PA[1] if beside_attention(b + 2) else PB[0]

        def mix_constants(v):
            nc.vector.memset(XS[:, 0:2], 0.0).then_inc(f_const, 1)
            for k, name in enumerate(("mu_r", "mu_k")):
                nc.vector.tensor_scalar(MU[:, k:k + 1], w(name), -1.0, 1.0, ALU.mult, ALU.add).then_inc(f_const, 1)

        def mix_vector(v, s, part):
            if has_work(s, 1) and part == 0:
                b = s - 1
                if b >= 1:
                    v.wait_ge(f_xs_ps, b)
                normalise(v, PRE, lambda i: xcols(b, i), lambda i: XN[:, i, :], f_rstd, (b + 1) * 2, f_ln)
            if has_work(s, 0) and part == 0:
                v.wait_ge(S2["x_done"], s + 1)
                if s:
                    v.wait_ge(f_ln, s)
                stats_of(v, PRE, lambda i: xcols(s, i), f_stats, s * 2)
            if has_work(s, 4) and part == 0:
                b = s - 4
                normalise(v, AGAIN, lambda i: YO[:, b % 2, i, :], lambda i: YO[:, b % 2, i, :],
                          f_rstd2, (b + 1) * 2, f_ln2)
            if has_work(s, 3) and part == 0:
                b = s - 3
                v.wait_ge(f_sig, b + 1)
                v.wait_ge(f_out_ps, b + 1)
                if b >= 2:
                    v.wait_ge(f_x, b - 1)
                nc.vector.tensor_tensor(YO[:, b % 2, :, :].rearrange("p i d -> p (i d)"),
                                        PA[1][:, :], SG[:, b % 2, :], ALU.mult).then_inc(f_gated, 1)
                v.wait_ge(f_gated, b + 1)
                if b >= 1:
                    v.wait_ge(f_ln2, b)
                stats_of(v, AGAIN, lambda i: YO[:, b % 2, i, :], f_stats2, b * 2)
            if has_work(s, 2) and part == 0:
                b = s - 2
                v.wait_ge(f_k, b + 1)
                nc.vector.tensor_tensor(KA[:, b % 2, :], KA[:, b % 2, :], KA[:, b % 2, :],
                                        ALU.mult).then_inc(f_k2, 1)
            if has_work(s, 1) and part == 1:
                b = s - 1
                if b >= 2:
                    v.wait_ge(f_r_ps, b - 1)
                for k, name in enumerate(("mu_r", "mu_k")):
                    v.wait_ge(f_prev, b * 2 + k + 1)
                    nc.vector.scalar_tensor_tensor(
                        out=XM[:, b % 2, k, :], in0=XS[:, 2:T + 2], scalar=w(name), in1=PR[:, k, :],
                        op0=ALU.mult, op1=ALU.add).then_inc(f_mix, 1)

        def mix_gpsimd(pool, s):
            if has_work(s, 0):
                rstd_of(pool, PRE, eps5, f_stats, (s + 1) * 2, f_rstd, s * 2)
            if has_work(s, 4):
                b = s - 4
                pool.wait_ge(f_ln2, b + 1)
                xb = X[:, b * T:(b + 1) * T]
                pool.tensor_tensor(xb, xb, YO[:, b % 2, :, :].rearrange("p i d -> p (i d)"), ALU.add).then_inc(f_x, 1)
            if has_work(s, 3):
                b = s - 3
                rstd_of(pool, AGAIN, eps5, f_stats2, (b + 1) * 2, f_rstd2, b * 2)

        def mix_tensor(pe, s, part):
            if has_work(s, 2) and part == 0:
                b = s - 2
                pe.wait_ge(f_mix, (b + 1) * 2)
                if b >= 1:
                    pe.wait_ge(f_k, b)
                pe.matmul(PA[0][:, :], w("wkk"), XM[:, b % 2, 1, :], start=True, stop=True).then_inc(f_k_ps, 1)
            if has_work(s, 1) and part == 1:
                b = s - 1
                pe.wait_ge(f_ln, b + 1)
                if b >= 1:
                    pe.wait_ge(f_xs, b)
                if b >= 1 and beside_attention(s):
                    pe.wait_ge(f_k, b)
                for i in range(NT):
                    m = pe.transpose(xs_bank(b)[:, i * 128:(i + 1) * 128], XN[:, i, :], ident)
                m.then_inc(f_xs_ps, 1)
            if has_work(s, 2) and part == 2:
                b = s - 2
                if b >= 1:
                    pe.wait_ge(*((f_gated, b) if beside_attention(s) else (f_sig, b)))
                for i in range(NT):
                    m = pe.matmul(r_bank(b)[:, i * 128:(i + 1) * 128], XM[:, b % 2, 0, i * 128:(i + 1) * 128],
                                  w("wr"), start=True, stop=True)
                m.then_inc(f_r_ps, 1)
            if has_work(s, 2) and part == 3:
                b = s - 2
                pe.wait_ge(f_k2, b + 1)
                if b >= 1:
                    pe.wait_ge(f_gated, b)
                if beside_attention(s):
                    pe.wait_ge(f_sig, b + 1)
                for i in range(NT):
                    m = pe.matmul(PA[1][:, i * 128:(i + 1) * 128], KA[:, b % 2, i * 128:(i + 1) * 128],
                                  w("wvv"), start=True, stop=True)
                m.then_inc(f_out_ps, 1)

        def mix_scalar(act, s, part):
            if has_work(s, 2) and part == 0:
                b = s - 2
                act.wait_ge(f_k_ps, b + 1)
                if b >= 2:
                    act.wait_ge(f_out_ps, b - 1)
                nc.scalar.activation(KA[:, b % 2, :], PA[0][:, :], ACT.Relu).then_inc(f_k, 1)
            if has_work(s, 1) and part == 1:
                b = s - 1
                act.wait_ge(f_xs_ps, b + 1)
                act.wait_ge(*((f_mix, b * 2) if b else (f_const, 3)))
                nc.scalar.activation(XS[:, 2:T + 2], xs_bank(b)[:, :], ACT.Copy).then_inc(f_xs, 1)
                act.wait_ge(f_xs, b + 1)
                for k in range(2):
                    nc.scalar.activation(PR[:, k, :], XS[:, 1:T + 1], ACT.Identity,
                                         scale=MU[:, k:k + 1]).then_inc(f_prev, 1)
            if has_work(s, 2) and part == 2:
                b = s - 2
                act.wait_ge(f_r_ps, b + 1)
                if b >= 2:
                    act.wait_ge(f_gated, b - 1)
                nc.scalar.activation(SG[:, b % 2, :], r_bank(b)[:, 0:T], ACT.Sigmoid).then_inc(f_sig, 1)

        def interleave(eng, mix, parts, offsets):
            def after(b, u):
                for part, offset in zip(parts, offsets):
                    if units_before(b, u, offset) in MIX_AT:
                        mix(eng, MIX_AT[units_before(b, u, offset)], part)
            return after

        def rest(eng, mix, parts):
            for s in range(len(MIX_AT), MIX_STEPS):
                for part in parts:
                    mix(eng, s, part)

        with nc.Block() as block:
            @block.tensor
            def _(pe):
                after = interleave(pe, mix_tensor, (0, 1, 2, 3), (0, 1, 1, 2))
                run_steps(pe, FIRST_STEP + 1, tensor2(pe), after, FIRST_UNIT)
                rest(pe, mix_tensor, (0, 1, 2, 3))

            @block.scalar
            def _(act):
                after = interleave(act, mix_scalar, (0, 1, 2), (0, 1, 1))
                run_steps(act, FIRST_STEP + 1, scalar2(act), after, FIRST_UNIT)
                rest(act, mix_scalar, (0, 1, 2))

            @block.gpsimd
            def _(pool):
                step = lambda pool, s, part: mix_gpsimd(pool, s)
                run_steps(pool, FIRST_STEP + 1, gpsimd2(pool), interleave(pool, step, (0,), (0,)), FIRST_UNIT)
                rest(pool, step, (0,))

            @block.vector
            def _(v):
                nc.vector.memset(W1[:, 2 * T:3 * T - 128], 0.0).then_inc(masks, 1)
                nc.vector.tensor_copy(W1[:, 3 * T - 128:3 * T], w("mask")).then_inc(masks, 1)
                clear_values(v, CLEARED)
                v.wait_ge(masks, 2)
                beside = interleave(v, mix_vector, (0, 1), (0, 2))

                def after(b, u):
                    if (b, u) == (NB - 1, 0):
                        mix_constants(v)
                    beside(b, u)
                run_steps(v, FIRST_STEP + 1, vector2(v), after, FIRST_UNIT)
                rest(v, mix_vector, (0, 1))

            @block.sync
            def _(sp):
                fill_operands(sp)
                unit = sync2(sp)
                unit(FIRST_STEP, FIRST_STEP, UNITS - 1)
                run_steps(sp, FIRST_STEP + 1, unit)
                with sp.Fori(0, NB) as b:
                    sp.wait_ge(f_x, b + 1)
                    sp.dma_start(out[bass.ds(b, 1)].rearrange("b (i p) d -> p (b i) d", p=128),
                                 X[:, bass.ds(b * T, T)].rearrange("p (c d) -> p c d", d=D)).then_inc(all_out, 16)
                sp.wait_ge(all_out, 16 * NB)


def kernel(**inputs):
    import numpy as _np
    import concourse.bacc as _bacc
    from concourse import mybir as _mybir
    from concourse.bass_utils import run_bass_kernel_spmd as _run

    a = {k: _np.asarray(v) for k, v in inputs.items()}
    columns = {
        "wq1": a["L0_attn_Wq"].T, "wk1": a["L0_attn_Wk"].T, "wv1": a["L0_attn_Wv"].T, "wu1": a["L0_attn_Wu"].T,
        "wq2": a["L1_attn_W_q"].T, "wk2": a["L1_attn_W_k"].T, "wv2": a["L1_attn_W_v"].T, "wo2": a["L1_attn_W_o"].T,
        "wr": a["L1_ffn_W_r"].T, "wkk": a["L1_ffn_W_k"].T, "wvv": a["L1_ffn_W_v"].T,
        "ident": _np.eye(128, dtype=_np.float32),
        "mask": _np.triu(_np.full((128, 128), -1e9, dtype=_np.float32), k=1), "router_w": a["L0_ffn_router_w"].T,
        "router_s": a["L0_ffn_router_ln_scale"][:, None], "router_t": a["L0_ffn_router_ln_bias"][:, None],
        "b2": a["L0_ffn_b2"].T, "expert_s": a["L0_ffn_expert_ln_scale"].T, "expert_t": a["L0_ffn_expert_ln_bias"].T,
        "b1": a["L0_ffn_b1"].reshape(NE * HB, 128).T,
        "mu_r": a["L1_ffn_mu_r"][:, None], "mu_k": a["L1_ffn_mu_k"][:, None],
    }
    rows = {"bu": a["L0_attn_bu"], "router_b": a["L0_ffn_router_b"],
            "order": _np.arange(NE, 0, -1, dtype=_np.float32)}
    half = D // 2
    angle = (_np.arange(T, dtype=_np.float32)[:, None]
             * (1.0 / 10000.0 ** (_np.arange(half, dtype=_np.float32) / half)).astype(_np.float32)[None, :])
    arrays = {
        "x_dram": _np.ascontiguousarray(a["L0_attn_x"]),
        "weights_dram": _np.ascontiguousarray(_np.concatenate([columns[n] for n, _ in WCOLS], axis=1)),
        "rows_dram": _np.ascontiguousarray(_np.concatenate([rows[n] for n, _ in RCOLS])),
        "w1_dram": _np.ascontiguousarray(a["L0_ffn_w1"].transpose(2, 0, 1).reshape(D, NE * HID)),
        "w2_dram": _np.ascontiguousarray(a["L0_ffn_w2"].reshape(NE, D, HB, 128).transpose(3, 0, 2, 1)
                                         .reshape(128, NE * HB * D)),
        "rope_dram": _np.concatenate([_np.cos(angle), _np.sin(angle)], axis=1).astype(_np.float32),
        "fill_dram": _np.concatenate([_np.zeros((MAX_ROW - TERM_ROWS, NH * T), _np.uint32),
                                      _np.full((MAX_PARTS, NH * T), 0x3F803F80, _np.uint32)]).view(_np.float32),
    }
    nc = _bacc.Bacc("TRN2", target_bir_lowering=False, num_devices=1)
    args = [nc.dram_tensor(n, v.shape, _mybir.dt.from_np(v.dtype), kind="ExternalInput").ap()
            for n, v in arrays.items()]
    args.append(nc.dram_tensor("out_dram", (NB, T, D), _mybir.dt.float32, kind="ExternalOutput").ap())
    build(nc, *args)
    r = _run(nc, [arrays], core_ids=[0])
    return r.results[0]["out_dram"]
```
